# Optimizing a Trainium2 kernel written in Bass

```python
import numpy as np
import jax
import jax.numpy as jnp

def _softmax(x, axis=-1):
    return jax.nn.softmax(x, axis=axis)

def _gelu(x):
    return jax.nn.gelu(x, approximate=True)

def _silu(x):
    return jax.nn.silu(x)

def _sigmoid(x):
    return jax.nn.sigmoid(x)

def _layernorm(x, axis=-1, eps=1e-05):
    m = jnp.mean(x, axis=axis, keepdims=True)
    v = jnp.var(x, axis=axis, keepdims=True)
    return (x - m) / jnp.sqrt(v + eps)

def _scatter_add(tgt, idx, src, axis=0):
    return tgt.at[idx].add(src)

def _segment_sum(src, seg, n):
    return jax.ops.segment_sum(src, seg, n)
kernel_name = 'mk_gps_d2_gnn_r32_554cbc'

def setup_inputs(seed: int=0):
    np.random.seed(seed)
    _w = jnp.asarray

    def _rec_inputs():
        import jax
        import jax.numpy as jnp
        _gk = jax.random.key(seed)
        x = -0.0002928 + 1 * jax.random.normal(jax.random.fold_in(_gk, 1), (256, 512), jnp.float32)
        src = jax.random.randint(jax.random.fold_in(_gk, 2), (4096,), 0, 256, jnp.int32)
        dst = jnp.minimum((256 * jax.random.uniform(jax.random.fold_in(_gk, 3), (4096,)) ** 2.0).astype(jnp.int32), 8191)
        _o = jnp.argsort(dst, stable=True)
        src = src[_o]
        dst = dst[_o]
        edge_weight = -0.00121341 + 0.998923 * jax.random.normal(jax.random.fold_in(_gk, 13), (4096,), jnp.float32)
        return (x, src, dst, edge_weight)
    x, src, dst, edge_weight = _rec_inputs()

    def _L0_gnn_setup():
        import jax, jax.numpy as jnp
        import numpy as np
        N_NODES = 256
        N_EDGES = 8192
        D_IN = 512
        D_OUT = 512
        key = jax.random.key(seed)
        k1, k2, k3 = jax.random.split(key, 3)
        x = jax.random.normal(k1, (N_NODES, D_IN), dtype=jnp.float32)
        edge_index = jax.random.randint(k2, (2, N_EDGES), 0, N_NODES, dtype=jnp.int64)
        weight = jax.random.normal(k3, (D_IN, D_OUT), dtype=jnp.float32)
        bias = jnp.zeros((D_OUT,), dtype=jnp.float32)
        return {'x': x, 'edge_index': edge_index, 'weight': weight, 'bias': bias}
    _L0_gnn_all = _L0_gnn_setup()
    _L0_gnn_in = {k: v for k, v in _L0_gnn_all.items() if k in ('weight', 'bias')}
    del _L0_gnn_all

    def _L0_mix_setup():
        import jax, jax.numpy as jnp
        import numpy as np
        B, S, DM = (4, 256, 512)
        H = 8
        D = DM // H

        def _feature_map(t):
            return jax.nn.elu(t) + 1.0
        key = jax.random.key(seed)
        ks = jax.random.split(key, 9)
        s = 1.0 / np.sqrt(DM)
        x = jax.random.normal(ks[0], (B, S, DM), dtype=jnp.float32)
        Wq = jax.random.normal(ks[1], (DM, DM), dtype=jnp.float32) * s
        bq = jnp.zeros((DM,), dtype=jnp.float32)
        Wk = jax.random.normal(ks[2], (DM, DM), dtype=jnp.float32) * s
        bk = jnp.zeros((DM,), dtype=jnp.float32)
        Wv = jax.random.normal(ks[3], (DM, DM), dtype=jnp.float32) * s
        bv = jnp.zeros((DM,), dtype=jnp.float32)
        Wp = jax.random.normal(ks[4], (DM, DM), dtype=jnp.float32) * s
        bp = jnp.zeros((DM,), dtype=jnp.float32)
        return {'x': x, 'Wq': Wq, 'bq': bq, 'Wk': Wk, 'bk': bk, 'Wv': Wv, 'bv': bv, 'Wp': Wp, 'bp': bp}
    _L0_mix_all = _L0_mix_setup()
    _L0_mix_in = {k: v for k, v in _L0_mix_all.items() if k in ('Wq', 'bq', 'Wk', 'bk', 'Wv', 'bv', 'Wp', 'bp')}
    del _L0_mix_all

    def _L0_ffn_setup():
        import jax, jax.numpy as jnp
        import numpy as np
        D_MODEL = 512
        N_HEADS = 8
        KV_OPTS = (8, 4, 1)
        D_K = D_MODEL // N_HEADS

        def gqa(x, wq, wk, wv, wo, n_kv):
            B, S, _ = x.shape
            groups = N_HEADS // n_kv
            q = (x @ wq).reshape(B, S, N_HEADS, D_K).transpose(0, 2, 1, 3)
            k = (x @ wk).reshape(B, S, n_kv, D_K).transpose(0, 2, 1, 3)
            v = (x @ wv).reshape(B, S, n_kv, D_K).transpose(0, 2, 1, 3)
            k = jnp.repeat(k, groups, axis=1)
            v = jnp.repeat(v, groups, axis=1)
            scores = jnp.einsum('bhqd,bhkd->bhqk', q, k) / jnp.sqrt(jnp.float32(D_K))
            attn = jax.nn.softmax(scores, axis=-1)
            out = jnp.einsum('bhqk,bhkd->bhqd', attn, v)
            out = out.transpose(0, 2, 1, 3).reshape(B, S, D_MODEL)
            return out @ wo
        key = jax.random.key(seed)
        ks = jax.random.split(key, 32)
        it = iter(ks)
        s = 0.02
        inp = {'x': jax.random.normal(next(it), (64, 1024, D_MODEL), dtype=jnp.float32)}
        inp['r_w1'] = jax.random.normal(next(it), (D_MODEL, D_MODEL // 4), jnp.float32) * s
        inp['r_b1'] = jnp.zeros((D_MODEL // 4,), jnp.float32)
        inp['r_w2'] = jax.random.normal(next(it), (D_MODEL // 4, len(KV_OPTS)), jnp.float32) * s
        inp['r_b2'] = jnp.zeros((len(KV_OPTS),), jnp.float32)
        for i, nkv in enumerate(KV_OPTS):
            inp[f'wq{i}'] = jax.random.normal(next(it), (D_MODEL, D_MODEL), jnp.float32) * s
            inp[f'wk{i}'] = jax.random.normal(next(it), (D_MODEL, nkv * D_K), jnp.float32) * s
            inp[f'wv{i}'] = jax.random.normal(next(it), (D_MODEL, nkv * D_K), jnp.float32) * s
            inp[f'wo{i}'] = jax.random.normal(next(it), (D_MODEL, D_MODEL), jnp.float32) * s
        return inp
    _L0_ffn_all = _L0_ffn_setup()
    _L0_ffn_in = {k: v for k, v in _L0_ffn_all.items() if k in ('r_w1', 'r_b1', 'r_w2', 'r_b2', 'wq0', 'wk0', 'wv0', 'wo0', 'wq1', 'wk1', 'wv1', 'wo1', 'wq2', 'wk2', 'wv2', 'wo2')}
    del _L0_ffn_all

    def _L1_gnn_setup():
        import jax, jax.numpy as jnp
        import numpy as np
        N = 625
        E = 6250
        D = 512
        H = 512

        def _layernorm(x, gamma, beta, eps=1e-05):
            mu = jnp.mean(x, axis=-1, keepdims=True)
            var = jnp.mean((x - mu) ** 2, axis=-1, keepdims=True)
            return (x - mu) * jax.lax.rsqrt(var + eps) * gamma + beta
        key = jax.random.key(seed)
        ks = jax.random.split(key, 12)
        s = 0.02
        return {'source_features': jax.random.normal(ks[0], (N, D), jnp.float32), 'weighting_gate': jax.random.normal(ks[1], (E,), jnp.float32), 'rel_pair_idx': jax.random.randint(ks[2], (E, 2), 0, N, dtype=jnp.int32), 'Wm': jax.random.normal(ks[3], (D, D // 2), jnp.float32) * s, 'bm': jnp.zeros((D // 2,), jnp.float32), 'W1': jax.random.normal(ks[4], (D, D // 4), jnp.float32) * s, 'b1': jnp.zeros((D // 4,), jnp.float32), 'gamma': jnp.ones((D // 4,), jnp.float32), 'beta': jnp.zeros((D // 4,), jnp.float32), 'W2': jax.random.normal(ks[5], (D // 4, H), jnp.float32) * s, 'b2': jnp.zeros((H,), jnp.float32)}
    _L1_gnn_all = _L1_gnn_setup()
    _L1_gnn_in = {k: v for k, v in _L1_gnn_all.items() if k in ('Wm', 'bm', 'W1', 'b1', 'gamma', 'beta', 'W2', 'b2')}
    del _L1_gnn_all

    def _L1_mix_setup():
        import jax, jax.numpy as jnp
        import numpy as np
        import math
        E = 512
        H = 8
        D = E // H
        M = 64
        EPS = 1e-08
        CLAMP_MAX = 50.0

        def _make_omega(key):
            w = jax.random.normal(key, (D, M), dtype=jnp.float32) / np.sqrt(D)
            q, _ = jnp.linalg.qr(w)
            return q

        def _positive_random_feature_map(v, omega):
            f = jnp.minimum(v @ omega, CLAMP_MAX)
            l2 = jnp.maximum(jnp.linalg.norm(v, axis=-1, keepdims=True), EPS)
            norm_term = jnp.maximum(jnp.exp(-0.5 * l2 * l2), EPS)
            return norm_term * jnp.exp(f)
        key = jax.random.key(seed)
        ks = jax.random.split(key, 8)
        B, S = (2, 512)
        x = jax.random.normal(ks[0], (B, S, E), dtype=jnp.float32)
        sc = 1.0 / np.sqrt(E)
        Wq = jax.random.normal(ks[1], (E, E), dtype=jnp.float32) * sc
        Wk = jax.random.normal(ks[2], (E, E), dtype=jnp.float32) * sc
        Wv = jax.random.normal(ks[3], (E, E), dtype=jnp.float32) * sc
        Wo = jax.random.normal(ks[4], (E, E), dtype=jnp.float32) * sc
        omega_q = _make_omega(ks[5])
        omega_k = _make_omega(ks[6])
        return {'x': x, 'Wq': Wq, 'Wk': Wk, 'Wv': Wv, 'Wo': Wo, 'omega_q': omega_q, 'omega_k': omega_k}
    _L1_mix_all = _L1_mix_setup()
    _L1_mix_in = {k: v for k, v in _L1_mix_all.items() if k in ('Wq', 'Wk', 'Wv', 'Wo', 'omega_q', 'omega_k')}
    del _L1_mix_all

    def _L1_ffn_setup():
        import jax, jax.numpy as jnp
        import numpy as np
        D = 512
        H = 8
        K = 4
        HD = D // H

        def _ln(x, w, b, eps=1e-05):
            m = x.mean(-1, keepdims=True)
            v = ((x - m) ** 2).mean(-1, keepdims=True)
            return (x - m) / jnp.sqrt(v + eps) * w + b

        def _spatial_experts(xn, idx, in_w, in_b, out_w, out_b):
            W = in_w[idx]
            qkv = jnp.einsum('btd,bed->bte', xn, W) + in_b[idx][:, None, :]
            q, k, v = jnp.split(qkv, 3, axis=-1)
            B, T, _ = xn.shape
            q = q.reshape(B, T, H, HD) * HD ** (-0.5)
            k = k.reshape(B, T, H, HD)
            v = v.reshape(B, T, H, HD)
            att = jax.nn.softmax(jnp.einsum('bthd,bshd->bhts', q, k), axis=-1)
            o = jnp.einsum('bhts,bshd->bthd', att, v).reshape(B, T, D)
            return jnp.einsum('btd,bod->bto', o, out_w[idx]) + out_b[idx][:, None, :]

        def _temporal_experts(xt, idx, qw, qb, kw, kb, vw, vb, pw, pb):
            B, T, _ = xt.shape
            q = (jnp.einsum('btd,bod->bto', xt, qw[idx]) + qb[idx][:, None, :]).reshape(B, T, H, HD)
            k = (jnp.einsum('btd,bod->bto', xt, kw[idx]) + kb[idx][:, None, :]).reshape(B, T, H, HD)
            v = (jnp.einsum('btd,bod->bto', xt, vw[idx]) + vb[idx][:, None, :]).reshape(B, T, H, HD)
            logits = jnp.einsum('bthd,bshd->bhts', q, k) * HD ** (-0.5)
            causal = jnp.tril(jnp.ones((T, T), dtype=bool))
            logits = jnp.where(causal, logits, -jnp.inf)
            att = jax.nn.softmax(logits, axis=-1)
            o = jnp.einsum('bhts,bshd->bthd', att, v).reshape(B, T, D)
            o = jnp.einsum('btd,bod->bto', o, pw[idx]) + pb[idx][:, None, :]
            return xt + o

        def _cross_mha(q_in, kv_in, in_w, in_b, out_w, out_b):
            B, T, _ = q_in.shape
            S = kv_in.shape[1]
            Wq, Wk, Wv = (in_w[:D], in_w[D:2 * D], in_w[2 * D:])
            bq, bk, bv = (in_b[:D], in_b[D:2 * D], in_b[2 * D:])
            q = (q_in @ Wq.T + bq).reshape(B, T, H, HD) * HD ** (-0.5)
            k = (kv_in @ Wk.T + bk).reshape(B, S, H, HD)
            v = (kv_in @ Wv.T + bv).reshape(B, S, H, HD)
            att = jax.nn.softmax(jnp.einsum('bthd,bshd->bhts', q, k), axis=-1)
            o = jnp.einsum('bhts,bshd->bthd', att, v).reshape(B, T, D)
            return o @ out_w.T + out_b
        key = jax.random.key(seed)
        ks = iter(jax.random.split(key, 40))
        B, T = (256, 64)
        p = lambda *shape: jax.random.normal(next(ks), shape, dtype=jnp.float32) * 0.02
        inp = {'x': jax.random.normal(next(ks), (B, T, D), dtype=jnp.float32), 'router_w1': p(128, D), 'router_b1': jnp.zeros((128,), jnp.float32), 'router_w2': p(2 * K, 128), 'router_b2': jnp.zeros((2 * K,), jnp.float32), 'norm_s_w': jnp.ones((D,), jnp.float32), 'norm_s_b': jnp.zeros((D,), jnp.float32), 'norm_t_w': jnp.ones((D,), jnp.float32), 'norm_t_b': jnp.zeros((D,), jnp.float32), 'sp_in_w': p(K, 3 * D, D), 'sp_in_b': jnp.zeros((K, 3 * D), jnp.float32), 'sp_out_w': p(K, D, D), 'sp_out_b': jnp.zeros((K, D), jnp.float32), 'tq_w': p(K, D, D), 'tq_b': jnp.zeros((K, D), jnp.float32), 'tk_w': p(K, D, D), 'tk_b': jnp.zeros((K, D), jnp.float32), 'tv_w': p(K, D, D), 'tv_b': jnp.zeros((K, D), jnp.float32), 'tp_w': p(K, D, D), 'tp_b': jnp.zeros((K, D), jnp.float32), 'cross_in_w': p(3 * D, D), 'cross_in_b': jnp.zeros((3 * D,), jnp.float32), 'cross_out_w': p(D, D), 'cross_out_b': jnp.zeros((D,), jnp.float32), 'norm_mlp_w': jnp.ones((D,), jnp.float32), 'norm_mlp_b': jnp.zeros((D,), jnp.float32), 'mlp_w1': p(4 * D, D), 'mlp_b1': jnp.zeros((4 * D,), jnp.float32), 'mlp_w2': p(D, 4 * D), 'mlp_b2': jnp.zeros((D,), jnp.float32)}
        return inp
    _L1_ffn_all = _L1_ffn_setup()
    _L1_ffn_in = {k: v for k, v in _L1_ffn_all.items() if k in ('router_w1', 'router_b1', 'router_w2', 'router_b2', 'norm_s_w', 'norm_s_b', 'norm_t_w', 'norm_t_b', 'sp_in_w', 'sp_in_b', 'sp_out_w', 'sp_out_b', 'tq_w', 'tq_b', 'tk_w', 'tk_b', 'tv_w', 'tv_b', 'tp_w', 'tp_b', 'cross_in_w', 'cross_in_b', 'cross_out_w', 'cross_out_b', 'norm_mlp_w', 'norm_mlp_b', 'mlp_w1', 'mlp_b1', 'mlp_w2', 'mlp_b2')}
    del _L1_ffn_all
    return {'x': x, 'src': src, 'dst': dst, 'edge_weight': edge_weight, 'L0_gnn_weight': _L0_gnn_in['weight'], 'L0_gnn_bias': _L0_gnn_in['bias'], 'L0_mix_Wq': _L0_mix_in['Wq'], 'L0_mix_bq': _L0_mix_in['bq'], 'L0_mix_Wk': _L0_mix_in['Wk'], 'L0_mix_bk': _L0_mix_in['bk'], 'L0_mix_Wv': _L0_mix_in['Wv'], 'L0_mix_bv': _L0_mix_in['bv'], 'L0_mix_Wp': _L0_mix_in['Wp'], 'L0_mix_bp': _L0_mix_in['bp'], 'L0_ffn_r_w1': _L0_ffn_in['r_w1'], 'L0_ffn_r_b1': _L0_ffn_in['r_b1'], 'L0_ffn_r_w2': _L0_ffn_in['r_w2'], 'L0_ffn_r_b2': _L0_ffn_in['r_b2'], 'L0_ffn_wq0': _L0_ffn_in['wq0'], 'L0_ffn_wk0': _L0_ffn_in['wk0'], 'L0_ffn_wv0': _L0_ffn_in['wv0'], 'L0_ffn_wo0': _L0_ffn_in['wo0'], 'L0_ffn_wq1': _L0_ffn_in['wq1'], 'L0_ffn_wk1': _L0_ffn_in['wk1'], 'L0_ffn_wv1': _L0_ffn_in['wv1'], 'L0_ffn_wo1': _L0_ffn_in['wo1'], 'L0_ffn_wq2': _L0_ffn_in['wq2'], 'L0_ffn_wk2': _L0_ffn_in['wk2'], 'L0_ffn_wv2': _L0_ffn_in['wv2'], 'L0_ffn_wo2': _L0_ffn_in['wo2'], 'L1_gnn_Wm': _L1_gnn_in['Wm'], 'L1_gnn_bm': _L1_gnn_in['bm'], 'L1_gnn_W1': _L1_gnn_in['W1'], 'L1_gnn_b1': _L1_gnn_in['b1'], 'L1_gnn_gamma': _L1_gnn_in['gamma'], 'L1_gnn_beta': _L1_gnn_in['beta'], 'L1_gnn_W2': _L1_gnn_in['W2'], 'L1_gnn_b2': _L1_gnn_in['b2'], 'L1_mix_Wq': _L1_mix_in['Wq'], 'L1_mix_Wk': _L1_mix_in['Wk'], 'L1_mix_Wv': _L1_mix_in['Wv'], 'L1_mix_Wo': _L1_mix_in['Wo'], 'L1_mix_omega_q': _L1_mix_in['omega_q'], 'L1_mix_omega_k': _L1_mix_in['omega_k'], 'L1_ffn_router_w1': _L1_ffn_in['router_w1'], 'L1_ffn_router_b1': _L1_ffn_in['router_b1'], 'L1_ffn_router_w2': _L1_ffn_in['router_w2'], 'L1_ffn_router_b2': _L1_ffn_in['router_b2'], 'L1_ffn_norm_s_w': _L1_ffn_in['norm_s_w'], 'L1_ffn_norm_s_b': _L1_ffn_in['norm_s_b'], 'L1_ffn_norm_t_w': _L1_ffn_in['norm_t_w'], 'L1_ffn_norm_t_b': _L1_ffn_in['norm_t_b'], 'L1_ffn_sp_in_w': _L1_ffn_in['sp_in_w'], 'L1_ffn_sp_in_b': _L1_ffn_in['sp_in_b'], 'L1_ffn_sp_out_w': _L1_ffn_in['sp_out_w'], 'L1_ffn_sp_out_b': _L1_ffn_in['sp_out_b'], 'L1_ffn_tq_w': _L1_ffn_in['tq_w'], 'L1_ffn_tq_b': _L1_ffn_in['tq_b'], 'L1_ffn_tk_w': _L1_ffn_in['tk_w'], 'L1_ffn_tk_b': _L1_ffn_in['tk_b'], 'L1_ffn_tv_w': _L1_ffn_in['tv_w'], 'L1_ffn_tv_b': _L1_ffn_in['tv_b'], 'L1_ffn_tp_w': _L1_ffn_in['tp_w'], 'L1_ffn_tp_b': _L1_ffn_in['tp_b'], 'L1_ffn_cross_in_w': _L1_ffn_in['cross_in_w'], 'L1_ffn_cross_in_b': _L1_ffn_in['cross_in_b'], 'L1_ffn_cross_out_w': _L1_ffn_in['cross_out_w'], 'L1_ffn_cross_out_b': _L1_ffn_in['cross_out_b'], 'L1_ffn_norm_mlp_w': _L1_ffn_in['norm_mlp_w'], 'L1_ffn_norm_mlp_b': _L1_ffn_in['norm_mlp_b'], 'L1_ffn_mlp_w1': _L1_ffn_in['mlp_w1'], 'L1_ffn_mlp_b1': _L1_ffn_in['mlp_b1'], 'L1_ffn_mlp_w2': _L1_ffn_in['mlp_w2'], 'L1_ffn_mlp_b2': _L1_ffn_in['mlp_b2']}

def reference(x, src, dst, edge_weight, L0_gnn_weight, L0_gnn_bias, L0_mix_Wq, L0_mix_bq, L0_mix_Wk, L0_mix_bk, L0_mix_Wv, L0_mix_bv, L0_mix_Wp, L0_mix_bp, L0_ffn_r_w1, L0_ffn_r_b1, L0_ffn_r_w2, L0_ffn_r_b2, L0_ffn_wq0, L0_ffn_wk0, L0_ffn_wv0, L0_ffn_wo0, L0_ffn_wq1, L0_ffn_wk1, L0_ffn_wv1, L0_ffn_wo1, L0_ffn_wq2, L0_ffn_wk2, L0_ffn_wv2, L0_ffn_wo2, L1_gnn_Wm, L1_gnn_bm, L1_gnn_W1, L1_gnn_b1, L1_gnn_gamma, L1_gnn_beta, L1_gnn_W2, L1_gnn_b2, L1_mix_Wq, L1_mix_Wk, L1_mix_Wv, L1_mix_Wo, L1_mix_omega_q, L1_mix_omega_k, L1_ffn_router_w1, L1_ffn_router_b1, L1_ffn_router_w2, L1_ffn_router_b2, L1_ffn_norm_s_w, L1_ffn_norm_s_b, L1_ffn_norm_t_w, L1_ffn_norm_t_b, L1_ffn_sp_in_w, L1_ffn_sp_in_b, L1_ffn_sp_out_w, L1_ffn_sp_out_b, L1_ffn_tq_w, L1_ffn_tq_b, L1_ffn_tk_w, L1_ffn_tk_b, L1_ffn_tv_w, L1_ffn_tv_b, L1_ffn_tp_w, L1_ffn_tp_b, L1_ffn_cross_in_w, L1_ffn_cross_in_b, L1_ffn_cross_out_w, L1_ffn_cross_out_b, L1_ffn_norm_mlp_w, L1_ffn_norm_mlp_b, L1_ffn_mlp_w1, L1_ffn_mlp_b1, L1_ffn_mlp_w2, L1_ffn_mlp_b2):
    import jax
    import jax.numpy as jnp

    def _L0_gnn_ref(x, edge_index, weight, bias):
        import jax, jax.numpy as jnp
        import numpy as np
        N_NODES = 256
        N_EDGES = 8192
        D_IN = 512
        D_OUT = 512
        n = x.shape[0]
        adj = jnp.zeros((n, n), dtype=x.dtype)
        adj = adj.at[edge_index[0], edge_index[1]].set(1.0)
        adj = adj.at[edge_index[1], edge_index[0]].set(1.0)
        adj = adj + jnp.eye(n, dtype=x.dtype)
        deg = jnp.sum(adj, axis=1)
        dinv = 1.0 / jnp.sqrt(deg)
        adj = adj * dinv[:, None] * dinv[None, :]
        return adj @ (x @ weight) + bias

    def _L0_mix_ref(x, Wq, bq, Wk, bk, Wv, bv, Wp, bp):
        import jax, jax.numpy as jnp
        import numpy as np
        B, S, DM = (4, 256, 512)
        H = 8
        D = DM // H

        def _feature_map(t):
            return jax.nn.elu(t) + 1.0
        b, s, _ = x.shape
        q = _feature_map(x @ Wq + bq).reshape(b, s, H, D)
        k = _feature_map(x @ Wk + bk).reshape(b, s, H, D)
        v = (x @ Wv + bv).reshape(b, s, H, D)
        kv = jnp.einsum('bshd,bshe->bhde', k, v)
        z = 1.0 / jnp.einsum('bshd,bhd->bsh', q, k.sum(axis=1))
        out = jnp.einsum('bshd,bhde,bsh->bshe', q, kv, z)
        out = out.reshape(b, s, H * D)
        return out @ Wp + bp

    def _L0_ffn_ref(x, r_w1, r_b1, r_w2, r_b2, wq0, wk0, wv0, wo0, wq1, wk1, wv1, wo1, wq2, wk2, wv2, wo2):
        import jax, jax.numpy as jnp
        import numpy as np
        D_MODEL = 512
        N_HEADS = 8
        KV_OPTS = (8, 4, 1)
        D_K = D_MODEL // N_HEADS

        def gqa(x, wq, wk, wv, wo, n_kv):
            B, S, _ = x.shape
            groups = N_HEADS // n_kv
            q = (x @ wq).reshape(B, S, N_HEADS, D_K).transpose(0, 2, 1, 3)
            k = (x @ wk).reshape(B, S, n_kv, D_K).transpose(0, 2, 1, 3)
            v = (x @ wv).reshape(B, S, n_kv, D_K).transpose(0, 2, 1, 3)
            k = jnp.repeat(k, groups, axis=1)
            v = jnp.repeat(v, groups, axis=1)
            scores = jnp.einsum('bhqd,bhkd->bhqk', q, k) / jnp.sqrt(jnp.float32(D_K))
            attn = jax.nn.softmax(scores, axis=-1)
            out = jnp.einsum('bhqk,bhkd->bhqd', attn, v)
            out = out.transpose(0, 2, 1, 3).reshape(B, S, D_MODEL)
            return out @ wo
        routing_input = x.mean(axis=1)
        logits = jax.nn.relu(routing_input @ r_w1 + r_b1) @ r_w2 + r_b2
        sel = jnp.argmax(jax.nn.softmax(logits, axis=-1), axis=-1)
        params = [(wq0, wk0, wv0, wo0), (wq1, wk1, wv1, wo1), (wq2, wk2, wv2, wo2)]
        out = jnp.zeros_like(x)
        for i, nkv in enumerate(KV_OPTS):
            yi = gqa(x, *params[i], nkv)
            mask = (sel == i)[:, None, None]
            out = jnp.where(mask, yi, out)
        return out

    def _L1_gnn_ref(source_features, weighting_gate, rel_pair_idx, Wm, bm, W1, b1, gamma, beta, W2, b2):
        import jax, jax.numpy as jnp
        import numpy as np
        N = 625
        E = 6250
        D = 512
        H = 512

        def _layernorm(x, gamma, beta, eps=1e-05):
            mu = jnp.mean(x, axis=-1, keepdims=True)
            var = jnp.mean((x - mu) ** 2, axis=-1, keepdims=True)
            return (x - mu) * jax.lax.rsqrt(var + eps) * gamma + beta
        src = rel_pair_idx[:, 0]
        dst = rel_pair_idx[:, 1]
        n_nodes = source_features.shape[0]
        m = jnp.maximum(jnp.max(weighting_gate), jnp.float32(0.0))
        exp_e = jnp.exp(weighting_gate - m)
        row_sum = jax.ops.segment_sum(exp_e, src, num_segments=n_nodes)
        atten_e = exp_e / (row_sum[src] + 1e-06)
        Mfeat = source_features @ Wm + bm
        out0 = jax.ops.segment_sum(atten_e[:, None] * Mfeat[dst], src, num_segments=n_nodes)
        out1 = jax.ops.segment_sum(atten_e[:, None] * Mfeat[src], dst, num_segments=n_nodes)
        message_feats = jnp.concatenate([out0, out1], axis=-1)
        h = message_feats @ W1 + b1
        h = jax.nn.relu(_layernorm(h, gamma, beta))
        h = jax.nn.relu(h @ W2 + b2)
        valid = (row_sum > 0)[:, None]
        return jnp.where(valid, h, jnp.float32(0.0))

    def _L1_mix_ref(x, Wq, Wk, Wv, Wo, omega_q, omega_k):
        import jax, jax.numpy as jnp
        import numpy as np
        import math
        E = 512
        H = 8
        D = E // H
        M = 64
        EPS = 1e-08
        CLAMP_MAX = 50.0

        def _make_omega(key):
            w = jax.random.normal(key, (D, M), dtype=jnp.float32) / np.sqrt(D)
            q, _ = jnp.linalg.qr(w)
            return q

        def _positive_random_feature_map(v, omega):
            f = jnp.minimum(v @ omega, CLAMP_MAX)
            l2 = jnp.maximum(jnp.linalg.norm(v, axis=-1, keepdims=True), EPS)
            norm_term = jnp.maximum(jnp.exp(-0.5 * l2 * l2), EPS)
            return norm_term * jnp.exp(f)
        B, S, _ = x.shape
        scale = 1.0 / np.sqrt(D)

        def heads(y):
            return y.reshape(B, S, H, D).transpose(0, 2, 1, 3)
        Q = heads(x @ Wq) * scale
        K = heads(x @ Wk) * scale
        V = heads(x @ Wv)
        Q_phi = _positive_random_feature_map(Q, omega_q)
        K_phi = _positive_random_feature_map(K, omega_k)
        KV = jnp.einsum('bhsm,bhsd->bhmd', K_phi, V)
        QKV = jnp.einsum('bhsm,bhmd->bhsd', Q_phi, KV)
        K_ones = K_phi.sum(axis=2)
        QK_ones = jnp.einsum('bhsm,bhm->bhs', Q_phi, K_ones)
        attn = QKV / QK_ones[..., None]
        out = attn.transpose(0, 2, 1, 3).reshape(B, S, E)
        return out @ Wo

    def _L1_ffn_ref(x, router_w1, router_b1, router_w2, router_b2, norm_s_w, norm_s_b, norm_t_w, norm_t_b, sp_in_w, sp_in_b, sp_out_w, sp_out_b, tq_w, tq_b, tk_w, tk_b, tv_w, tv_b, tp_w, tp_b, cross_in_w, cross_in_b, cross_out_w, cross_out_b, norm_mlp_w, norm_mlp_b, mlp_w1, mlp_b1, mlp_w2, mlp_b2):
        import jax, jax.numpy as jnp
        import numpy as np
        D = 512
        H = 8
        K = 4
        HD = D // H

        def _ln(x, w, b, eps=1e-05):
            m = x.mean(-1, keepdims=True)
            v = ((x - m) ** 2).mean(-1, keepdims=True)
            return (x - m) / jnp.sqrt(v + eps) * w + b

        def _spatial_experts(xn, idx, in_w, in_b, out_w, out_b):
            W = in_w[idx]
            qkv = jnp.einsum('btd,bed->bte', xn, W) + in_b[idx][:, None, :]
            q, k, v = jnp.split(qkv, 3, axis=-1)
            B, T, _ = xn.shape
            q = q.reshape(B, T, H, HD) * HD ** (-0.5)
            k = k.reshape(B, T, H, HD)
            v = v.reshape(B, T, H, HD)
            att = jax.nn.softmax(jnp.einsum('bthd,bshd->bhts', q, k), axis=-1)
            o = jnp.einsum('bhts,bshd->bthd', att, v).reshape(B, T, D)
            return jnp.einsum('btd,bod->bto', o, out_w[idx]) + out_b[idx][:, None, :]

        def _temporal_experts(xt, idx, qw, qb, kw, kb, vw, vb, pw, pb):
            B, T, _ = xt.shape
            q = (jnp.einsum('btd,bod->bto', xt, qw[idx]) + qb[idx][:, None, :]).reshape(B, T, H, HD)
            k = (jnp.einsum('btd,bod->bto', xt, kw[idx]) + kb[idx][:, None, :]).reshape(B, T, H, HD)
            v = (jnp.einsum('btd,bod->bto', xt, vw[idx]) + vb[idx][:, None, :]).reshape(B, T, H, HD)
            logits = jnp.einsum('bthd,bshd->bhts', q, k) * HD ** (-0.5)
            causal = jnp.tril(jnp.ones((T, T), dtype=bool))
            logits = jnp.where(causal, logits, -jnp.inf)
            att = jax.nn.softmax(logits, axis=-1)
            o = jnp.einsum('bhts,bshd->bthd', att, v).reshape(B, T, D)
            o = jnp.einsum('btd,bod->bto', o, pw[idx]) + pb[idx][:, None, :]
            return xt + o

        def _cross_mha(q_in, kv_in, in_w, in_b, out_w, out_b):
            B, T, _ = q_in.shape
            S = kv_in.shape[1]
            Wq, Wk, Wv = (in_w[:D], in_w[D:2 * D], in_w[2 * D:])
            bq, bk, bv = (in_b[:D], in_b[D:2 * D], in_b[2 * D:])
            q = (q_in @ Wq.T + bq).reshape(B, T, H, HD) * HD ** (-0.5)
            k = (kv_in @ Wk.T + bk).reshape(B, S, H, HD)
            v = (kv_in @ Wv.T + bv).reshape(B, S, H, HD)
            att = jax.nn.softmax(jnp.einsum('bthd,bshd->bhts', q, k), axis=-1)
            o = jnp.einsum('bhts,bshd->bthd', att, v).reshape(B, T, D)
            return o @ out_w.T + out_b
        pooled = x.mean(axis=1)
        h = jax.nn.gelu(pooled @ router_w1.T + router_b1, approximate=False)
        route = jax.nn.softmax(h @ router_w2.T + router_b2, axis=-1)
        idx_s = jnp.argmax(route[:, :K], axis=-1)
        idx_t = jnp.argmax(route[:, K:], axis=-1)
        xn = _ln(x, norm_s_w, norm_s_b)
        spatial_out = _spatial_experts(xn, idx_s, sp_in_w, sp_in_b, sp_out_w, sp_out_b)
        xt = _ln(x, norm_t_w, norm_t_b)
        temporal_out = _temporal_experts(xt, idx_t, tq_w, tq_b, tk_w, tk_b, tv_w, tv_b, tp_w, tp_b)
        fused = _cross_mha(spatial_out, temporal_out, cross_in_w, cross_in_b, cross_out_w, cross_out_b)
        x = x + fused
        h2 = _ln(x, norm_mlp_w, norm_mlp_b)
        x = x + (jax.nn.gelu(h2 @ mlp_w1.T + mlp_b1, approximate=False) @ mlp_w2.T + mlp_b2)
        return x
    edge_index = jnp.stack([src, dst])
    edge_index_t = jnp.stack([src, dst], axis=1)
    xn = _layernorm(x, axis=-1)
    x = x + _L0_gnn_ref(xn, edge_index, L0_gnn_weight, L0_gnn_bias) + _L0_mix_ref(xn[None], L0_mix_Wq, L0_mix_bq, L0_mix_Wk, L0_mix_bk, L0_mix_Wv, L0_mix_bv, L0_mix_Wp, L0_mix_bp)[0]
    x = x + _L0_ffn_ref(_layernorm(x, axis=-1)[None], L0_ffn_r_w1, L0_ffn_r_b1, L0_ffn_r_w2, L0_ffn_r_b2, L0_ffn_wq0, L0_ffn_wk0, L0_ffn_wv0, L0_ffn_wo0, L0_ffn_wq1, L0_ffn_wk1, L0_ffn_wv1, L0_ffn_wo1, L0_ffn_wq2, L0_ffn_wk2, L0_ffn_wv2, L0_ffn_wo2)[0]
    xn = _layernorm(x, axis=-1)
    x = x + _L1_gnn_ref(xn, edge_weight, edge_index_t, L1_gnn_Wm, L1_gnn_bm, L1_gnn_W1, L1_gnn_b1, L1_gnn_gamma, L1_gnn_beta, L1_gnn_W2, L1_gnn_b2) + _L1_mix_ref(xn[None], L1_mix_Wq, L1_mix_Wk, L1_mix_Wv, L1_mix_Wo, L1_mix_omega_q, L1_mix_omega_k)[0]
    x = x + _L1_ffn_ref(_layernorm(x, axis=-1)[None], L1_ffn_router_w1, L1_ffn_router_b1, L1_ffn_router_w2, L1_ffn_router_b2, L1_ffn_norm_s_w, L1_ffn_norm_s_b, L1_ffn_norm_t_w, L1_ffn_norm_t_b, L1_ffn_sp_in_w, L1_ffn_sp_in_b, L1_ffn_sp_out_w, L1_ffn_sp_out_b, L1_ffn_tq_w, L1_ffn_tq_b, L1_ffn_tk_w, L1_ffn_tk_b, L1_ffn_tv_w, L1_ffn_tv_b, L1_ffn_tp_w, L1_ffn_tp_b, L1_ffn_cross_in_w, L1_ffn_cross_in_b, L1_ffn_cross_out_w, L1_ffn_cross_out_b, L1_ffn_norm_mlp_w, L1_ffn_norm_mlp_b, L1_ffn_mlp_w1, L1_ffn_mlp_b1, L1_ffn_mlp_w2, L1_ffn_mlp_b2)[0]
    return x

_drawn_inputs = setup_inputs


def setup_inputs(seed=0):
    import zlib

    import numpy as np

    out = dict(_drawn_inputs(seed))
    spreads = {'L0_gnn_bias': (0.0, 0.324),
     'L0_mix_bq': (0.0, 0.8),
     'L0_mix_bk': (0.0, 0.8),
     'L0_mix_bv': (0.0, 0.313),
     'L0_mix_bp': (0.0, 0.306),
     'L0_ffn_r_b1': (0.0, 0.1),
     'L0_ffn_r_b2': (0.0, 0.1),
     'L1_gnn_bm': (0.0, 0.8),
     'L1_gnn_b1': (0.0, 0.443),
     'L1_gnn_gamma': (1.0, 0.6),
     'L1_gnn_beta': (0.0, 0.8),
     'L1_gnn_b2': (0.0, 0.487),
     'L1_ffn_router_b1': (0.0, 0.8),
     'L1_ffn_router_b2': (0.0, 0.1),
     'L1_ffn_norm_s_w': (1.0, 0.6),
     'L1_ffn_norm_s_b': (0.0, 0.8),
     'L1_ffn_norm_t_w': (1.0, 0.6),
     'L1_ffn_norm_t_b': (0.0, 0.8),
     'L1_ffn_sp_in_b': (0.0, 0.8),
     'L1_ffn_sp_out_b': (0.0, 0.8),
     'L1_ffn_tq_b': (0.0, 0.8),
     'L1_ffn_tk_b': (0.0, 2.0),
     'L1_ffn_tv_b': (0.0, 0.8),
     'L1_ffn_tp_b': (0.0, 0.8),
     'L1_ffn_cross_in_b': (0.0, 0.8),
     'L1_ffn_cross_out_b': (0.0, 2.0),
     'L1_ffn_norm_mlp_w': (1.0, 0.6),
     'L1_ffn_norm_mlp_b': (0.0, 2.0),
     'L1_ffn_mlp_b1': (0.0, 2.0),
     'L1_ffn_mlp_b2': (0.0, 2.0)}
    factors = {'edge_weight': 6.696,
     'L0_mix_Wq': 8.0,
     'L0_mix_Wk': 8.0,
     'L0_mix_Wv': 4.036,
     'L0_ffn_r_w2': 4.039,
     'L0_ffn_wq2': 8.0,
     'L0_ffn_wk2': 8.0,
     'L0_ffn_wv2': 4.435,
     'L0_ffn_wo2': 3.995,
     'L1_gnn_Wm': 3.592,
     'L1_gnn_W1': 3.443,
     'L1_mix_Wq': 8.0,
     'L1_mix_Wk': 8.0,
     'L1_mix_omega_q': 8.0,
     'L1_mix_omega_k': 8.0,
     'L1_ffn_router_w1': 8.0,
     'L1_ffn_router_w2': 8.0,
     'L1_ffn_sp_in_w': 8.0,
     'L1_ffn_sp_out_w': 8.0,
     'L1_ffn_tq_w': 8.0,
     'L1_ffn_tk_w': 8.0,
     'L1_ffn_tv_w': 8.0,
     'L1_ffn_tp_w': 8.0,
     'L1_ffn_cross_in_w': 4.035,
     'L1_ffn_cross_out_w': 3.292,
     'L1_ffn_mlp_w1': 7.683,
     'L1_ffn_mlp_w2': 5.32}
    for name, (base, spread) in spreads.items():
        noise = np.random.default_rng([zlib.crc32(name.encode()), seed]).standard_normal(out[name].shape)
        drawn = base * np.exp(spread * noise) if base else spread * noise
        out[name] = jnp.asarray(drawn.astype(out[name].dtype))
    for name, factor in factors.items():
        out[name] = (out[name] * factor).astype(out[name].dtype)
    return out
```

```python
from contextlib import ExitStack

import numpy as np

import concourse.bass as bass
from concourse import mybir

ALU = mybir.AluOpType
ACT = mybir.ActivationFunctionType
AX = mybir.AxisListType
F32 = mybir.dt.float32
BF16 = mybir.dt.bfloat16
I32 = mybir.dt.int32

P = 128
N = 256
D = 512
H = 8
NT = N // P
DC = D // P
HP = H // 2
HID = 128
E = 4096
EC = E // P
EG = 4
FC = 4 * D // P
K0, K1 = 3, 4
EPS = 1e-5
SCALE = 0.125
MASKED = -1e30

SLOTS = 12
ROWS = 4
WF = DC * D

WEIGHTS = (["mix_k", "mix_v", "mix_q", "gnn", "mix_p", "ffn_q", "ffn_k", "ffn_v", "ffn_o", "graph",
            "per_k", "per_v", "per_q", "per_o", "sp_q", "sp_k", "sp_v", "tm_q", "tm_k", "tm_v",
            "sp_o", "cr_q", "tm_o", "cr_k", "cr_v", "cr_o"]
           + [f"up_{i}" for i in range(4)] + [f"down_{i}" for i in range(4)])
STATIC = [w for w in WEIGHTS if w.split("_")[0] not in ("ffn", "sp", "tm")]
PART = {"q": 0, "k": 1, "v": 2, "o": 3}
BIAS_ROWS = ["mix_k", "mix_v", "gnn", "mix_p", "graph_in", "graph_out", "sp_v", "tm_v", "cr_v", "cr_o", "down"]
ROW_BEFORE = {"mix_k": ["mix_k"], "mix_v": ["mix_v"], "mix_p": ["gnn", "mix_p"], "graph": ["graph_in", "graph_out"],
              "sp_v": ["sp_v"], "tm_v": ["tm_v"], "cr_v": ["cr_v"], "cr_o": ["cr_o"], "down_0": ["down"]}
STATIC_ROWS = [r for r in BIAS_ROWS if r not in ("sp_v", "tm_v")]

COLS, _at = {}, 0
for _name, _width in [("mix_bq", DC), ("r0_b1", 1), ("gamma", 1), ("beta", 1), ("r1_b1", 1), ("ns_w", DC), ("ns_b", DC),
                      ("nt_w", DC), ("nt_b", DC), ("nm_w", DC), ("nm_b", DC), ("up_b", FC), ("cr_bq", DC),
                      ("cr_bk", DC), ("r0_w2", K0), ("r1_w2", 2 * K1)]:
    COLS[_name] = (_at, _at + _width)
    _at += _width
NCOLS = _at


def attention_jobs(a):
    out = []
    for i in range(H + 3):
        if i < H:
            out.append(f"{a}.s{i}")
        if 0 <= i - 2 < H:
            out.append(f"{a}.t{i - 2}")
    return out


def both(*names):
    return [f"{n}.{t}" for n in names for t in range(2)]


JOBS = (both("xT0", "mix_k", "mix_v", "mix_q", "gnn") + ["mix.ks", "mix.kv", "mix.den"]
        + both("mix.num", "mix.oT") + ["cntT"] + ["mix_p.0", "attT", "mix_p.1"] + both("adj")
        + both("xT1") + ["r0.pool", "r0.hid", "r0.out"] + both("ffn_q", "ffn_k", "ffn_v")
        + attention_jobs("ffn") + both("ffn.oT", "ffn_o")
        + both("xT2") + ["g.feat"] + both("per_k", "g.msg", "per_v") + ["g.hid"] + both("per_q")
        + ["g.zT"] + both("per.kf", "per.kn", "g.out", "per.qf", "per.qn")
        + ["per.ks", "per.kv", "per.den"] + both("per.num", "per.oT", "per_o")
        + ["r1.pool", "r1.hid", "r1.out"] + both("xT3", "sp_q", "sp_k", "sp_v")
        + attention_jobs("sp") + both("tm_q", "tm_k", "tm_v", "sp.oT") + attention_jobs("tm")
        + both("sp_o", "cr_q", "tm.oT", "tm_o", "cr_k", "cr_v") + attention_jobs("cr")
        + both("cr.oT", "cr_o", "xT4") + [f"up.{j}" for j in range(FC // 2)] + both("down"))
ROTATING = 6
TURN = {name: divmod(i, ROTATING) for i, name in enumerate(JOBS)}
ATTENTIONS = ["ffn", "sp", "tm", "cr"]

LAST_JOB = {w: f"{w}.1" for w in WEIGHTS} | {"graph": "g.out.1"}
LAST_JOB |= {f"up_{i}": f"up.{2 * i + 1}" for i in range(4)} | {f"down_{i}": "down.1" for i in range(4)}
ROW_DONE = {"mix_k": "mix_k.1", "mix_v": "mix_v.1", "gnn": "adj.1", "mix_p": "adj.1", "graph_in": "g.hid",
            "graph_out": "g.out.1", "sp_v": "sp_v.1", "tm_v": "tm_v.1", "cr_v": "cr_v.1", "cr_o": "cr_o.1",
            "down": "down.1"}

FIRST_CONSTS, ALL_CONSTS = 3, 16

LN_IN0, LN_FFN, LN_IN1, LN_GRAPH, LN_X3, LN_Z, LN_MLP = range(7)


def build(nc, x, edges, gate, cols, rows, router_rows, routers, omegas, weights, ffn_w, sp_w, tm_w,
          sp_cols, tm_cols, sp_row, tm_row, out):
    with ExitStack() as ctx:
        def sb(name, shape, dt=F32):
            return ctx.enter_context(nc.sbuf_tensor(name, shape, dt))

        def sem(name):
            return ctx.enter_context(nc.semaphore(name))

        wslot = sb("wslot", [P, SLOTS, WF])
        rslot = sb("rslot", [P, ROWS, D])
        X = sb("X", [P, NT, D])
        XN = sb("XN", [P, NT, D])
        ZN = sb("ZN", [P, NT, D])
        XT = sb("XT", [P, DC, N])
        XT2 = sb("XT2", [P, DC, N])
        Q = sb("Q", [P, DC, N])
        K = sb("K", [P, DC, N])
        V = sb("V", [P, NT, D])
        O = sb("O", [P, NT, D])
        OT = sb("OT", [P, DC, N])
        SP = sb("SP", [P, DC, N])
        TM = sb("TM", [P, DC, N])
        PR = sb("PR", [P, 4, NT * N])
        PT = sb("PT", [P, 4, NT * N])
        big = sb("big", [P, FC * N])
        big2 = sb("big2", [P, 1024])
        KV = sb("KV", [P, HP, P])
        KS = sb("KS", [P, HP, 2])
        att = sb("att", [P, NT, N])
        attT = sb("attT", [P, NT, N])
        ident = sb("ident", [P, P])
        ident16 = sb("ident16", [P, P], BF16)
        mask16 = sb("mask16", [P, P], BF16)
        ones = sb("ones", [P, 1])
        halves = sb("halves", [P, P])
        omega = sb("omega", [P, 2, P])
        router_w = sb("router_w", [P, 2, DC * HID])
        col = sb("col", [P, NCOLS])
        scol = sb("scol", [P, 3 * DC])
        tcol = sb("tcol", [P, 3 * DC])
        rrow = sb("rrow", [1, 16])
        desc = sb("desc", [1, 4])
        iota16 = sb("iota16", [P, N], BF16)
        edge_i = sb("edge_i", [P, 2, EC], I32)
        edge_f = sb("edge_f", [P, 2, EC])
        ew = sb("ew", [P, 4, EC])
        ew16 = sb("ew16", [P, 2, EC], BF16)
        gmax = sb("gmax", [P, 4])
        bn = sb("bn", [P, NT, 6])
        mv = sb("mv", [P, NT, 2])
        ve = sb("ve", [P, NT])
        rstd = sb("rstd", [P, NT])
        half = sb("half", [P, NT])
        deg = sb("deg", [P, NT])
        dinv = sb("dinv", [P, NT])
        rowsum = sb("rowsum", [P, NT])
        rsum = sb("rsum", [P, NT])
        valid = sb("valid", [P, NT])
        nmax = sb("nmax", [P, H, NT])
        psum_ = sb("psum_", [P, H, NT])
        rprob = sb("rprob", [P, NT, H])
        den = sb("den", [P, NT, H])
        pool_c = sb("pool_c", [P, DC])
        hid_c = sb("hid_c", [P, 1])
        r = sb("r", [1, 64])
        ridx = sb("ridx", [1, 4], I32)
        hot = big[:, :].bitcast(BF16).rearrange("p (b c k n) -> p b c k n", b=2, c=EG, k=4)
        hotlo = big2[:, :].bitcast(BF16).rearrange("p (b c n) -> p b c n", b=2, c=EG)
        G = big[:, :].rearrange("p (c n) -> p c n", c=FC)
        cnt, adj = SP[:, 0:2, :], SP[:, 2:4, :]
        hg = ZN
        msg = SP
        mfeat = TM[:, 0:2, :]
        hgr = TM[:, 2, :].rearrange("p (t f) -> p t f", t=NT)
        zT = TM[:, 3, :]
        kphi_m, qphi_m = K[:, :, :].rearrange("p (t a) n -> p t (a n)", t=NT), Q
        kphi_p, qphi_p = O, XT2
        ksq, qsq = ZN[:, :, :].rearrange("p t (a n) -> p (t a) n", n=N), OT

        banks = [ctx.enter_context(nc.psum_tensor(f"bank{i}", [P, 512], F32)) for i in range(8)]
        acc = banks[6:8]

        slot_loaded = [sem(f"slot_loaded{i}") for i in range(SLOTS)]
        row_loaded = [sem(f"row_loaded{i}") for i in range(ROWS)]
        full = [sem(f"bank_full{i}") for i in range(ROTATING)]
        read = [sem(f"bank_read{i}") for i in range(ROTATING)]
        acc_full, acc_read = sem("acc_full"), sem("acc_read")
        x_loaded, edges_loaded, params_loaded = sem("x_loaded"), sem("edges_loaded"), sem("params_loaded")
        scol_loaded, tcol_loaded = sem("scol_loaded"), sem("tcol_loaded")
        consts = sem("consts")
        gate_max, gate_all, gate_neg, gate_exp = sem("gate_max"), sem("gate_all"), sem("gate_neg"), sem("gate_exp")
        hots_ready, hots_used = sem("hots_ready"), sem("hots_used")
        ln_var, ln_rstd, ln_out = sem("ln_var"), sem("ln_rstd"), sem("ln_out")
        deg_ready, dinv_ready = sem("deg_ready"), sem("dinv_ready")
        adj_ready, att_ready = sem("adj_ready"), sem("att_ready")
        phi_in, phi_exp, phi_ready = sem("phi_in"), sem("phi_exp"), sem("phi_ready")
        score_max = sem("score_max")
        logit_max, logit_exp, route_ready = sem("logit_max"), sem("logit_exp"), sem("route_ready")
        x4_ready, xx_ready, out_ready, out_stored = sem("x4_ready"), sem("xx_ready"), sem("out_ready"), sem("out_stored")
        dve_step = sem("dve_step")

        def bank(job):
            return banks[TURN[job][1]]

        def filled(eng, job):
            eng.wait_ge(full[TURN[job][1]], TURN[job][0] + 1)

        def stored(eng, job):
            eng.wait_ge(read[TURN[job][1]], TURN[job][0] + 1)

        def full_of(job):
            return full[TURN[job][1]]

        def read_of(job):
            return read[TURN[job][1]]

        def slot(w):
            return WEIGHTS.index(w) % SLOTS

        def row(name):
            return rslot[:, BIAS_ROWS.index(name) % ROWS, :]

        def column(name, i=0):
            return col[:, COLS[name][0] + i:COLS[name][0] + i + 1]

        def token(t):
            return slice(t * P, (t + 1) * P)

        block = ctx.enter_context(nc.Block())

        @block.sync
        def _(sp):
            for t in range(NT):
                sp.dma_start(X[:, t, :], x[t * P:(t + 1) * P, :]).then_inc(x_loaded, 16)
            sp.dma_start(edge_i[:, :, :], edges).then_inc(edges_loaded, 16)
            sp.dma_start(ew[:, 0, :], gate).then_inc(edges_loaded, 16)

            index = {}

            def load_row(name):
                i = BIAS_ROWS.index(name)
                if i >= ROWS:
                    stored(sp, ROW_DONE[BIAS_ROWS[i - ROWS]])
                if name == "sp_v":
                    src = sp_row[bass.ds(index["sp"], 1), :]
                elif name == "tm_v":
                    src = tm_row[bass.ds(index["tm"], 1), :]
                else:
                    j = STATIC_ROWS.index(name)
                    src = rows[j:j + 1, :]
                sp.dma_start(row(name), src.partition_broadcast(P)).then_inc(row_loaded[i % ROWS], 16)

            def load_weight(w):
                i = WEIGHTS.index(w)
                if i >= SLOTS:
                    filled(sp, LAST_JOB[WEIGHTS[i - SLOTS]])
                family, part = (w.split("_") + [""])[:2]
                if family in ("ffn", "sp", "tm"):
                    table = {"ffn": ffn_w, "sp": sp_w, "tm": tm_w}[family]
                    src = table[bass.ds(index[family], 1), PART[part], :, :].rearrange("a p n -> p (a n)")
                else:
                    src = weights[STATIC.index(w), :, :]
                sp.dma_start(wslot[:, i % SLOTS, :], src).then_inc(slot_loaded[i % SLOTS], 16)

            for w in WEIGHTS:
                if w == "ffn_q":
                    sp.wait_ge(route_ready, 1)
                    index["ffn"] = nc.sync.value_load(ridx[0:1, 0:1], min_val=0, max_val=K0 - 1)
                if w == "sp_q":
                    sp.wait_ge(route_ready, 2)
                    index["sp"] = nc.sync.value_load(ridx[0:1, 2:3], min_val=0, max_val=K1 - 1)
                    index["tm"] = nc.sync.value_load(ridx[0:1, 3:4], min_val=0, max_val=K1 - 1)
                for name in ROW_BEFORE.get(w, []):
                    load_row(name)
                load_weight(w)
                if w == "sp_q":
                    sp.dma_start(scol[:, :], sp_cols[bass.ds(index["sp"], 1), :, :].rearrange("a p n -> p (a n)"))\
                      .then_inc(scol_loaded, 16)
                    sp.dma_start(tcol[:, :], tm_cols[bass.ds(index["tm"], 1), :, :].rearrange("a p n -> p (a n)"))\
                      .then_inc(tcol_loaded, 16)
                if w == "mix_k":
                    sp.dma_start(col[:, :], cols).then_inc(params_loaded, 16)
                if w == "mix_p":
                    sp.dma_start(router_w[:, :, :], routers).then_inc(params_loaded, 16)
                    sp.dma_start(rrow[:, :], router_rows).then_inc(params_loaded, 16)
                    sp.wait_ge(consts, ALL_CONSTS)
                    for i in range(2):
                        for b in range(2):
                            sp.dma_start(omega[64 * b:64 * b + 64, i, 64 * b:64 * b + 64], omegas[i, :, :])\
                              .then_inc(params_loaded, 16)
            for t in range(NT):
                sp.wait_ge(out_ready, t + 1)
                sp.dma_start(out[t * P:(t + 1) * P, :], ZN[:, t, :]).then_inc(out_stored, 16)
            sp.wait_ge(out_stored, 16 * NT)

        @block.tensor
        def _(pe):
            mm, transpose = nc.tensor.matmul, nc.tensor.transpose

            def take(job):
                turn, b = TURN[job]
                if turn:
                    pe.wait_ge(read[b], turn)
                return banks[b]

            def weight(w):
                i = WEIGHTS.index(w)
                pe.wait_ge(slot_loaded[i % SLOTS], 16 * (i // SLOTS + 1))
                return wslot[:, i % SLOTS, :]

            def to_features(prefix, src):
                for t in range(NT):
                    ps = take(f"{prefix}.{t}")
                    for c in range(DC):
                        last = transpose(ps[:, token(c)], src[:, t, token(c)], ident[:, :])
                    last.then_inc(full_of(f"{prefix}.{t}"), 1)

            def per_token(w, src, t):
                ws, ps = weight(w), take(f"{w}.{t}")
                for c in range(DC):
                    last = mm(ps[:, :], src[:, c, token(t)], ws[:, c * D:(c + 1) * D], start=c == 0, stop=c == DC - 1)
                last.then_inc(full_of(f"{w}.{t}"), 1)

            def per_feature(w, src, j, job=None):
                ws, ps = weight(w), take(job or f"{w}.{j % 2}")
                for f in range(2):
                    for c in range(DC):
                        at = c * D + (2 * (j % 2) + f) * P
                        last = mm(ps[:, f * N:(f + 1) * N], ws[:, at:at + P], src[:, c, :], start=c == 0,
                                  stop=c == DC - 1)
                last.then_inc(full_of(job or f"{w}.{j % 2}"), 1)

            def edge_group(g):
                pe.wait_ge(hots_ready, g + 1)
                for c in range(EG):
                    h = hot[:, g % 2, c, :, :]
                    for t in range(NT):
                        src = h[:, 0, token(t)]
                        mm(acc[t][:, :], src, h[:, 1:3, :], start=g == c == 0, stop=False, skip_group_check=True)
                        mm(acc[t][:, N:], src, h[:, 3, :], start=False, stop=False, skip_group_check=True)
                        last = mm(acc[t][:, N:], src, hotlo[:, g % 2, c, :], start=False,
                                  stop=g == EC // EG - 1 and c == EG - 1, skip_group_check=True)
                last.then_inc(hots_used, 1)

            def linear_attention(name, kphi, qphi, v, first):
                pe.wait_ge(phi_ready, first + 2)
                ps = take(f"{name}.ks")
                for p in range(HP):
                    for t in range(NT):
                        last = mm(ps[:, p:p + 1], kphi[:, t, token(p)], ones[:, :], start=t == 0, stop=t == NT - 1)
                last.then_inc(full_of(f"{name}.ks"), 1)
                ps = take(f"{name}.kv")
                for p in range(HP):
                    for t in range(NT):
                        last = mm(ps[:, token(p)], kphi[:, t, token(p)], v[:, t, token(p)], start=t == 0,
                                  stop=t == NT - 1)
                last.then_inc(full_of(f"{name}.kv"), 1)
                pe.wait_ge(phi_ready, first + 4)
                stored(pe, f"{name}.ks")
                ps = take(f"{name}.den")
                for t in range(NT):
                    for p in range(HP):
                        at = t * H + 2 * p
                        last = mm(ps[:, at:at + 2], qphi[:, p, token(t)], KS[:, p, :], start=True, stop=True)
                last.then_inc(full_of(f"{name}.den"), 1)
                stored(pe, f"{name}.kv")
                for t in range(NT):
                    ps = take(f"{name}.num.{t}")
                    for p in range(HP):
                        last = mm(ps[:, token(p)], qphi[:, p, token(t)], KV[:, p, :], start=True, stop=True)
                    last.then_inc(full_of(f"{name}.num.{t}"), 1)

            def heads_to_features(name):
                for t in range(NT):
                    if name in ATTENTIONS:
                        pe.wait_ge(acc_read, 1 + 2 * ATTENTIONS.index(name) + t + 1)
                    else:
                        stored(pe, f"{name}.num.{t}")
                    ps = take(f"{name}.oT.{t}")
                    for c in range(DC):
                        last = transpose(ps[:, token(c)], O[:, t, token(c)], ident[:, :])
                    last.then_inc(full_of(f"{name}.oT.{t}"), 1)

            def router(n):
                ps = take(f"r{n}.pool")
                for c in range(DC):
                    for t in range(NT):
                        last = mm(ps[:, c:c + 1], XN[:, t, token(c)], ones[:, :], start=t == 0, stop=t == NT - 1)
                last.then_inc(full_of(f"r{n}.pool"), 1)

            def router_hidden(n):
                pe.wait_ge(params_loaded, 16 * 7)
                stored(pe, f"r{n}.pool")
                ps = take(f"r{n}.hid")
                for c in range(DC):
                    last = mm(ps[:, 0:1], router_w[:, n, token(c)], pool_c[:, c:c + 1], start=c == 0, stop=c == DC - 1)
                last.then_inc(full_of(f"r{n}.hid"), 1)
                stored(pe, f"r{n}.hid")
                ps = take(f"r{n}.out")
                a, b = COLS[f"r{n}_w2"]
                mm(ps[0:1, 0:b - a], hid_c[:, :], col[:, a:b], start=True, stop=True)\
                    .then_inc(full_of(f"r{n}.out"), 1)

            def attention(name):
                a, causal = ATTENTIONS.index(name), name == "tm"

                def scores(h):
                    ps = take(f"{name}.s{h}")
                    lo = 64 * (h % 2)
                    q, k = Q[lo:lo + 64, h // 2, :], K[lo:lo + 64, h // 2, :]
                    for t in range(NT):
                        keys = (t + 1) * P if causal else N
                        last = mm(ps[:, t * N:t * N + keys], q[:, token(t)], k[:, 0:keys], start=True, stop=True)
                        if causal:
                            last = mm(ps[:, t * N + keys - P:t * N + keys], ident16[:, :], mask16[:, :], start=False,
                                      stop=True, skip_group_check=True)
                    last.then_inc(full_of(f"{name}.s{h}"), 1)

                def turn_probs(h):
                    stored(pe, f"{name}.s{h}")
                    ps = take(f"{name}.t{h}")
                    for i, (k, q) in enumerate([(0, 0), (0, 1), (1, 1)] + [(1, 0)] * (not causal)):
                        last = transpose(ps[:, token(i)], PR[:, h % 4, q * N + k * P:q * N + (k + 1) * P], ident[:, :])
                    last.then_inc(full_of(f"{name}.t{h}"), 1)

                def values(h):
                    stored(pe, f"{name}.t{h}")
                    if h == 0:
                        pe.wait_ge(acc_read, 1 + NT * a)
                    pt = PT[:, h % 4, :]
                    for t in range(NT):
                        o = acc[t][:, 64 * h:64 * h + 64]
                        first = pt[:, token(t)]
                        last = mm(o, first, V[:, 0, 64 * h:64 * h + 64], start=True, stop=causal and t == 0)
                        if not (causal and t == 0):
                            last = mm(o, pt[:, token(3 - t)], V[:, 1, 64 * h:64 * h + 64], start=False, stop=True)
                    return last

                for i in range(H + 3):
                    if i < H:
                        scores(i)
                    if 0 <= i - 2 < H:
                        turn_probs(i - 2)
                    if 0 <= i - 3:
                        last = values(i - 3)
                last.then_inc(acc_full, 1)

            pe.wait_ge(consts, FIRST_CONSTS)
            pe.wait_ge(ln_out, 2 * LN_IN0 + 2)
            to_features("xT0", XN)
            for t in range(NT):
                stored(pe, f"xT0.{t}")
            pe.wait_ge(consts, ALL_CONSTS)
            for t in range(NT):
                per_token("mix_k", XT, t)
            edge_group(0)
            for t in range(NT):
                per_token("mix_v", XT, t)
            edge_group(1)
            for j in range(2):
                per_feature("mix_q", XT, j)
            edge_group(2)
            for t in range(NT):
                per_token("gnn", XT, t)
            edge_group(3)
            for t in range(NT):
                stored(pe, f"mix_v.{t}")
            linear_attention("mix", kphi_m, qphi_m, V, 0)
            edge_group(4)
            edge_group(5)
            heads_to_features("mix")
            edge_group(6)
            edge_group(7)
            pe.wait_ge(acc_read, 1)
            ps = take("cntT")
            for t in range(NT):
                for u in range(NT):
                    last = transpose(ps[:, u * N + t * P:u * N + (t + 1) * P], cnt[:, t, token(u)], ident[:, :])
            last.then_inc(full_of("cntT"), 1)
            for t in range(NT):
                stored(pe, f"mix.oT.{t}")
            per_token("mix_p", OT, 0)
            pe.wait_ge(att_ready, 1)
            ps = take("attT")
            for t in range(NT):
                for u in range(NT):
                    last = transpose(ps[:, u * N + t * P:u * N + (t + 1) * P], att[:, t, token(u)], ident[:, :])
            last.then_inc(full_of("attT"), 1)
            per_token("mix_p", OT, 1)
            pe.wait_ge(adj_ready, 1)
            for t in range(NT):
                stored(pe, f"gnn.{t}")
            for t in range(NT):
                ps = take(f"adj.{t}")
                for u in range(NT):
                    last = mm(ps[:, :], adj[:, u, token(t)], hg[:, u, :], start=u == 0, stop=u == NT - 1)
                last.then_inc(full_of(f"adj.{t}"), 1)

            pe.wait_ge(ln_out, 2 * LN_FFN + 2)
            to_features("xT1", XN)
            router(0)
            router_hidden(0)
            for t in range(NT):
                stored(pe, f"xT1.{t}")
            for w in ("ffn_q", "ffn_k"):
                for j in range(2):
                    per_feature(w, XT, j)
            for t in range(NT):
                per_token("ffn_v", XT, t)
            for w in ("ffn_q", "ffn_k", "ffn_v"):
                for j in range(2):
                    stored(pe, f"{w}.{j}")
            attention("ffn")
            heads_to_features("ffn")
            for t in range(NT):
                stored(pe, f"ffn.oT.{t}")
            for t in range(NT):
                per_token("ffn_o", OT, t)

            pe.wait_ge(ln_out, 2 * LN_IN1 + 2)
            to_features("xT2", XN)
            for t in range(NT):
                stored(pe, f"xT2.{t}")
            gw = weight("graph")
            ps = take("g.feat")
            for t in range(NT):
                for c in range(DC):
                    last = mm(ps[:, t * N:(t + 1) * N], XT[:, c, token(t)], gw[:, c * N:(c + 1) * N], start=c == 0,
                              stop=c == DC - 1)
            last.then_inc(full_of("g.feat"), 1)
            for j in range(2):
                per_feature("per_k", XT, j)
            stored(pe, "g.feat")
            stored(pe, "attT")
            for i, table in enumerate((attT, att)):
                ps = take(f"g.msg.{i}")
                for f in range(2):
                    for u in range(NT):
                        last = mm(ps[:, f * N:(f + 1) * N], mfeat[:, u, token(f)], table[:, u, :], start=u == 0,
                                  stop=u == NT - 1)
                last.then_inc(full_of(f"g.msg.{i}"), 1)
            for t in range(NT):
                per_token("per_v", XT, t)
            for i in range(2):
                stored(pe, f"g.msg.{i}")
            ps = take("g.hid")
            for t in range(NT):
                for c in range(DC):
                    at = DC * N + c * HID
                    last = mm(ps[:, token(t)], msg[:, c, token(t)], gw[:, at:at + HID], start=c == 0, stop=c == DC - 1)
            last.then_inc(full_of("g.hid"), 1)
            for j in range(2):
                per_feature("per_q", XT, j)
            pe.wait_ge(ln_out, 2 * LN_GRAPH + 2)
            ps = take("g.zT")
            for t in range(NT):
                last = transpose(ps[:, token(t)], hgr[:, t, :], ident[:, :])
            last.then_inc(full_of("g.zT"), 1)
            for j in range(2):
                stored(pe, f"per_k.{j}")
            for job, lhs in (("kf", K), ("kn", ksq)):
                for t in range(NT):
                    ps = take(f"per.{job}.{t}")
                    for p in range(HP):
                        last = mm(ps[:, token(p)], lhs[:, p, token(t)], omega[:, 1, :] if job == "kf" else halves[:, :],
                                  start=True, stop=True)
                    last.then_inc(full_of(f"per.{job}.{t}"), 1)
            stored(pe, "g.zT")
            for t in range(NT):
                ps = take(f"g.out.{t}")
                mm(ps[:, :], zT[:, token(t)], gw[:, DC * (N + HID):DC * (N + HID) + D], start=True, stop=True)\
                    .then_inc(full_of(f"g.out.{t}"), 1)
            for j in range(2):
                stored(pe, f"per_q.{j}")
            for job, rhs in (("qf", Q), ("qn", qsq)):
                for j in range(2):
                    ps = take(f"per.{job}.{j}")
                    for f in range(2):
                        last = mm(ps[:, f * N:(f + 1) * N], omega[:, 0, :] if job == "qf" else halves[:, :],
                                  rhs[:, 2 * j + f, :], start=True, stop=True)
                    last.then_inc(full_of(f"per.{job}.{j}"), 1)
            for t in range(NT):
                stored(pe, f"per_v.{t}")
            linear_attention("per", kphi_p, qphi_p, V, 4)
            heads_to_features("per")
            for t in range(NT):
                stored(pe, f"per.oT.{t}")
            for t in range(NT):
                per_token("per_o", OT, t)

            pe.wait_ge(ln_out, 2 * LN_X3 + 2)
            router(1)
            router_hidden(1)
            pe.wait_ge(ln_out, 2 * LN_Z + 2)
            two_chunks(pe, take, transpose, "xT3", ZN, ident, full_of, token)
            for j in range(2):
                stored(pe, f"xT3.{j}")
            for w in ("sp_q", "sp_k"):
                for j in range(2):
                    per_feature(w, XT, j)
            for t in range(NT):
                per_token("sp_v", XT, t)
            for w in ("sp_q", "sp_k", "sp_v"):
                for j in range(2):
                    stored(pe, f"{w}.{j}")
            attention("sp")
            for w in ("tm_q", "tm_k"):
                for j in range(2):
                    per_feature(w, XT2, j)
            for t in range(NT):
                per_token("tm_v", XT2, t)
            heads_to_features("sp")
            for w in ("tm_q", "tm_k", "tm_v"):
                for j in range(2):
                    stored(pe, f"{w}.{j}")
            attention("tm")
            for t in range(NT):
                stored(pe, f"sp.oT.{t}")
            for j in range(2):
                per_feature("sp_o", OT, j)
            for j in range(2):
                stored(pe, f"sp_o.{j}")
            for j in range(2):
                per_feature("cr_q", SP, j)
            heads_to_features("tm")
            for t in range(NT):
                stored(pe, f"tm.oT.{t}")
            for j in range(2):
                per_feature("tm_o", OT, j)
            for j in range(2):
                stored(pe, f"tm_o.{j}")
            for j in range(2):
                per_feature("cr_k", TM, j)
            for t in range(NT):
                per_token("cr_v", TM, t)
            for w in ("cr_q", "cr_k", "cr_v"):
                for j in range(2):
                    stored(pe, f"{w}.{j}")
            attention("cr")
            heads_to_features("cr")
            for t in range(NT):
                stored(pe, f"cr.oT.{t}")
            for t in range(NT):
                per_token("cr_o", OT, t)

            pe.wait_ge(ln_out, 2 * LN_MLP + 2)
            two_chunks(pe, take, transpose, "xT4", ZN, ident, full_of, token)
            for j in range(2):
                stored(pe, f"xT4.{j}")
            for j in range(FC // 2):
                per_feature(f"up_{j // 2}", XT, j, f"up.{j}")
            for t in range(NT):
                ps = take(f"down.{t}")
                for c in range(FC):
                    if t == 0 and c % DC == 0:
                        ws = weight(f"down_{c // DC}")
                    if t == 0 and c % 2 == 0:
                        stored(pe, f"up.{c // 2}")
                    ws = wslot[:, slot(f"down_{c // DC}"), :]
                    last = mm(ps[:, :], G[:, c, token(t)], ws[:, (c % DC) * D:(c % DC + 1) * D], start=c == 0,
                              stop=c == FC - 1)
                last.then_inc(full_of(f"down.{t}"), 1)

        @block.vector
        def _(dve):
            v = nc.vector
            steps = [0]

            def link(ins):
                steps[0] += 1
                ins.then_inc(dve_step, 1)
                dve.wait_ge(dve_step, steps[0])

            def row_there(name):
                i = BIAS_ROWS.index(name)
                dve.wait_ge(row_loaded[i % ROWS], 16 * (i // ROWS + 1))
                return row(name)

            def layernorm(n, src, dst, width=D):
                for t in range(NT):
                    last = v.bn_stats(bn[:, t, :], src[:, t, 0:width])
                link(last)
                for t in range(NT):
                    last = v.bn_aggr(mv[:, t, :], bn[:, t, :])
                link(last)
                v.tensor_scalar(ve[:, :], mv[:, :, 1], EPS, None, ALU.add).then_inc(ln_var, 1)
                dve.wait_ge(ln_rstd, n + 1)
                for t in range(NT):
                    v.tensor_scalar(dst[:, t, 0:width], src[:, t, 0:width], mv[:, t, 0:1], rstd[:, t:t + 1],
                                    ALU.subtract, ALU.mult).then_inc(ln_out, 1)
                dve.wait_ge(ln_out, 2 * n + 2)

            def one_hots(g):
                if g >= 2:
                    dve.wait_ge(hots_used, g - 1)
                for c in range(EG):
                    e = g * EG + c
                    h = hot[:, g % 2, c, :, :]
                    s, d = edge_f[:, 0, e:e + 1], edge_f[:, 1, e:e + 1]
                    v.tensor_scalar(h[:, 0, :], iota16[:, :], s, None, ALU.is_equal)
                    v.tensor_scalar(h[:, 1, :], iota16[:, :], d, None, ALU.is_equal)
                    for i, o in enumerate((h[:, 2, :], h[:, 3, :], hotlo[:, g % 2, c, :])):
                        last = v.tensor_scalar(o, iota16[:, :], d, ew[:, 1 + i, e:e + 1], ALU.is_equal, ALU.mult)
                last.then_inc(hots_ready, 1)

            def to_token_half(prefix, dst):
                job = f"{prefix}.1"
                filled(dve, job)
                v.tensor_copy(dst[:, :, token(1)], bank(job)[:, :].rearrange("p (c n) -> p c n", c=DC))\
                    .then_inc(read_of(job), 1)

            def add_row(job, dst, name):
                filled(dve, job)
                v.tensor_tensor(dst, bank(job)[:, :], row_there(name), ALU.add).then_inc(read_of(job), 1)

            def elu_in(u, job):
                stored(dve, job)
                v.tensor_scalar(PT[:, u, :], PR[:, u, :], 0.0, None, ALU.min).then_inc(phi_in, 1)

            def elu_out(u, dst):
                dve.wait_ge(phi_exp, u + 1)
                v.scalar_tensor_tensor(dst, PR[:, u, :], 0.0, PT[:, u, :], ALU.max, ALU.add).then_inc(phi_ready, 1)

            def diagonals(name):
                filled(dve, f"{name}.ks")
                for b in range(2):
                    s = slice(64 * b, 64 * b + 64)
                    last = v.tensor_copy(KS[s, :, b], bank(f"{name}.ks")[s, 0:HP])
                last.then_inc(read_of(f"{name}.ks"), 1)
                filled(dve, f"{name}.kv")
                for b in range(2):
                    s = slice(64 * b, 64 * b + 64)
                    last = v.tensor_copy(KV[s, :, s], bank(f"{name}.kv")[:, :].rearrange("p (h n) -> p h n", h=HP)[s, :, s])
                last.then_inc(read_of(f"{name}.kv"), 1)

            def by_head(ap):
                return ap.rearrange("p (h d) -> p h d", h=H)

            def linear_out(name):
                filled(dve, f"{name}.den")
                v.reciprocal(den[:, :, :].rearrange("p t h -> p (t h)"), bank(f"{name}.den")[:, 0:NT * H])\
                    .then_inc(read_of(f"{name}.den"), 1)
                stored(dve, f"{name}.den")
                for t in range(NT):
                    job = f"{name}.num.{t}"
                    filled(dve, job)
                    v.tensor_tensor(by_head(O[:, t, :]), by_head(bank(job)[:, :]),
                                    den[:, t, :].unsqueeze(2).broadcast_to([P, H, 64]), ALU.mult)\
                        .then_inc(read_of(job), 1)

            def route(n, k, groups):
                w = k * groups
                a, b = (0, K0) if n == 0 else (K0, K0 + 2 * K1)
                lg, pr, hit, at = r[:, 0:w], r[:, 8:8 + w], r[:, 16:16 + w], r[:, 24:24 + groups]
                grouped = lambda ap: ap.rearrange("p (g k) -> p g k", g=groups)
                filled(dve, f"r{n}.out")
                v.tensor_tensor(lg, bank(f"r{n}.out")[0:1, 0:w], rrow[:, a:b], ALU.add).then_inc(read_of(f"r{n}.out"), 1)
                stored(dve, f"r{n}.out")
                v.tensor_reduce(r[:, 32:33], lg, AX.X, ALU.max, negate=True).then_inc(logit_max, 1)
                dve.wait_ge(logit_exp, n + 1)
                link(v.reciprocal(r[:, 33:34], r[:, 34:35]))
                link(v.tensor_scalar(lg, pr, r[:, 33:34], None, ALU.mult))
                link(v.tensor_reduce(r[:, 26:26 + groups], grouped(lg), AX.X, ALU.max))
                link(v.tensor_tensor(grouped(hit), grouped(lg), r[:, 26:26 + groups].unsqueeze(2)
                                     .broadcast_to([1, groups, k]), ALU.is_ge))
                link(v.tensor_tensor(grouped(hit), grouped(hit), desc[:, 4 - k:4].unsqueeze(1)
                                     .broadcast_to([1, groups, k]), ALU.mult))
                link(v.tensor_reduce(at, grouped(hit), AX.X, ALU.max))
                link(v.tensor_scalar(at, at, -1.0, float(k), ALU.mult, ALU.add))
                v.tensor_scalar(ridx[:, 2 * n:2 * n + groups], at, float(k - 1), None, ALU.min).then_inc(route_ready, 1)

            def attention(name):
                a, causal = ATTENTIONS.index(name), name == "tm"
                for i in range(H + 2):
                    if i < H:
                        filled(dve, f"{name}.s{i}")
                        ps = bank(f"{name}.s{i}")
                        if causal:
                            v.tensor_reduce(nmax[:, i, 0:1], ps[:, 0:P], AX.X, ALU.max, negate=True)
                            v.tensor_reduce(nmax[:, i, 1:2], ps[:, N:2 * N], AX.X, ALU.max, negate=True)\
                                .then_inc(score_max, 1)
                        else:
                            v.tensor_reduce(nmax[:, i, :], ps[:, :].rearrange("p (t n) -> p t n", t=NT), AX.X, ALU.max,
                                            negate=True).then_inc(score_max, 1)
                    if i >= 2:
                        h, w = i - 2, 3 * P if causal else 4 * P
                        filled(dve, f"{name}.t{h}")
                        v.tensor_copy(PT[:, h % 4, 0:w], bank(f"{name}.t{h}")[:, 0:w]).then_inc(read_of(f"{name}.t{h}"), 1)
                stored(dve, f"{name}.s{H - 1}")
                link(v.reciprocal(rprob[:, :, :].rearrange("p t h -> p h t"), psum_[:, :, :]))
                dve.wait_ge(acc_full, a + 1)
                for t in range(NT):
                    v.tensor_tensor(by_head(O[:, t, :]), by_head(acc[t][:, :]),
                                    rprob[:, t, :].unsqueeze(2).broadcast_to([P, H, 64]), ALU.mult).then_inc(acc_read, 1)

            def add_to_x(job):
                t = int(job[-1])
                filled(dve, job)
                v.tensor_tensor(X[:, t, :], bank(job)[:, :], X[:, t, :], ALU.add).then_inc(read_of(job), 1)
                stored(dve, job)

            def scale_shift(prefix, dst, w, b):
                for j in range(2):
                    filled(dve, f"{prefix}.{j}")
                    for f in range(2):
                        c = 2 * j + f
                        last = v.tensor_scalar(dst[:, c, :], bank(f"{prefix}.{j}")[:, f * N:(f + 1) * N], column(w, c),
                                               column(b, c), ALU.mult, ALU.add)
                    yield last, f"{prefix}.{j}"

            dve.wait_ge(edges_loaded, 32)
            v.tensor_copy(edge_f[:, :, :], edge_i[:, :, :])
            v.tensor_reduce(gmax[:, 0:1], ew[:, 0, :], AX.X, ALU.max).then_inc(gate_max, 1)
            dve.wait_ge(x_loaded, 16 * NT)
            layernorm(LN_IN0, X, XN)
            dve.wait_ge(gate_all, 1)
            v.tensor_scalar(gmax[:, 2:3], gmax[:, 1:2], 0.0, -1.0, ALU.max, ALU.mult).then_inc(gate_neg, 1)
            dve.wait_ge(gate_exp, 1)
            link(v.tensor_copy(ew16[:, 0, :], ew[:, 1, :]))
            link(v.tensor_tensor(ew[:, 2, :], ew[:, 1, :], ew16[:, 0, :], ALU.subtract))
            link(v.tensor_copy(ew16[:, 1, :], ew[:, 2, :]))
            link(v.tensor_tensor(ew[:, 3, :], ew[:, 2, :], ew16[:, 1, :], ALU.subtract))
            to_token_half("xT0", XT)

            dve.wait_ge(consts, ALL_CONSTS)
            one_hots(0)
            for t in range(NT):
                job = f"mix_k.{t}"
                filled(dve, job)
                v.tensor_tensor(PR[:, t, :], bank(job)[:, :], row_there("mix_k"), ALU.add).then_inc(read_of(job), 1)
                elu_in(t, job)
            one_hots(1)
            for t in range(NT):
                elu_out(t, kphi_m[:, t, :])
            for t in range(NT):
                add_row(f"mix_v.{t}", V[:, t, :], "mix_v")
            one_hots(2)
            for j in range(2):
                job = f"mix_q.{j}"
                filled(dve, job)
                for f in range(2):
                    last = v.tensor_scalar(PR[:, 2 + j, f * N:(f + 1) * N], bank(job)[:, f * N:(f + 1) * N],
                                           column("mix_bq", 2 * j + f), None, ALU.add)
                last.then_inc(read_of(job), 1)
                elu_in(2 + j, job)
            one_hots(3)
            for j in range(2):
                elu_out(2 + j, qphi_m[:, 2 * j:2 * j + 2, :].rearrange("p c n -> p (c n)"))
            diagonals("mix")
            one_hots(4)
            linear_out("mix")
            one_hots(5)
            to_token_half("mix.oT", OT)
            one_hots(6)
            one_hots(7)

            dve.wait_ge(hots_used, EC // EG)
            for t in range(NT):
                v.tensor_scalar(cnt[:, t, :], acc[t][:, 0:N], 1.0, None, ALU.min)
                last = v.tensor_copy(att[:, t, :], acc[t][:, N:])
            last.then_inc(acc_read, 1)
            dve.wait_ge(acc_read, 1)
            link(v.tensor_reduce(rowsum[:, :], att[:, :, :], AX.X, ALU.add))
            v.tensor_scalar(valid[:, :], rowsum[:, :], 0.0, None, ALU.is_gt)
            link(v.tensor_scalar(rsum[:, :], rowsum[:, :], 1e-6, None, ALU.add))
            link(v.reciprocal(rsum[:, :], rsum[:, :]))
            for t in range(NT):
                last = v.tensor_scalar(att[:, t, :], att[:, t, :], rsum[:, t:t + 1], None, ALU.mult)
            last.then_inc(att_ready, 1)
            filled(dve, "cntT")
            for t in range(NT):
                last = v.tensor_tensor(adj[:, t, :], bank("cntT")[:, t * N:(t + 1) * N], cnt[:, t, :], ALU.max)
            last.then_inc(read_of("cntT"), 1)
            stored(dve, "cntT")
            for t in range(NT):
                last = v.tensor_tensor(adj[:, t, token(t)], adj[:, t, token(t)], ident[:, :], ALU.add)
            link(last)
            v.tensor_reduce(deg[:, :], adj[:, :, :], AX.X, ALU.add).then_inc(deg_ready, 1)
            add_to_x("mix_p.0")
            dve.wait_ge(dinv_ready, 1)
            for t in range(NT):
                last = v.tensor_scalar(adj[:, t, :], adj[:, t, :], dinv[:, t:t + 1], None, ALU.mult)
            last.then_inc(adj_ready, 1)
            filled(dve, "attT")
            v.tensor_copy(attT[:, :, :].rearrange("p t n -> p (t n)"), bank("attT")[:, :]).then_inc(read_of("attT"), 1)
            add_to_x("mix_p.1")
            for name in ("gnn", "mix_p"):
                for t in range(NT):
                    last = v.tensor_tensor(X[:, t, :], X[:, t, :], row_there(name), ALU.add)
                link(last)
            for t in range(NT):
                job = f"adj.{t}"
                filled(dve, job)
                last = v.scalar_tensor_tensor(X[:, t, :], bank(job)[:, :], dinv[:, t:t + 1], X[:, t, :], ALU.mult, ALU.add)
                last.then_inc(read_of(job), 1)
                stored(dve, job)

            layernorm(LN_FFN, X, XN)
            to_token_half("xT1", XT)

            def pooled(n):
                filled(dve, f"r{n}.pool")
                v.tensor_scalar(pool_c[:, :], bank(f"r{n}.pool")[:, 0:DC], 1.0 / N, None, ALU.mult)\
                    .then_inc(read_of(f"r{n}.pool"), 1)

            pooled(0)
            filled(dve, "r0.hid")
            v.tensor_scalar(hid_c[:, :], bank("r0.hid")[:, 0:1], column("r0_b1"), 0.0, ALU.add, ALU.max)\
                .then_inc(read_of("r0.hid"), 1)
            dve.wait_ge(params_loaded, 16 * 7)
            route(0, K0, 1)
            for j in range(2):
                job = f"ffn_k.{j}"
                filled(dve, job)
                v.tensor_copy(K[:, 2 * j:2 * j + 2, :].rearrange("p c n -> p (c n)"), bank(job)[:, :])\
                    .then_inc(read_of(job), 1)
            filled(dve, "ffn_v.1")
            v.tensor_copy(V[:, 1, :], bank("ffn_v.1")[:, :]).then_inc(read_of("ffn_v.1"), 1)
            attention("ffn")
            to_token_half("ffn.oT", OT)
            for t in range(NT):
                add_to_x(f"ffn_o.{t}")

            layernorm(LN_IN1, X, XN)
            to_token_half("xT2", XT)
            filled(dve, "g.feat")
            brow = row_there("graph_in")
            v.tensor_tensor(mfeat, bank("g.feat")[:, :].rearrange("p (t n) -> p t n", t=NT),
                            brow[:, 0:N].unsqueeze(1).broadcast_to([P, NT, N]), ALU.add).then_inc(read_of("g.feat"), 1)
            for i in range(2):
                job = f"g.msg.{i}"
                filled(dve, job)
                v.tensor_copy(msg[:, 2 * i:2 * i + 2, :].rearrange("p c n -> p (c n)"), bank(job)[:, :])\
                    .then_inc(read_of(job), 1)
            filled(dve, "per_v.1")
            v.tensor_copy(V[:, 1, :], bank("per_v.1")[:, :]).then_inc(read_of("per_v.1"), 1)
            filled(dve, "g.hid")
            v.tensor_tensor(hgr, bank("g.hid")[:, 0:N].rearrange("p (t n) -> p t n", t=NT),
                            brow[:, N:N + HID].unsqueeze(1).broadcast_to([P, NT, HID]), ALU.add)\
                .then_inc(read_of("g.hid"), 1)
            stored(dve, "g.hid")
            layernorm(LN_GRAPH, hgr, hgr, HID)
            filled(dve, "g.zT")
            link(v.tensor_scalar(zT, bank("g.zT")[:, 0:N], column("gamma"), column("beta"), ALU.mult, ALU.add))
            v.tensor_scalar(zT, zT, 0.0, None, ALU.max).then_inc(read_of("g.zT"), 1)

            def exp_in(u, f_job, n_job):
                filled(dve, f_job)
                v.tensor_scalar(PR[:, u, :], bank(f_job)[:, :], 50.0, None, ALU.min).then_inc(read_of(f_job), 1)
                filled(dve, n_job)
                v.tensor_scalar(PT[:, u, :], bank(n_job)[:, :], 1e-16, -0.5, ALU.max, ALU.mult)\
                    .then_inc(read_of(n_job), 1)

            def exp_out(u, dst):
                dve.wait_ge(phi_exp, 4 + u + 1)
                v.scalar_tensor_tensor(dst, PT[:, u, :], 1e-8, PR[:, u, :], ALU.max, ALU.mult).then_inc(phi_ready, 1)

            for t in range(NT):
                exp_in(t, f"per.kf.{t}", f"per.kn.{t}")
            for t in range(NT):
                job = f"g.out.{t}"
                filled(dve, job)
                v.tensor_tensor(O[:, t, :], bank(job)[:, :], row_there("graph_out"), ALU.add).then_inc(read_of(job), 1)
                stored(dve, job)
                link(v.tensor_scalar(O[:, t, :], O[:, t, :], 0.0, valid[:, t:t + 1], ALU.max, ALU.mult))
                link(v.tensor_tensor(X[:, t, :], X[:, t, :], O[:, t, :], ALU.add))
            for t in range(NT):
                exp_out(t, kphi_p[:, t, :])
            for j in range(2):
                exp_in(2 + j, f"per.qf.{j}", f"per.qn.{j}")
            for j in range(2):
                exp_out(2 + j, qphi_p[:, 2 * j:2 * j + 2, :].rearrange("p c n -> p (c n)"))
            diagonals("per")
            linear_out("per")
            to_token_half("per.oT", OT)
            for t in range(NT):
                add_to_x(f"per_o.{t}")

            layernorm(LN_X3, X, XN)
            pooled(1)
            layernorm(LN_Z, XN, ZN)
            route(1, K1, 2)
            for last, job in scale_shift("xT3", XT, "ns_w", "ns_b"):
                last.then_inc(phi_in, 1)
            dve.wait_ge(scol_loaded, 16)
            for j in range(2):
                job = f"sp_q.{j}"
                filled(dve, job)
                for f in range(2):
                    c = 2 * j + f
                    last = v.tensor_scalar(Q[:, c, :], bank(job)[:, f * N:(f + 1) * N], scol[:, c:c + 1], SCALE, ALU.add,
                                           ALU.mult)
                last.then_inc(read_of(job), 1)
            for t in range(NT):
                add_row(f"sp_v.{t}", V[:, t, :], "sp_v")
            attention("sp")
            dve.wait_ge(tcol_loaded, 16)
            for j in range(2):
                job = f"tm_q.{j}"
                filled(dve, job)
                for f in range(2):
                    c = 2 * j + f
                    last = v.tensor_scalar(Q[:, c, :], bank(job)[:, f * N:(f + 1) * N], tcol[:, c:c + 1], SCALE, ALU.add,
                                           ALU.mult)
                last.then_inc(read_of(job), 1)
            for t in range(NT):
                add_row(f"tm_v.{t}", V[:, t, :], "tm_v")
            to_token_half("sp.oT", OT)
            attention("tm")
            for j in range(2):
                job = f"cr_q.{j}"
                filled(dve, job)
                for f in range(2):
                    c = 2 * j + f
                    last = v.tensor_scalar(Q[:, c, :], bank(job)[:, f * N:(f + 1) * N], column("cr_bq", c), SCALE, ALU.add,
                                           ALU.mult)
                last.then_inc(read_of(job), 1)
            to_token_half("tm.oT", OT)
            for j in range(2):
                job = f"tm_o.{j}"
                filled(dve, job)
                for f in range(2):
                    c = 2 * j + f
                    last = v.scalar_tensor_tensor(TM[:, c, :], bank(job)[:, f * N:(f + 1) * N],
                                                  tcol[:, 2 * DC + c:2 * DC + c + 1], XT2[:, c, :], ALU.add, ALU.add)
                last.then_inc(read_of(job), 1)
            for t in range(NT):
                add_row(f"cr_v.{t}", V[:, t, :], "cr_v")
            attention("cr")
            to_token_half("cr.oT", OT)
            for t in range(NT):
                job = f"cr_o.{t}"
                filled(dve, job)
                v.tensor_tensor(O[:, t, :], bank(job)[:, :], row_there("cr_o"), ALU.add).then_inc(read_of(job), 1)
                stored(dve, job)
                v.tensor_tensor(XN[:, t, :], XN[:, t, :], O[:, t, :], ALU.add).then_inc(x4_ready, 1)
            dve.wait_ge(x4_ready, NT)
            layernorm(LN_MLP, XN, ZN)
            for last, job in scale_shift("xT4", XT, "nm_w", "nm_b"):
                last.then_inc(read_of(job), 1)
            dve.wait_ge(xx_ready, 1)
            for t in range(NT):
                job = f"down.{t}"
                filled(dve, job)
                v.tensor_tensor(O[:, t, :], bank(job)[:, :], row_there("down"), ALU.add).then_inc(read_of(job), 1)
                stored(dve, job)
                v.tensor_tensor(ZN[:, t, :], O[:, t, :], X[:, t, :], ALU.add).then_inc(out_ready, 1)

        @block.scalar
        def _(act):
            s = nc.scalar

            def to_token_half(prefix, dst):
                job = f"{prefix}.0"
                filled(act, job)
                s.copy(dst[:, :, token(0)], bank(job)[:, :].rearrange("p (c n) -> p c n", c=DC)).then_inc(read_of(job), 1)

            def elu_exp(u):
                act.wait_ge(phi_in, u + 1)
                s.activation(PT[:, u, :], PT[:, u, :], ACT.Exp).then_inc(phi_exp, 1)

            def performer_exp(u, job):
                stored(act, job)
                s.activation(PT[:, u, :], PT[:, u, :], ACT.Exp)
                s.activation(PR[:, u, :], PR[:, u, :], ACT.Exp).then_inc(phi_exp, 1)

            def attention(name):
                a, causal = ATTENTIONS.index(name), name == "tm"
                for h in range(H):
                    act.wait_ge(score_max, H * a + h + 1)
                    if h >= 4:
                        filled(act, f"{name}.t{h - 4}")
                    for t in range(NT):
                        keys = P if causal and t == 0 else N
                        last = s.activation(PR[:, h % 4, t * N:t * N + keys], bank(f"{name}.s{h}")[:, t * N:t * N + keys],
                                            ACT.Exp, bias=nmax[:, h, t:t + 1], accum_out=psum_[:, h, t:t + 1])
                    last.then_inc(read_of(f"{name}.s{h}"), 1)

            def by_chunk(job, dst, bias, j):
                filled(act, job)
                for f in range(2):
                    last = s.activation(dst[:, 2 * j + f, :], bank(job)[:, f * N:(f + 1) * N], ACT.Identity, bias=bias(2 * j + f))
                last.then_inc(read_of(job), 1)

            def scaled(job, dst, j, square=None):
                filled(act, job)
                flat = lambda ap: ap[:, 2 * j:2 * j + 2, :].rearrange("p c n -> p (c n)")
                last = s.activation(flat(dst), bank(job)[:, :], ACT.Copy, scale=SCALE)
                if square is not None:
                    last = s.activation(flat(square), bank(job)[:, :], ACT.Square, scale=SCALE)
                last.then_inc(read_of(job), 1)

            act.wait_ge(gate_neg, 1)
            s.activation(ew[:, 1, :], ew[:, 0, :], ACT.Exp, bias=gmax[:, 2:3]).then_inc(gate_exp, 1)
            to_token_half("xT0", XT)
            for u in range(4):
                elu_exp(u)
            for t in range(NT):
                filled(act, f"gnn.{t}")
                s.copy(hg[:, t, :], bank(f"gnn.{t}")[:, :]).then_inc(read_of(f"gnn.{t}"), 1)
            to_token_half("mix.oT", OT)
            to_token_half("xT1", XT)
            act.wait_ge(logit_max, 1)
            s.activation(r[:, 8:8 + K0], r[:, 0:K0], ACT.Exp, bias=r[:, 32:33], accum_out=r[:, 34:35]).then_inc(logit_exp, 1)
            for j in range(2):
                scaled(f"ffn_q.{j}", Q, j)
            filled(act, "ffn_v.0")
            s.copy(V[:, 0, :], bank("ffn_v.0")[:, :]).then_inc(read_of("ffn_v.0"), 1)
            attention("ffn")
            to_token_half("ffn.oT", OT)
            to_token_half("xT2", XT)
            for j in range(2):
                scaled(f"per_k.{j}", K, j, ksq)
            filled(act, "per_v.0")
            s.copy(V[:, 0, :], bank("per_v.0")[:, :]).then_inc(read_of("per_v.0"), 1)
            for j in range(2):
                scaled(f"per_q.{j}", Q, j, qsq)
            for u, job in enumerate(both("per.kn", "per.qn")):
                performer_exp(u, job)
            to_token_half("per.oT", OT)
            filled(act, "r1.hid")
            s.activation(hid_c[:, :], bank("r1.hid")[:, 0:1], ACT.Gelu, bias=column("r1_b1")).then_inc(read_of("r1.hid"), 1)
            act.wait_ge(logit_max, 2)
            s.activation(r[:, 8:8 + 2 * K1], r[:, 0:2 * K1], ACT.Exp, bias=r[:, 32:33], accum_out=r[:, 34:35])\
                .then_inc(logit_exp, 1)
            for j in range(2):
                job = f"xT3.{j}"
                act.wait_ge(phi_in, 4 + j + 1)
                for f in range(2):
                    c = 2 * j + f
                    last = s.activation(XT2[:, c, :], bank(job)[:, f * N:(f + 1) * N], ACT.Identity, bias=column("nt_b", c),
                                        scale=column("nt_w", c))
                last.then_inc(read_of(job), 1)
            act.wait_ge(scol_loaded, 16)
            for j in range(2):
                by_chunk(f"sp_k.{j}", K, lambda c: scol[:, DC + c:DC + c + 1], j)
            attention("sp")
            act.wait_ge(tcol_loaded, 16)
            for j in range(2):
                by_chunk(f"tm_k.{j}", K, lambda c: tcol[:, DC + c:DC + c + 1], j)
            to_token_half("sp.oT", OT)
            attention("tm")
            for j in range(2):
                by_chunk(f"sp_o.{j}", SP, lambda c: scol[:, 2 * DC + c:2 * DC + c + 1], j)
            to_token_half("tm.oT", OT)
            for j in range(2):
                by_chunk(f"cr_k.{j}", K, lambda c: column("cr_bk", c), j)
            attention("cr")
            to_token_half("cr.oT", OT)
            for j in range(FC // 2):
                job = f"up.{j}"
                filled(act, job)
                for f in range(2):
                    c = 2 * j + f
                    last = s.activation(G[:, c, :], bank(job)[:, f * N:(f + 1) * N], ACT.Gelu, bias=column("up_b", c))
                last.then_inc(read_of(job), 1)

        @block.gpsimd
        def _(pool):
            g = nc.gpsimd
            made = [0]

            def make(ins):
                made[0] += 1
                ins.then_inc(consts, 1)
                pool.wait_ge(consts, made[0])

            def diagonal(tile):
                make(g.memset(tile[:, :], 0.0))
                make(g.affine_select(out=tile[:, :], in_=tile[:, :], compare_op=ALU.not_equal, fill=1.0, base=0,
                                     pattern=[[-1, P]], channel_multiplier=1))

            def rsqrt(out, in_, wait, value, done):
                pool.wait_ge(wait, value)
                g.tensor_tensor(out[:, :], in_[:, :], half[:, :], ALU.pow).then_inc(done, 1)
                pool.wait_ge(done, value)

            diagonal(ident)
            make(g.memset(half[:, :], -0.5))
            assert made[0] == FIRST_CONSTS
            pool.wait_ge(gate_max, 1)
            g.partition_all_reduce(gmax[:, 1:2], gmax[:, 0:1], P, bass.bass_isa.ReduceOp.max).then_inc(gate_all, 1)
            pool.wait_ge(gate_all, 1)
            rsqrt(rstd, ve, ln_var, 1, ln_rstd)
            make(g.iota(iota16[:, :], [[1, N]], base=0, channel_multiplier=0, allow_small_or_imprecise_dtypes=True))
            make(g.iota(desc[:, :], [[-1, 4]], base=4, channel_multiplier=0, allow_small_or_imprecise_dtypes=True))
            diagonal(ident16)
            make(g.memset(mask16[:, :], 0.0))
            make(g.affine_select(out=mask16[:, :], in_=mask16[:, :], compare_op=ALU.is_ge, fill=MASKED, base=0,
                                 pattern=[[-1, P]], channel_multiplier=1))
            make(g.memset(ones[:, :], 1.0))
            make(g.memset(halves[:, :], 0.0))
            for b in range(2):
                s = slice(64 * b, 64 * b + 64)
                make(g.memset(halves[s, s], 1.0))
            make(g.memset(KV[:, :, :], 0.0))
            make(g.memset(KS[:, :, :], 0.0))
            make(g.memset(omega[:, :, :], 0.0))
            assert made[0] == ALL_CONSTS
            rsqrt(dinv, deg, deg_ready, 1, dinv_ready)
            for n in range(LN_FFN, LN_MLP + 1):
                rsqrt(rstd, ve, ln_var, n + 1, ln_rstd)
            pool.wait_ge(x4_ready, NT)
            g.tensor_tensor(X[:, :, :], X[:, :, :], XN[:, :, :], ALU.add).then_inc(xx_ready, 1)


def two_chunks(pe, take, transpose, prefix, src, ident, full_of, token):
    for j in range(2):
        ps = take(f"{prefix}.{j}")
        for f in range(2):
            for t in range(NT):
                at = f * N + t * P
                last = transpose(ps[:, at:at + P], src[:, t, token(2 * j + f)], ident[:, :])
        last.then_inc(full_of(f"{prefix}.{j}"), 1)


def chunked(w):
    k, n = w.shape
    return w.reshape(k // P, P, n).transpose(1, 0, 2).reshape(P, k // P * n)


def by_column(b):
    return b.reshape(-1, P).T


def kernel(**inputs):
    import concourse.bacc as bacc
    from concourse.bass_utils import run_bass_kernel_spmd

    i = {k: np.asarray(a) for k, a in inputs.items()}
    f0, f1, g1, m0, m1 = "L0_ffn_", "L1_ffn_", "L1_gnn_", "L0_mix_", "L1_mix_"

    def heads(w):
        kv = w.shape[1] // 64
        return np.repeat(w.reshape(D, kv, 1, 64), H // kv, axis=2).reshape(D, D)

    static = {"mix_k": i[m0 + "Wk"], "mix_v": i[m0 + "Wv"], "mix_q": i[m0 + "Wq"], "mix_p": i[m0 + "Wp"],
              "gnn": i["L0_gnn_weight"], "per_k": i[m1 + "Wk"], "per_v": i[m1 + "Wv"], "per_q": i[m1 + "Wq"],
              "per_o": i[m1 + "Wo"], "cr_o": i[f1 + "cross_out_w"].T}
    for j, part in enumerate("qkv"):
        static[f"cr_{part}"] = i[f1 + "cross_in_w"][j * D:(j + 1) * D].T
    for j in range(4):
        static[f"up_{j}"] = i[f1 + "mlp_w1"][j * D:(j + 1) * D].T
        static[f"down_{j}"] = i[f1 + "mlp_w2"][:, j * D:(j + 1) * D].T
    laid = {k: chunked(w) for k, w in static.items()}
    laid["graph"] = np.concatenate([chunked(i[g1 + "Wm"]), chunked(i[g1 + "W1"]), i[g1 + "W2"]], axis=1)
    sp_in = i[f1 + "sp_in_w"].reshape(K1, 3, D, D)
    sp_b = i[f1 + "sp_in_b"].reshape(K1, 3, D)
    arrays = {
        "x": i["x"],
        "edges": np.stack([i["src"].reshape(P, EC), i["dst"].reshape(P, EC)], axis=1),
        "gate": i["edge_weight"].reshape(P, EC),
        "cols": np.concatenate(
            [by_column(i[k]) for k in (m0 + "bq", f0 + "r_b1", g1 + "gamma", g1 + "beta", f1 + "router_b1",
                                       f1 + "norm_s_w", f1 + "norm_s_b", f1 + "norm_t_w", f1 + "norm_t_b",
                                       f1 + "norm_mlp_w", f1 + "norm_mlp_b", f1 + "mlp_b1")]
            + [by_column(i[f1 + "cross_in_b"][j * D:(j + 1) * D]) for j in range(2)]
            + [i[f0 + "r_w2"], i[f1 + "router_w2"].T], axis=1),
        "rows": np.stack([i[m0 + "bk"], i[m0 + "bv"], i["L0_gnn_bias"], i[m0 + "bp"],
                          np.concatenate([i[g1 + "bm"], i[g1 + "b1"], np.zeros(D - N - HID, np.float32)]),
                          i[g1 + "b2"], i[f1 + "cross_in_b"][2 * D:], i[f1 + "cross_out_b"], i[f1 + "mlp_b2"]]),
        "router_rows": np.concatenate([i[f0 + "r_b2"], i[f1 + "router_b2"],
                                       np.zeros(16 - K0 - 2 * K1, np.float32)]).reshape(1, 16),
        "routers": np.stack([chunked(i[f0 + "r_w1"]), chunked(i[f1 + "router_w1"].T)], axis=1),
        "omegas": np.stack([i[m1 + "omega_q"], i[m1 + "omega_k"]]),
        "weights": np.stack([laid[w] for w in STATIC]),
        "ffn_w": np.stack([np.stack([chunked(i[f"{f0}wq{e}"]), chunked(heads(i[f"{f0}wk{e}"])),
                                     chunked(heads(i[f"{f0}wv{e}"])), chunked(i[f"{f0}wo{e}"])]) for e in range(K0)]),
        "sp_w": np.stack([np.stack([chunked(sp_in[e, j].T) for j in range(3)] + [chunked(i[f1 + "sp_out_w"][e].T)])
                          for e in range(K1)]),
        "tm_w": np.stack([np.stack([chunked(i[f"{f1}t{p}_w"][e].T) for p in "qkvp"]) for e in range(K1)]),
        "sp_cols": np.stack([np.concatenate([by_column(sp_b[e, 0]), by_column(sp_b[e, 1]),
                                             by_column(i[f1 + "sp_out_b"][e])], axis=1) for e in range(K1)]),
        "tm_cols": np.stack([np.concatenate([by_column(i[f"{f1}t{p}_b"][e]) for p in "qkp"], axis=1)
                             for e in range(K1)]),
        "sp_row": sp_b[:, 2],
        "tm_row": i[f1 + "tv_b"],
    }
    nc = bacc.Bacc("TRN2", target_bir_lowering=False, num_devices=1)
    feed, args = {}, {}
    for name, a in arrays.items():
        a = np.ascontiguousarray(a)
        feed[f"in_{name}"] = a
        args[name] = nc.dram_tensor(f"in_{name}", a.shape, mybir.dt.from_np(a.dtype), kind="ExternalInput").ap()
    args["out"] = nc.dram_tensor("out_0", (N, D), F32, kind="ExternalOutput").ap()
    build(nc, **args)
    result = run_bass_kernel_spmd(nc, [feed], core_ids=[0])
    return result.results[0]["out_0"]
```

```python
from contextlib import ExitStack

import numpy as np

import concourse.bass as bass
from concourse import mybir

ALU = mybir.AluOpType
ACT = mybir.ActivationFunctionType
AX = mybir.AxisListType
F32 = mybir.dt.float32
BF16 = mybir.dt.bfloat16
I32 = mybir.dt.int32
F32R = mybir.dt.float32r

P = 128
N = 256
D = 512
H = 8
NT = N // P
DC = D // P
HP = H // 2
HID = 128
E = 4096
EC = E // P
EG = 4
FC = 4 * D // P
K0, K1 = 3, 4
EPS = 1e-5
SCALE = 0.125
MASKED = -1e30

RAW = 12
SPLIT = 4
ROWS = 4

WEIGHTS = (["mix_v", "mix_k", "mix_q", "gnn", "mix_p", "ffn_v", "ffn_q", "ffn_k", "ffn_o", "graph",
            "per_k", "per_v", "per_q", "per_o", "sp_v", "sp_q", "sp_k", "tm_q", "tm_k", "tm_v",
            "sp_o", "cr_q", "tm_o", "cr_k", "cr_v", "cr_o"]
           + [f"up_{i}" for i in range(4)] + [f"down_{i}" for i in range(4)])
STATIC = [w for w in WEIGHTS if w.split("_")[0] not in ("ffn", "sp", "tm")]
PART = {"q": 0, "k": 1, "v": 2, "o": 3}
BIAS_ROWS = ["mix_v", "mix_k", "gnn", "mix_p", "graph_in", "graph_out", "sp_v", "tm_v", "cr_v", "cr_o", "down"]
ROW_BEFORE = {"mix_k": ["mix_v", "mix_k"], "mix_q": ["gnn", "mix_p"], "graph": ["graph_in", "graph_out"],
              "sp_v": ["sp_v"], "tm_v": ["tm_v"], "cr_v": ["cr_v"], "cr_o": ["cr_o"], "down_0": ["down"]}
STATIC_ROWS = [r for r in BIAS_ROWS if r not in ("sp_v", "tm_v")]

COLS, _at = {}, 0
for _name, _width in [("mix_bq", DC), ("r0_b1", 1), ("gamma", 1), ("beta", 1), ("r1_b1", 1), ("ns_w", DC), ("ns_b", DC),
                      ("nt_w", DC), ("nt_b", DC), ("nm_w", DC), ("nm_b", DC), ("up_b", FC), ("cr_bq", DC),
                      ("cr_bk", DC), ("r0_w2", K0), ("r1_w2", 2 * K1)]:
    COLS[_name] = (_at, _at + _width)
    _at += _width
NCOLS = _at


def attention_jobs(a):
    out = []
    for i in range(H + 3):
        if i < H:
            out.append(f"{a}.s{i}")
        if 0 <= i - 2 < H:
            out.append(f"{a}.t{i - 2}")
    return out


def both(*names):
    return [f"{n}.{t}" for n in names for t in range(2)]


JOBS = (both("xT0", "mix_v", "mix_k", "mix_q", "gnn") + ["mix.ks", "mix.kv", "mix.den"]
        + both("mix.num", "mix.oT") + ["cntT", "mix_p.0", "attT", "adj.0", "mix_p.1", "adj.1"]
        + both("xT1") + ["r0.pool", "r0.hid", "r0.out"] + both("ffn_v", "ffn_q", "ffn_k")
        + attention_jobs("ffn") + both("ffn.oT", "ffn_o")
        + both("xT2") + ["g.feat"] + both("per_k", "g.msg", "per_v") + ["g.hid"] + both("per_q")
        + ["g.zT"] + both("per.kf", "per.kn", "g.out", "per.qf", "per.qn")
        + ["per.ks", "per.kv", "per.den"] + both("per.num", "per.oT", "per_o")
        + ["r1.pool", "r1.hid", "r1.out"] + both("xT3", "sp_v", "sp_q", "sp_k")
        + attention_jobs("sp") + both("tm_q", "tm_k", "tm_v", "sp.oT") + attention_jobs("tm")
        + both("sp_o", "tm.oT", "cr_q", "tm_o", "cr_k", "cr_v") + attention_jobs("cr")
        + both("cr.oT", "cr_o", "xT4") + [f"up.{j}" for j in range(FC // 2)] + both("down"))
ROTATING = 6
TURN = {name: divmod(i, ROTATING) for i, name in enumerate(JOBS)}
ATTENTIONS = ["ffn", "sp", "tm", "cr"]

LAST_JOB = {w: f"{w}.1" for w in WEIGHTS} | {"graph": "g.out.1"}
LAST_JOB |= {f"up_{i}": f"up.{2 * i + 1}" for i in range(4)} | {f"down_{i}": "down.1" for i in range(4)}
ROW_DONE = {"mix_k": "mix_k.1", "mix_v": "mix_v.1", "gnn": "mix_p.1", "mix_p": "mix_p.1", "graph_in": "g.hid",
            "graph_out": "g.out.1", "sp_v": "sp_v.1", "tm_v": "tm_v.1", "cr_v": "cr_v.1", "cr_o": "cr_o.1",
            "down": "down.1"}

FIRST_CONSTS, IOTA_CONST, ALL_CONSTS = 3, 4, 16

LOW_ON_VECTOR = [4 * WEIGHTS.index(w) + c for w in ("mix_v", "ffn_v", "sp_v") for c in (1, 3)]
LOW_ON_POOL = [k for k in range(4 * len(WEIGHTS)) if k not in LOW_ON_VECTOR]
HIGH = both("xT0", "mix.oT", "xT1", "ffn.oT", "xT2", "g.msg", "per.oT", "sp.oT", "tm.oT", "cr.oT")

LN_IN0, LN_FFN, LN_IN1, LN_GRAPH, LN_X3, LN_Z, LN_MLP = range(7)


def build(nc, x, edges, gate, cols, rows, router_rows, routers, omegas, weights, ffn_w, sp_w, tm_w,
          sp_cols, tm_cols, sp_row, tm_row, out):
    with ExitStack() as ctx:
        def sb(name, shape, dt=F32):
            return ctx.enter_context(nc.sbuf_tensor(name, shape, dt))

        def sem(name):
            return ctx.enter_context(nc.semaphore(name))

        wraw = sb("wraw", [P, RAW, D])
        wh = sb("wh", [P, SPLIT, DC, D], F32R)
        wl = sb("wl", [P, SPLIT, DC, D], F32R)
        rslot = sb("rslot", [P, ROWS, D])
        X = sb("X", [P, NT, D])
        XN = sb("XN", [P, NT, D])
        ZN = sb("ZN", [P, NT, D])
        XT = [sb(f"XT{i}", [P, DC, N], F32R) for i in range(2)]
        XT2 = [sb(f"XT2{i}", [P, DC, N], F32R) for i in range(2)]
        OT = [sb(f"OT{i}", [P, DC, N], F32R) for i in range(2)]
        zT = [sb(f"zT{i}", [P, N], F32R) for i in range(2)]
        Q = sb("Q", [P, DC, N])
        K = sb("K", [P, DC, N])
        V = sb("V", [P, NT, D])
        O = sb("O", [P, NT, D])
        with ExitStack() as early:
            PR = early.enter_context(nc.sbuf_tensor("PR", [P, 4, NT * N], F32))
            PT = early.enter_context(nc.sbuf_tensor("PT", [P, 4, NT * N], F32))
            big = early.enter_context(nc.sbuf_tensor("big", [P, FC * N], F32))
        G = [sb(f"G{i}", [P, FC, N], F32R) for i in range(2)]
        big2 = sb("big2", [P, 1024])
        KV = sb("KV", [P, HP, P])
        KS = sb("KS", [P, HP, 2])
        att = sb("att", [P, NT, N])
        attT = sb("attT", [P, NT, N])
        ident = sb("ident", [P, P])
        ident16 = sb("ident16", [P, P], BF16)
        mask16 = sb("mask16", [P, P], BF16)
        ones = sb("ones", [P, 1])
        halves = sb("halves", [P, P])
        omega = sb("omega", [P, 2, P])
        router_w = sb("router_w", [P, 2, DC * HID])
        col = sb("col", [P, NCOLS])
        scol = sb("scol", [P, 3 * DC])
        tcol = sb("tcol", [P, 3 * DC])
        rrow = sb("rrow", [1, 16])
        desc = sb("desc", [1, 4])
        iota16 = sb("iota16", [P, N], BF16)
        edge_i = sb("edge_i", [P, 2, EC], I32)
        sq16 = sb("sq16", [P, 2, EG, N], BF16)
        edge_f = sb("edge_f", [P, 3, EC])
        ew = sb("ew", [P, 4, EC])
        ew16 = sb("ew16", [P, 2, EC], BF16)
        gmax = sb("gmax", [P, 4])
        bn = sb("bn", [P, NT, 6])
        mv = sb("mv", [P, NT, 2])
        ve = sb("ve", [P, NT])
        rstd = sb("rstd", [P, NT])
        half = sb("half", [P, NT])
        deg = sb("deg", [P, NT])
        dinv = sb("dinv", [P, NT])
        rowsum = sb("rowsum", [P, NT])
        rsum = sb("rsum", [P, NT])
        valid = sb("valid", [P, NT])
        nmax = sb("nmax", [P, H, NT])
        psum_ = sb("psum_", [P, H, NT])
        rprob = sb("rprob", [P, NT, H])
        den = sb("den", [P, NT, H])
        pool_c = sb("pool_c", [P, DC])
        hid_c = sb("hid_c", [P, 1])
        r = sb("r", [1, 64])
        ridx = sb("ridx", [1, 4], I32)
        hot = big[:, :].bitcast(BF16).rearrange("p (b c k n) -> p b c k n", b=2, c=EG, k=4)
        hotlo = big2[:, :].bitcast(BF16).rearrange("p (b c n) -> p b c n", b=2, c=EG)
        cnt, adj = XN[:, 0, :].rearrange("p (t n) -> p t n", t=NT), XN[:, 1, :].rearrange("p (t n) -> p t n", t=NT)
        hg = ZN
        graph_out = K[:, :, :].rearrange("p (t a) n -> p t (a n)", t=NT)
        kphi_m, qphi_m = K[:, :, :].rearrange("p (t a) n -> p t (a n)", t=NT), Q
        ksq = big[:, 0:1024].rearrange("p (c n) -> p c n", c=DC)
        qsq = big[:, 1024:2048].rearrange("p (c n) -> p c n", c=DC)
        kphi_p = big[:, 2048:3072].rearrange("p (t n) -> p t n", t=NT)
        mfeat = big[:, 3072:3584].rearrange("p (t n) -> p t n", t=NT)
        hgr = big[:, 3584:3840].rearrange("p (t f) -> p t f", t=NT)
        zTf = big[:, 3840:4096]
        qphi_p = ZN[:, :, :].rearrange("p t (a n) -> p (t a) n", n=N)
        msg = XT2
        SP, TM = XT, XT2
        xsf = K
        xtf = ZN[:, :, :].rearrange("p t (a n) -> p (t a) n", n=N)
        tmf = PT[:, 0:2, :].rearrange("p a (b n) -> p (a b) n", n=N)
        gf = [Q[:, 0:2, :], Q[:, 2:4, :], K[:, 0:2, :], K[:, 2:4, :]]

        banks = [ctx.enter_context(nc.psum_tensor(f"bank{i}", [P, 512], F32)) for i in range(8)]
        acc = banks[6:8]

        raw_loaded = [sem(f"raw_loaded{i}") for i in range(RAW)]
        high_done = sem("high_done")
        low_done = [sem("low_by_pool"), sem("low_by_vector")]
        high_taken = sem("high_taken")
        full_form = sem("full_form")
        split_high = sem("split_high")
        split_low = sem("split_low")
        row_loaded = [sem(f"row_loaded{i}") for i in range(ROWS)]
        full = [sem(f"bank_full{i}") for i in range(ROTATING)]
        read = [sem(f"bank_read{i}") for i in range(ROTATING)]
        acc_full, acc_read = sem("acc_full"), sem("acc_read")
        x_loaded = [sem(f"x_loaded{t}") for t in range(NT)]
        edges_loaded, params_loaded = sem("edges_loaded"), sem("params_loaded")
        scol_loaded, tcol_loaded = sem("scol_loaded"), sem("tcol_loaded")
        consts = sem("consts")
        gate_max, gate_all, gate_neg, gate_exp = sem("gate_max"), sem("gate_all"), sem("gate_neg"), sem("gate_exp")
        hots_src, hots_dst, hots_weighted = sem("hots_src"), sem("hots_dst"), sem("hots_weighted")
        hots_used, dst_ready, sq_ready, row_sum = sem("hots_used"), sem("dst_ready"), sem("sq_ready"), sem("row_sum")
        ln_var, ln_rstd, ln_out = sem("ln_var"), sem("ln_rstd"), sem("ln_out")
        deg_ready, dinv_ready = sem("deg_ready"), sem("dinv_ready")
        adj_ready, att_ready = sem("adj_ready"), sem("att_ready")
        phi_in, phi_exp, phi_ready = sem("phi_in"), sem("phi_exp"), sem("phi_ready")
        score_max = sem("score_max")
        logit_max, logit_exp, route_ready = sem("logit_max"), sem("logit_exp"), sem("route_ready")
        out_ready, out_stored = sem("out_ready"), sem("out_stored")
        dve_step = sem("dve_step")

        def bank(job):
            return banks[TURN[job][1]]

        def filled(eng, job):
            eng.wait_ge(full[TURN[job][1]], TURN[job][0] + 1)

        def stored(eng, job):
            eng.wait_ge(read[TURN[job][1]], TURN[job][0] + 1)

        def full_of(job):
            return full[TURN[job][1]]

        def read_of(job):
            return read[TURN[job][1]]

        def quarter(w, c):
            return 4 * WEIGHTS.index(w) + c

        def low_ready(eng, k):
            if k in LOW_ON_VECTOR:
                eng.wait_ge(low_done[1], LOW_ON_VECTOR.index(k) + 1)
            else:
                eng.wait_ge(low_done[0], LOW_ON_POOL.index(k) + 1)

        def parts(k):
            i, c = divmod(k, 4)
            return wh[:, i % SPLIT, c, :], wl[:, i % SPLIT, c, :]

        def high_out(eng, job):
            eng.wait_ge(high_taken, HIGH.index(job) + 1)

        def row(name):
            return rslot[:, BIAS_ROWS.index(name) % ROWS, :]

        def column(name, i=0):
            return col[:, COLS[name][0] + i:COLS[name][0] + i + 1]

        def token(t):
            return slice(t * P, (t + 1) * P)

        block = ctx.enter_context(nc.Block())

        @block.sync
        def _(sp):
            sp.dma_start(edge_i[:, :, :], edges).then_inc(edges_loaded, 16)
            sp.dma_start(ew[:, 0, :], gate).then_inc(edges_loaded, 16)
            for t in range(NT):
                sp.dma_start(X[:, t, :], x[t * P:(t + 1) * P, :]).then_inc(x_loaded[t], 16)

            index = {}

            def load_row(name):
                i = BIAS_ROWS.index(name)
                if i >= ROWS:
                    stored(sp, ROW_DONE[BIAS_ROWS[i - ROWS]])
                if name == "sp_v":
                    src = sp_row[bass.ds(index["sp"], 1), :]
                elif name == "tm_v":
                    src = tm_row[bass.ds(index["tm"], 1), :]
                else:
                    j = STATIC_ROWS.index(name)
                    src = rows[j:j + 1, :]
                sp.dma_start(row(name), src.partition_broadcast(P)).then_inc(row_loaded[i % ROWS], 16)

            def load_weight(w):
                family, part = (w.split("_") + [""])[:2]
                for c in range(DC):
                    k = quarter(w, c)
                    if k >= RAW:
                        sp.wait_ge(high_done, k - RAW + 1)
                        low_ready(sp, k - RAW)
                    if family in ("ffn", "sp", "tm"):
                        table = {"ffn": ffn_w, "sp": sp_w, "tm": tm_w}[family]
                        src = table[bass.ds(index[family], 1), PART[part], :, c * D:(c + 1) * D]\
                            .rearrange("a p n -> p (a n)")
                    else:
                        src = weights[STATIC.index(w), :, c * D:(c + 1) * D]
                    sp.dma_start(wraw[:, k % RAW, :], src).then_inc(raw_loaded[k % RAW], 16)

            for w in WEIGHTS:
                if w == "ffn_v":
                    sp.wait_ge(route_ready, 1)
                    index["ffn"] = nc.sync.value_load(ridx[0:1, 0:1], min_val=0, max_val=K0 - 1)
                if w == "sp_v":
                    sp.wait_ge(route_ready, 2)
                    index["sp"] = nc.sync.value_load(ridx[0:1, 2:3], min_val=0, max_val=K1 - 1)
                    index["tm"] = nc.sync.value_load(ridx[0:1, 3:4], min_val=0, max_val=K1 - 1)
                for name in ROW_BEFORE.get(w, []):
                    load_row(name)
                load_weight(w)
                if w == "sp_q":
                    sp.dma_start(scol[:, :], sp_cols[bass.ds(index["sp"], 1), :, :].rearrange("a p n -> p (a n)"))\
                      .then_inc(scol_loaded, 16)
                    sp.dma_start(tcol[:, :], tm_cols[bass.ds(index["tm"], 1), :, :].rearrange("a p n -> p (a n)"))\
                      .then_inc(tcol_loaded, 16)
                if w == "mix_v":
                    sp.dma_start(col[:, :], cols).then_inc(params_loaded, 16)
                if w == "mix_p":
                    sp.dma_start(router_w[:, :, :], routers).then_inc(params_loaded, 16)
                    sp.dma_start(rrow[:, :], router_rows).then_inc(params_loaded, 16)
                    sp.wait_ge(consts, ALL_CONSTS)
                    for i in range(2):
                        for b in range(2):
                            sp.dma_start(omega[64 * b:64 * b + 64, i, 64 * b:64 * b + 64], omegas[i, :, :])\
                              .then_inc(params_loaded, 16)
            for t in range(NT):
                sp.wait_ge(out_ready, t + 1)
                sp.dma_start(out[t * P:(t + 1) * P, :], ZN[:, t, :]).then_inc(out_stored, 16)
            sp.wait_ge(out_stored, 16 * NT)

        @block.tensor
        def _(pe):
            mm, transpose = nc.tensor.matmul, nc.tensor.transpose

            def take(job):
                turn, b = TURN[job]
                if turn:
                    pe.wait_ge(read[b], turn)
                return banks[b]

            def weight(w):
                for c in range(DC):
                    low_ready(pe, quarter(w, c))
                i = WEIGHTS.index(w)
                return wh[:, i % SPLIT, :, :], wl[:, i % SPLIT, :, :]

            def three(out, lhs, rhs, first, last):
                mm(out, lhs[0], rhs[0], start=first, stop=False)
                mm(out, lhs[0], rhs[1], start=False, stop=False)
                return mm(out, lhs[1], rhs[0], start=False, stop=last)

            def of(pair, *index):
                return [part[index] for part in pair]

            def to_features(prefix, src, n):
                for t in range(NT):
                    pe.wait_ge(ln_out, 2 * n + t + 1)
                    ps = take(f"{prefix}.{t}")
                    for c in range(DC):
                        last = transpose(ps[:, token(c)], src[:, t, token(c)], ident[:, :])
                    last.then_inc(full_of(f"{prefix}.{t}"), 1)

            def per_token(w, src, t):
                ws, ps = weight(w), take(f"{w}.{t}")
                for c in range(DC):
                    last = three(ps[:, :], of(src, slice(None), c, token(t)), of(ws, slice(None), c), c == 0, c == DC - 1)
                last.then_inc(full_of(f"{w}.{t}"), 1)

            def both_tiles(w, src):
                pss = [take(f"{w}.{t}") for t in range(NT)]
                for c in range(DC):
                    k = quarter(w, c)
                    low_ready(pe, k)
                    for t in range(NT):
                        last = three(pss[t][:, :], of(src, slice(None), c, token(t)), parts(k), c == 0, c == DC - 1)
                        if c == DC - 1:
                            last.then_inc(full_of(f"{w}.{t}"), 1)

            def per_feature(w, src, j, job=None):
                ws, ps = weight(w), take(job or f"{w}.{j % 2}")
                for f in range(2):
                    for c in range(DC):
                        last = three(ps[:, f * N:(f + 1) * N], of(ws, slice(None), c, token(2 * (j % 2) + f)),
                                     of(src, slice(None), c), c == 0, c == DC - 1)
                last.then_inc(full_of(job or f"{w}.{j % 2}"), 1)

            def two_chunks(prefix, src, n):
                pss = [take(f"{prefix}.{j}") for j in range(2)]
                for t in range(NT):
                    pe.wait_ge(ln_out, 2 * n + t + 1)
                    for j in range(2):
                        for f in range(2):
                            at = f * N + t * P
                            last = transpose(pss[j][:, at:at + P], src[:, t, token(2 * j + f)], ident[:, :])
                        if t == NT - 1:
                            last.then_inc(full_of(f"{prefix}.{j}"), 1)

            def graph_w(at, n):
                i = WEIGHTS.index("graph") % SPLIT
                return [part[:, i, at // D, at % D:at % D + n] for part in (wh, wl)]

            def edge_group(g):
                pe.wait_ge(hots_src, EG * (g + 1))
                pe.wait_ge(hots_dst, g + 1)
                pe.wait_ge(hots_weighted, g + 1)
                for c in range(EG):
                    h = hot[:, g % 2, c, :, :]
                    for t in range(NT):
                        src = h[:, 0, token(t)]
                        mm(acc[t][:, :], src, h[:, 1:3, :], start=g == c == 0, stop=False, skip_group_check=True)
                        mm(acc[t][:, N:], src, h[:, 3, :], start=False, stop=False, skip_group_check=True)
                        last = mm(acc[t][:, N:], src, hotlo[:, g % 2, c, :], start=False,
                                  stop=g == EC // EG - 1 and c == EG - 1, skip_group_check=True)
                last.then_inc(hots_used, 1)

            def linear_sums(name, kphi, v, first):
                pe.wait_ge(phi_ready, first + 2)
                ps = take(f"{name}.ks")
                for p in range(HP):
                    for t in range(NT):
                        last = mm(ps[:, p:p + 1], kphi[:, t, token(p)], ones[:, :], start=t == 0, stop=t == NT - 1)
                last.then_inc(full_of(f"{name}.ks"), 1)
                ps = take(f"{name}.kv")
                for p in range(HP):
                    for t in range(NT):
                        last = mm(ps[:, token(p)], kphi[:, t, token(p)], v[:, t, token(p)], start=t == 0,
                                  stop=t == NT - 1)
                last.then_inc(full_of(f"{name}.kv"), 1)

            def linear_products(name, qphi, first):
                pe.wait_ge(phi_ready, first + 4)
                stored(pe, f"{name}.ks")
                ps = take(f"{name}.den")
                for t in range(NT):
                    for p in range(HP):
                        at = t * H + 2 * p
                        last = mm(ps[:, at:at + 2], qphi[:, p, token(t)], KS[:, p, :], start=True, stop=True)
                last.then_inc(full_of(f"{name}.den"), 1)
                stored(pe, f"{name}.kv")
                for t in range(NT):
                    ps = take(f"{name}.num.{t}")
                    for p in range(HP):
                        last = mm(ps[:, token(p)], qphi[:, p, token(t)], KV[:, p, :], start=True, stop=True)
                    last.then_inc(full_of(f"{name}.num.{t}"), 1)

            def heads_to_features(name):
                for t in range(NT):
                    if name in ATTENTIONS:
                        pe.wait_ge(acc_read, 1 + 2 * ATTENTIONS.index(name) + t + 1)
                    else:
                        stored(pe, f"{name}.num.{t}")
                    ps = take(f"{name}.oT.{t}")
                    for c in range(DC):
                        last = transpose(ps[:, token(c)], O[:, t, token(c)], ident[:, :])
                    last.then_inc(full_of(f"{name}.oT.{t}"), 1)

            def router(n):
                ps = take(f"r{n}.pool")
                for c in range(DC):
                    for t in range(NT):
                        last = mm(ps[:, c:c + 1], XN[:, t, token(c)], ones[:, :], start=t == 0, stop=t == NT - 1)
                last.then_inc(full_of(f"r{n}.pool"), 1)

            def router_hidden(n):
                pe.wait_ge(params_loaded, 16 * 7)
                stored(pe, f"r{n}.pool")
                ps = take(f"r{n}.hid")
                for c in range(DC):
                    last = mm(ps[:, 0:1], router_w[:, n, token(c)], pool_c[:, c:c + 1], start=c == 0, stop=c == DC - 1)
                last.then_inc(full_of(f"r{n}.hid"), 1)
                stored(pe, f"r{n}.hid")
                ps = take(f"r{n}.out")
                a, b = COLS[f"r{n}_w2"]
                mm(ps[0:1, 0:b - a], hid_c[:, :], col[:, a:b], start=True, stop=True)\
                    .then_inc(full_of(f"r{n}.out"), 1)

            def attention(name):
                a, causal = ATTENTIONS.index(name), name == "tm"

                def scores(h):
                    ps = take(f"{name}.s{h}")
                    lo = 64 * (h % 2)
                    q, k = Q[lo:lo + 64, h // 2, :], K[lo:lo + 64, h // 2, :]
                    for t in range(NT):
                        keys = (t + 1) * P if causal else N
                        last = mm(ps[:, t * N:t * N + keys], q[:, token(t)], k[:, 0:keys], start=True, stop=True)
                        if causal:
                            last = mm(ps[:, t * N + keys - P:t * N + keys], ident16[:, :], mask16[:, :], start=False,
                                      stop=True, skip_group_check=True)
                    last.then_inc(full_of(f"{name}.s{h}"), 1)

                def turn_probs(h):
                    stored(pe, f"{name}.s{h}")
                    ps = take(f"{name}.t{h}")
                    for i, (k, q) in enumerate([(0, 0), (0, 1), (1, 1)] + [(1, 0)] * (not causal)):
                        last = transpose(ps[:, token(i)], PR[:, h % 4, q * N + k * P:q * N + (k + 1) * P], ident[:, :])
                    last.then_inc(full_of(f"{name}.t{h}"), 1)

                def values(h):
                    stored(pe, f"{name}.t{h}")
                    if h == 0:
                        pe.wait_ge(acc_read, 1 + NT * a)
                    pt = PT[:, h % 4, :]
                    for t in range(NT):
                        o = acc[t][:, 64 * h:64 * h + 64]
                        first = pt[:, token(t)]
                        last = mm(o, first, V[:, 0, 64 * h:64 * h + 64], start=True, stop=causal and t == 0)
                        if not (causal and t == 0):
                            last = mm(o, pt[:, token(3 - t)], V[:, 1, 64 * h:64 * h + 64], start=False, stop=True)
                    return last

                for i in range(H + 3):
                    if i < H:
                        scores(i)
                    if 0 <= i - 2 < H:
                        turn_probs(i - 2)
                    if 0 <= i - 3:
                        last = values(i - 3)
                last.then_inc(acc_full, 1)

            pe.wait_ge(consts, FIRST_CONSTS)
            to_features("xT0", XN, LN_IN0)
            for t in range(NT):
                stored(pe, f"xT0.{t}")
            both_tiles("mix_v", XT)
            edge_group(0)
            for t in range(NT):
                per_token("mix_k", XT, t)
            edge_group(1)
            for j in range(2):
                per_feature("mix_q", XT, j)
            edge_group(2)
            for t in range(NT):
                per_token("gnn", XT, t)
            edge_group(3)
            pe.wait_ge(consts, ALL_CONSTS)
            for t in range(NT):
                stored(pe, f"mix_v.{t}")
            linear_sums("mix", kphi_m, V, 0)
            edge_group(4)
            linear_products("mix", qphi_m, 0)
            edge_group(5)
            edge_group(6)
            heads_to_features("mix")
            edge_group(7)
            def turn_table(job, table):
                ps = take(job)
                for t in range(NT):
                    for u in range(NT):
                        last = transpose(ps[:, u * N + t * P:u * N + (t + 1) * P], table[:, t, token(u)], ident[:, :])
                last.then_inc(full_of(job), 1)

            pe.wait_ge(acc_read, 1)
            turn_table("cntT", cnt)
            for t in range(NT):
                stored(pe, f"mix.oT.{t}")
            for t in range(NT):
                per_token("mix_p", OT, t)
                if t == 0:
                    pe.wait_ge(att_ready, 1)
                    turn_table("attT", att)
                    pe.wait_ge(adj_ready, 1)
                for u in range(NT):
                    stored(pe, f"gnn.{u}")
                ps = take(f"adj.{t}")
                for u in range(NT):
                    last = mm(ps[:, :], adj[:, u, token(t)], hg[:, u, :], start=u == 0, stop=u == NT - 1)
                last.then_inc(full_of(f"adj.{t}"), 1)

            to_features("xT1", XN, LN_FFN)
            router(0)
            router_hidden(0)
            for t in range(NT):
                stored(pe, f"xT1.{t}")
            both_tiles("ffn_v", XT)
            for w in ("ffn_q", "ffn_k"):
                for j in range(2):
                    per_feature(w, XT, j)
            for w in ("ffn_q", "ffn_k", "ffn_v"):
                for j in range(2):
                    stored(pe, f"{w}.{j}")
            attention("ffn")
            heads_to_features("ffn")
            for t in range(NT):
                stored(pe, f"ffn.oT.{t}")
            for t in range(NT):
                per_token("ffn_o", OT, t)

            to_features("xT2", XN, LN_IN1)
            for t in range(NT):
                stored(pe, f"xT2.{t}")
            weight("graph")
            ps = take("g.feat")
            for t in range(NT):
                for c in range(DC):
                    last = three(ps[:, t * N:(t + 1) * N], of(XT, slice(None), c, token(t)),
                                 graph_w(c * N, N), c == 0, c == DC - 1)
            last.then_inc(full_of("g.feat"), 1)
            for j in range(2):
                per_feature("per_k", XT, j)
            stored(pe, "g.feat")
            stored(pe, "attT")
            for i, table in enumerate((attT, att)):
                ps = take(f"g.msg.{i}")
                for f in range(2):
                    for u in range(NT):
                        last = mm(ps[:, f * N:(f + 1) * N], mfeat[:, u, token(f)], table[:, u, :], start=u == 0,
                                  stop=u == NT - 1)
                last.then_inc(full_of(f"g.msg.{i}"), 1)
            for t in range(NT):
                per_token("per_v", XT, t)
            for i in range(2):
                stored(pe, f"g.msg.{i}")
            ps = take("g.hid")
            for t in range(NT):
                for c in range(DC):
                    last = three(ps[:, token(t)], of(msg, slice(None), c, token(t)), graph_w(DC * N + c * HID, HID),
                                 c == 0, c == DC - 1)
            last.then_inc(full_of("g.hid"), 1)
            for j in range(2):
                per_feature("per_q", XT, j)
            pe.wait_ge(ln_out, 2 * LN_GRAPH + 2)
            ps = take("g.zT")
            for t in range(NT):
                last = transpose(ps[:, token(t)], hgr[:, t, :], ident[:, :])
            last.then_inc(full_of("g.zT"), 1)
            for j in range(2):
                stored(pe, f"per_k.{j}")
            for job, lhs in (("kf", K), ("kn", ksq)):
                for t in range(NT):
                    ps = take(f"per.{job}.{t}")
                    for p in range(HP):
                        last = mm(ps[:, token(p)], lhs[:, p, token(t)], omega[:, 1, :] if job == "kf" else halves[:, :],
                                  start=True, stop=True)
                    last.then_inc(full_of(f"per.{job}.{t}"), 1)
            pe.wait_ge(split_low, 1)
            for t in range(NT):
                ps = take(f"g.out.{t}")
                three(ps[:, :], of(zT, slice(None), token(t)), graph_w(DC * (N + HID), D), True, True)\
                    .then_inc(full_of(f"g.out.{t}"), 1)
            for j in range(2):
                stored(pe, f"per_q.{j}")
            for job, rhs in (("qf", Q), ("qn", qsq)):
                for j in range(2):
                    ps = take(f"per.{job}.{j}")
                    for f in range(2):
                        last = mm(ps[:, f * N:(f + 1) * N], omega[:, 0, :] if job == "qf" else halves[:, :],
                                  rhs[:, 2 * j + f, :], start=True, stop=True)
                    last.then_inc(full_of(f"per.{job}.{j}"), 1)
            for t in range(NT):
                stored(pe, f"per_v.{t}")
            linear_sums("per", kphi_p, V, 4)
            linear_products("per", qphi_p, 4)
            heads_to_features("per")
            for t in range(NT):
                stored(pe, f"per.oT.{t}")
            for t in range(NT):
                per_token("per_o", OT, t)

            pe.wait_ge(ln_out, 2 * LN_X3 + 2)
            router(1)
            router_hidden(1)
            two_chunks("xT3", ZN, LN_Z)
            pe.wait_ge(split_low, 3)
            both_tiles("sp_v", XT)
            for w in ("sp_q", "sp_k"):
                for j in range(2):
                    per_feature(w, XT, j)
            for w in ("sp_q", "sp_k", "sp_v"):
                for j in range(2):
                    stored(pe, f"{w}.{j}")
            attention("sp")
            pe.wait_ge(split_low, 5)
            for w in ("tm_q", "tm_k"):
                for j in range(2):
                    per_feature(w, XT2, j)
            for t in range(NT):
                per_token("tm_v", XT2, t)
            heads_to_features("sp")
            for w in ("tm_q", "tm_k", "tm_v"):
                for j in range(2):
                    stored(pe, f"{w}.{j}")
            attention("tm")
            for t in range(NT):
                stored(pe, f"sp.oT.{t}")
            for j in range(2):
                per_feature("sp_o", OT, j)
            heads_to_features("tm")
            for j in range(2):
                stored(pe, f"sp_o.{j}")
            for j in range(2):
                per_feature("cr_q", SP, j)
            for t in range(NT):
                stored(pe, f"tm.oT.{t}")
            for j in range(2):
                per_feature("tm_o", OT, j)
            pe.wait_ge(split_low, 7)
            for j in range(2):
                per_feature("cr_k", TM, j)
            for t in range(NT):
                per_token("cr_v", TM, t)
            for w in ("cr_q", "cr_k", "cr_v"):
                for j in range(2):
                    stored(pe, f"{w}.{j}")
            attention("cr")
            heads_to_features("cr")
            for t in range(NT):
                stored(pe, f"cr.oT.{t}")
            for t in range(NT):
                per_token("cr_o", OT, t)

            two_chunks("xT4", ZN, LN_MLP)
            for j in range(2):
                stored(pe, f"xT4.{j}")
            for j in range(FC // 2):
                per_feature(f"up_{j // 2}", XT, j, f"up.{j}")
            for t in range(NT):
                ps = take(f"down.{t}")
                for c in range(FC):
                    if t == 0:
                        low_ready(pe, quarter("down_0", c))
                    if t == 0 and c % 2 == 0:
                        pe.wait_ge(split_low, 7 + c // 2 + 1)
                    last = three(ps[:, :], of(G, slice(None), c, token(t)), parts(quarter("down_0", c)), c == 0,
                                 c == FC - 1)
                last.then_inc(full_of(f"down.{t}"), 1)

        @block.vector
        def _(dve):
            v = nc.vector
            steps = [0]

            def link(ins):
                steps[0] += 1
                ins.then_inc(dve_step, 1)
                dve.wait_ge(dve_step, steps[0])

            def row_there(name):
                i = BIAS_ROWS.index(name)
                dve.wait_ge(row_loaded[i % ROWS], 16 * (i // ROWS + 1))
                return row(name)

            def ln_stats(n, t, src, width=D):
                link(v.bn_stats(bn[:, t, :], src[:, t, 0:width]))
                link(v.bn_aggr(mv[:, t, :], bn[:, t, :]))
                v.tensor_scalar(ve[:, t:t + 1], mv[:, t, 1:2], EPS, None, ALU.add).then_inc(ln_var, 1)

            def ln_apply(n, t, src, dst, width=D):
                dve.wait_ge(ln_rstd, 2 * n + t + 1)
                v.tensor_scalar(dst[:, t, 0:width], src[:, t, 0:width], mv[:, t, 0:1], rstd[:, t:t + 1],
                                ALU.subtract, ALU.mult).then_inc(ln_out, 1)

            def weighted_hots(g):
                if g >= 2:
                    dve.wait_ge(hots_used, g - 1)
                for c in range(EG):
                    e = g * EG + c
                    h = hot[:, g % 2, c, :, :]
                    for i, o in enumerate((h[:, 2, :], h[:, 3, :], hotlo[:, g % 2, c, :])):
                        last = v.tensor_scalar(o, iota16[:, :], edge_f[:, 1, e:e + 1], ew[:, 1 + i, e:e + 1],
                                               ALU.is_equal, ALU.mult)
                last.then_inc(hots_weighted, 1)

            def weight_low(w):
                for c in range(DC):
                    k = quarter(w, c)
                    if k in LOW_ON_VECTOR:
                        dve.wait_ge(high_done, k + 1)
                        hi, lo = parts(k)
                        v.tensor_tensor(lo, wraw[:, k % RAW, :], hi.bitcast(F32), ALU.subtract).then_inc(low_done[1], 1)

            def turned_low(prefix, pair, t):
                job = f"{prefix}.{t}"
                high_out(dve, job)
                v.tensor_tensor(pair[1][:, :, token(t)], bank(job)[:, :].rearrange("p (c n) -> p c n", c=DC),
                                pair[0][:, :, token(t)].bitcast(F32), ALU.subtract).then_inc(read_of(job), 1)

            def chunks(ap, j):
                return ap[:, 2 * j:2 * j + 2, :]

            def by_chunk(job):
                return bank(job)[:, :].rearrange("p (c n) -> p c n", c=2)

            def add_row(job, dst, name):
                filled(dve, job)
                v.tensor_tensor(dst, bank(job)[:, :], row_there(name), ALU.add).then_inc(read_of(job), 1)

            def elu_in(u, job):
                stored(dve, job)
                v.tensor_scalar(PT[:, u, :], PR[:, u, :], 0.0, None, ALU.min).then_inc(phi_in, 1)

            def elu_out(u, dst):
                dve.wait_ge(phi_exp, u + 1)
                v.scalar_tensor_tensor(dst, PR[:, u, :], 0.0, PT[:, u, :], ALU.max, ALU.add).then_inc(phi_ready, 1)

            def diagonals(name):
                filled(dve, f"{name}.ks")
                for b in range(2):
                    s = slice(64 * b, 64 * b + 64)
                    last = v.tensor_copy(KS[s, :, b], bank(f"{name}.ks")[s, 0:HP])
                last.then_inc(read_of(f"{name}.ks"), 1)
                filled(dve, f"{name}.kv")
                for b in range(2):
                    s = slice(64 * b, 64 * b + 64)
                    last = v.tensor_copy(KV[s, :, s], bank(f"{name}.kv")[:, :].rearrange("p (h n) -> p h n", h=HP)[s, :, s])
                last.then_inc(read_of(f"{name}.kv"), 1)

            def by_head(ap):
                return ap.rearrange("p (h d) -> p h d", h=H)

            def linear_out(name):
                filled(dve, f"{name}.den")
                v.reciprocal(den[:, :, :].rearrange("p t h -> p (t h)"), bank(f"{name}.den")[:, 0:NT * H])\
                    .then_inc(read_of(f"{name}.den"), 1)
                stored(dve, f"{name}.den")
                for t in range(NT):
                    job = f"{name}.num.{t}"
                    filled(dve, job)
                    v.tensor_tensor(by_head(O[:, t, :]), by_head(bank(job)[:, :]),
                                    den[:, t, :].unsqueeze(2).broadcast_to([P, H, 64]), ALU.mult)\
                        .then_inc(read_of(job), 1)

            def pooled(n):
                filled(dve, f"r{n}.pool")
                v.tensor_scalar(pool_c[:, :], bank(f"r{n}.pool")[:, 0:DC], 1.0 / N, None, ALU.mult)\
                    .then_inc(read_of(f"r{n}.pool"), 1)

            def route(n, k, groups):
                w = k * groups
                a, b = (0, K0) if n == 0 else (K0, K0 + 2 * K1)
                lg, pr, hit, at = r[:, 0:w], r[:, 8:8 + w], r[:, 16:16 + w], r[:, 24:24 + groups]
                grouped = lambda ap: ap.rearrange("p (g k) -> p g k", g=groups)
                filled(dve, f"r{n}.out")
                v.tensor_tensor(lg, bank(f"r{n}.out")[0:1, 0:w], rrow[:, a:b], ALU.add).then_inc(read_of(f"r{n}.out"), 1)
                stored(dve, f"r{n}.out")
                v.tensor_reduce(r[:, 32:33], lg, AX.X, ALU.max, negate=True).then_inc(logit_max, 1)
                dve.wait_ge(logit_exp, n + 1)
                link(v.reciprocal(r[:, 33:34], r[:, 34:35]))
                link(v.tensor_scalar(lg, pr, r[:, 33:34], None, ALU.mult))
                link(v.tensor_reduce(r[:, 26:26 + groups], grouped(lg), AX.X, ALU.max))
                link(v.tensor_tensor(grouped(hit), grouped(lg), r[:, 26:26 + groups].unsqueeze(2)
                                     .broadcast_to([1, groups, k]), ALU.is_ge))
                link(v.tensor_tensor(grouped(hit), grouped(hit), desc[:, 4 - k:4].unsqueeze(1)
                                     .broadcast_to([1, groups, k]), ALU.mult))
                link(v.tensor_reduce(at, grouped(hit), AX.X, ALU.max))
                link(v.tensor_scalar(at, at, -1.0, float(k), ALU.mult, ALU.add))
                v.tensor_scalar(ridx[:, 2 * n:2 * n + groups], at, float(k - 1), None, ALU.min).then_inc(route_ready, 1)

            def attention(name):
                a, causal = ATTENTIONS.index(name), name == "tm"
                for i in range(H + 2):
                    if i < H:
                        filled(dve, f"{name}.s{i}")
                        ps = bank(f"{name}.s{i}")
                        if causal:
                            v.tensor_reduce(nmax[:, i, 0:1], ps[:, 0:P], AX.X, ALU.max, negate=True)
                            v.tensor_reduce(nmax[:, i, 1:2], ps[:, N:2 * N], AX.X, ALU.max, negate=True)\
                                .then_inc(score_max, 1)
                        else:
                            v.tensor_reduce(nmax[:, i, :], ps[:, :].rearrange("p (t n) -> p t n", t=NT), AX.X, ALU.max,
                                            negate=True).then_inc(score_max, 1)
                    if i >= 2:
                        h, w = i - 2, 3 * P if causal else 4 * P
                        filled(dve, f"{name}.t{h}")
                        v.tensor_copy(PT[:, h % 4, 0:w], bank(f"{name}.t{h}")[:, 0:w]).then_inc(read_of(f"{name}.t{h}"), 1)
                stored(dve, f"{name}.s{H - 1}")
                link(v.reciprocal(rprob[:, :, :].rearrange("p t h -> p h t"), psum_[:, :, :]))
                dve.wait_ge(acc_full, a + 1)
                for t in range(NT):
                    v.tensor_tensor(by_head(O[:, t, :]), by_head(acc[t][:, :]),
                                    rprob[:, t, :].unsqueeze(2).broadcast_to([P, H, 64]), ALU.mult).then_inc(acc_read, 1)

            def add_to_x(job):
                t = int(job[-1])
                filled(dve, job)
                v.tensor_tensor(X[:, t, :], bank(job)[:, :], X[:, t, :], ALU.add).then_inc(read_of(job), 1)
                stored(dve, job)

            def scaled_query(job, j, bias):
                filled(dve, job)
                for f in range(2):
                    last = v.tensor_scalar(Q[:, 2 * j + f, :], bank(job)[:, f * N:(f + 1) * N], bias(2 * j + f), SCALE,
                                           ALU.add, ALU.mult)
                last.then_inc(read_of(job), 1)

            def scale_shift(job, dst, j, w, b):
                filled(dve, job)
                for f in range(2):
                    c = 2 * j + f
                    last = v.tensor_scalar(dst[:, c, :], bank(job)[:, f * N:(f + 1) * N], column(w, c), column(b, c),
                                           ALU.mult, ALU.add)
                return last

            def low_of(pair, whole, j, high):
                dve.wait_ge(split_high, high)
                return v.tensor_tensor(chunks(pair[1], j), whole, chunks(pair[0], j).bitcast(F32), ALU.subtract)

            dve.wait_ge(edges_loaded, 32)
            v.tensor_reduce(gmax[:, 0:1], ew[:, 0, :], AX.X, ALU.max).then_inc(gate_max, 1)
            v.tensor_copy(edge_f[:, 0:2, :], edge_i[:, :, :])
            v.tensor_scalar(edge_f[:, 2, :], edge_i[:, 1, :], -1.0, None, ALU.mult).then_inc(dst_ready, 1)
            dve.wait_ge(dst_ready, 1)
            for t in range(NT):
                dve.wait_ge(x_loaded[t], 16)
                ln_stats(LN_IN0, t, X)
            dve.wait_ge(gate_all, 1)
            v.tensor_scalar(gmax[:, 2:3], gmax[:, 1:2], 0.0, -1.0, ALU.max, ALU.mult).then_inc(gate_neg, 1)
            for t in range(NT):
                ln_apply(LN_IN0, t, X, XN)
            dve.wait_ge(gate_exp, 1)
            link(v.tensor_copy(ew16[:, 0, :], ew[:, 1, :]))
            link(v.tensor_tensor(ew[:, 2, :], ew[:, 1, :], ew16[:, 0, :], ALU.subtract))
            link(v.tensor_copy(ew16[:, 1, :], ew[:, 2, :]))
            link(v.tensor_tensor(ew[:, 3, :], ew[:, 2, :], ew16[:, 1, :], ALU.subtract))
            for t in range(NT):
                turned_low("xT0", XT, t)
            weight_low("mix_v")

            dve.wait_ge(consts, IOTA_CONST)
            weighted_hots(0)
            for t in range(NT):
                add_row(f"mix_v.{t}", V[:, t, :], "mix_v")
            weighted_hots(1)
            for t in range(NT):
                job = f"mix_k.{t}"
                filled(dve, job)
                v.tensor_tensor(PR[:, t, :], bank(job)[:, :], row_there("mix_k"), ALU.add).then_inc(read_of(job), 1)
                elu_in(t, job)
            weighted_hots(2)
            for t in range(NT):
                elu_out(t, kphi_m[:, t, :])
            for j in range(2):
                job = f"mix_q.{j}"
                filled(dve, job)
                for f in range(2):
                    last = v.tensor_scalar(PR[:, 2 + j, f * N:(f + 1) * N], bank(job)[:, f * N:(f + 1) * N],
                                           column("mix_bq", 2 * j + f), None, ALU.add)
                last.then_inc(read_of(job), 1)
                elu_in(2 + j, job)
            weighted_hots(3)
            for j in range(2):
                elu_out(2 + j, qphi_m[:, 2 * j:2 * j + 2, :].rearrange("p c n -> p (c n)"))
            weighted_hots(4)
            dve.wait_ge(consts, ALL_CONSTS)
            diagonals("mix")
            weighted_hots(5)
            linear_out("mix")
            weighted_hots(6)
            weighted_hots(7)
            for t in range(NT):
                turned_low("mix.oT", OT, t)
            for name in ("gnn", "mix_p"):
                for t in range(NT):
                    last = v.tensor_tensor(X[:, t, :], X[:, t, :], row_there(name), ALU.add)
                link(last)

            dve.wait_ge(hots_used, EC // EG)
            for t in range(NT):
                last = v.tensor_scalar(cnt[:, t, :], acc[t][:, 0:N], 1.0, None, ALU.min)
            last.then_inc(acc_read, 1)
            dve.wait_ge(acc_read, 1)
            filled(dve, "cntT")
            for t in range(NT):
                last = v.tensor_tensor(adj[:, t, :], bank("cntT")[:, t * N:(t + 1) * N], cnt[:, t, :], ALU.max)
            last.then_inc(read_of("cntT"), 1)
            stored(dve, "cntT")
            for t in range(NT):
                last = v.tensor_tensor(adj[:, t, token(t)], adj[:, t, token(t)], ident[:, :], ALU.add)
            link(last)
            v.tensor_reduce(deg[:, :], adj[:, :, :], AX.X, ALU.add).then_inc(deg_ready, 1)
            dve.wait_ge(row_sum, 1)
            v.tensor_scalar(valid[:, :], rowsum[:, :], 0.0, None, ALU.is_gt)
            link(v.tensor_scalar(rsum[:, :], rowsum[:, :], 1e-6, None, ALU.add))
            link(v.reciprocal(rsum[:, :], rsum[:, :]))
            for t in range(NT):
                last = v.tensor_scalar(att[:, t, :], att[:, t, :], rsum[:, t:t + 1], None, ALU.mult)
            last.then_inc(att_ready, 1)
            dve.wait_ge(dinv_ready, 1)
            for t in range(NT):
                last = v.tensor_scalar(adj[:, t, :], adj[:, t, :], dinv[:, t:t + 1], None, ALU.mult)
            last.then_inc(adj_ready, 1)

            def add_adj(t):
                job = f"adj.{t}"
                filled(dve, job)
                v.scalar_tensor_tensor(X[:, t, :], bank(job)[:, :], dinv[:, t:t + 1], X[:, t, :], ALU.mult, ALU.add)\
                    .then_inc(read_of(job), 1)
                stored(dve, job)

            add_to_x("mix_p.0")
            add_adj(0)
            ln_stats(LN_FFN, 0, X)
            add_to_x("mix_p.1")
            ln_apply(LN_FFN, 0, X, XN)
            add_adj(1)
            ln_stats(LN_FFN, 1, X)
            ln_apply(LN_FFN, 1, X, XN)
            pooled(0)
            filled(dve, "r0.hid")
            v.tensor_scalar(hid_c[:, :], bank("r0.hid")[:, 0:1], column("r0_b1"), 0.0, ALU.add, ALU.max)\
                .then_inc(read_of("r0.hid"), 1)
            dve.wait_ge(params_loaded, 16 * 7)
            route(0, K0, 1)
            for t in range(NT):
                turned_low("xT1", XT, t)
            weight_low("ffn_v")
            filled(dve, "ffn_v.1")
            v.tensor_copy(V[:, 1, :], bank("ffn_v.1")[:, :]).then_inc(read_of("ffn_v.1"), 1)
            for j in range(2):
                job = f"ffn_k.{j}"
                filled(dve, job)
                v.tensor_copy(chunks(K, j), by_chunk(job)).then_inc(read_of(job), 1)
            attention("ffn")
            for t in range(NT):
                turned_low("ffn.oT", OT, t)
            for t in range(NT):
                add_to_x(f"ffn_o.{t}")
                ln_stats(LN_IN1, t, X)
            for t in range(NT):
                ln_apply(LN_IN1, t, X, XN)

            for t in range(NT):
                turned_low("xT2", XT, t)
            filled(dve, "g.feat")
            brow = row_there("graph_in")
            v.tensor_tensor(mfeat, bank("g.feat")[:, :].rearrange("p (t n) -> p t n", t=NT),
                            brow[:, 0:N].unsqueeze(1).broadcast_to([P, NT, N]), ALU.add).then_inc(read_of("g.feat"), 1)
            for i in range(2):
                job = f"g.msg.{i}"
                high_out(dve, job)
                v.tensor_tensor(chunks(msg[1], i), by_chunk(job), chunks(msg[0], i).bitcast(F32), ALU.subtract)\
                    .then_inc(read_of(job), 1)
            filled(dve, "per_v.1")
            v.tensor_copy(V[:, 1, :], bank("per_v.1")[:, :]).then_inc(read_of("per_v.1"), 1)
            filled(dve, "g.hid")
            v.tensor_tensor(hgr, bank("g.hid")[:, 0:N].rearrange("p (t n) -> p t n", t=NT),
                            brow[:, N:N + HID].unsqueeze(1).broadcast_to([P, NT, HID]), ALU.add)\
                .then_inc(read_of("g.hid"), 1)
            stored(dve, "g.hid")
            for t in range(NT):
                ln_stats(LN_GRAPH, t, hgr, HID)
            for t in range(NT):
                ln_apply(LN_GRAPH, t, hgr, hgr, HID)
            filled(dve, "g.zT")
            v.tensor_scalar(zTf, bank("g.zT")[:, 0:N], column("gamma"), column("beta"), ALU.mult, ALU.add)\
                .then_inc(read_of("g.zT"), 1)
            stored(dve, "g.zT")
            link(v.tensor_scalar(zT[0][:, :], zTf, 0.0, None, ALU.max))
            v.scalar_tensor_tensor(zT[1][:, :], zTf, 0.0, zT[0][:, :].bitcast(F32), ALU.max, ALU.subtract)\
                .then_inc(split_low, 1)

            def exp_in(u, f_job, n_job):
                filled(dve, f_job)
                v.tensor_scalar(PR[:, u, :], bank(f_job)[:, :], 50.0, None, ALU.min).then_inc(read_of(f_job), 1)
                filled(dve, n_job)
                v.tensor_scalar(PT[:, u, :], bank(n_job)[:, :], 1e-16, -0.5, ALU.max, ALU.mult)\
                    .then_inc(read_of(n_job), 1)

            def exp_out(u, dst):
                dve.wait_ge(phi_exp, 4 + u + 1)
                v.scalar_tensor_tensor(dst, PT[:, u, :], 1e-8, PR[:, u, :], ALU.max, ALU.mult).then_inc(phi_ready, 1)

            for t in range(NT):
                exp_in(t, f"per.kf.{t}", f"per.kn.{t}")
            for t in range(NT):
                add_row(f"g.out.{t}", graph_out[:, t, :], "graph_out")
            for t in range(NT):
                exp_out(t, kphi_p[:, t, :])
            for j in range(2):
                exp_in(2 + j, f"per.qf.{j}", f"per.qn.{j}")
            for j in range(2):
                exp_out(2 + j, qphi_p[:, 2 * j:2 * j + 2, :].rearrange("p c n -> p (c n)"))
            diagonals("per")
            stored(dve, "g.out.1")
            for t in range(NT):
                last = v.tensor_scalar(graph_out[:, t, :], graph_out[:, t, :], 0.0, valid[:, t:t + 1], ALU.max, ALU.mult)
            link(last)
            linear_out("per")
            for t in range(NT):
                last = v.tensor_tensor(X[:, t, :], X[:, t, :], graph_out[:, t, :], ALU.add)
            link(last)
            for t in range(NT):
                turned_low("per.oT", OT, t)
            for t in range(NT):
                add_to_x(f"per_o.{t}")
                ln_stats(LN_X3, t, X)

            for t in range(NT):
                ln_apply(LN_X3, t, X, XN)
            dve.wait_ge(ln_out, 2 * LN_X3 + 2)
            ln_stats(LN_Z, 0, XN)
            pooled(1)
            ln_stats(LN_Z, 1, XN)
            route(1, K1, 2)
            for t in range(NT):
                ln_apply(LN_Z, t, XN, ZN)
            for j in range(2):
                scale_shift(f"xT3.{j}", xsf, j, "ns_w", "ns_b").then_inc(full_form, 1)
            for j in range(2):
                dve.wait_ge(full_form, j + 1)
                low_of(XT, chunks(xsf, j), j, 1 + j).then_inc(split_low, 1)
            weight_low("sp_v")
            for j in range(2):
                low_of(XT2, chunks(xtf, j), j, 3 + j).then_inc(split_low, 1)
            for t in range(NT):
                add_row(f"sp_v.{t}", V[:, t, :], "sp_v")
            dve.wait_ge(scol_loaded, 16)
            for j in range(2):
                scaled_query(f"sp_q.{j}", j, lambda c: scol[:, c:c + 1])
            attention("sp")
            dve.wait_ge(tcol_loaded, 16)
            for j in range(2):
                scaled_query(f"tm_q.{j}", j, lambda c: tcol[:, c:c + 1])
            for t in range(NT):
                add_row(f"tm_v.{t}", V[:, t, :], "tm_v")
            for t in range(NT):
                turned_low("sp.oT", OT, t)
            attention("tm")
            for j in range(2):
                job = f"sp_o.{j}"
                dve.wait_ge(split_high, 5 + j)
                for f in range(2):
                    c = 2 * j + f
                    last = v.scalar_tensor_tensor(SP[1][:, c, :], bank(job)[:, f * N:(f + 1) * N],
                                                  scol[:, 2 * DC + c:2 * DC + c + 1], SP[0][:, c, :].bitcast(F32),
                                                  ALU.add, ALU.subtract)
                last.then_inc(read_of(job), 1)
            for t in range(NT):
                turned_low("tm.oT", OT, t)
            for j in range(2):
                scaled_query(f"cr_q.{j}", j, lambda c: column("cr_bq", c))
            for j in range(2):
                job = f"tm_o.{j}"
                filled(dve, job)
                for f in range(2):
                    c = 2 * j + f
                    last = v.scalar_tensor_tensor(tmf[:, c, :], bank(job)[:, f * N:(f + 1) * N],
                                                  tcol[:, 2 * DC + c:2 * DC + c + 1], xtf[:, c, :], ALU.add, ALU.add)
                last.then_inc(read_of(job), 1)
            for j in range(2):
                stored(dve, f"tm_o.{j}")
                low_of(TM, chunks(tmf, j), j, 7 + j).then_inc(split_low, 1)
            for t in range(NT):
                add_row(f"cr_v.{t}", V[:, t, :], "cr_v")
            attention("cr")
            for t in range(NT):
                turned_low("cr.oT", OT, t)
            for t in range(NT):
                last = v.tensor_tensor(XN[:, t, :], XN[:, t, :], row_there("cr_o"), ALU.add)
            link(last)
            for t in range(NT):
                job = f"cr_o.{t}"
                filled(dve, job)
                v.tensor_tensor(XN[:, t, :], bank(job)[:, :], XN[:, t, :], ALU.add).then_inc(read_of(job), 1)
                stored(dve, job)
                ln_stats(LN_MLP, t, XN)
            for t in range(NT):
                ln_apply(LN_MLP, t, XN, ZN)

            for j in range(2):
                scale_shift(f"xT4.{j}", xsf, j, "nm_w", "nm_b").then_inc(full_form, 1)
            for j in range(2):
                dve.wait_ge(full_form, 3 + j)
                low_of(XT, chunks(xsf, j), j, 9 + j).then_inc(read_of(f"xT4.{j}"), 1)
            for other in (XN[:, :, :], row_there("down").unsqueeze(1).broadcast_to([P, NT, D])):
                link(v.tensor_tensor(X[:, :, :], X[:, :, :], other, ALU.add))
            for j in range(FC // 2):
                stored(dve, f"up.{j}")
                link(v.tensor_copy(chunks(G[0], j), gf[j % 4]))
                v.tensor_tensor(chunks(G[1], j), gf[j % 4], chunks(G[0], j).bitcast(F32), ALU.subtract)\
                    .then_inc(split_low, 1)
            for t in range(NT):
                job = f"down.{t}"
                filled(dve, job)
                v.tensor_tensor(ZN[:, t, :], bank(job)[:, :], X[:, t, :], ALU.add).then_inc(out_ready, 1)

        @block.scalar
        def _(act):
            s = nc.scalar

            def round_quarter(k):
                act.wait_ge(raw_loaded[k % RAW], 16 * (k // RAW + 1))
                i, c = divmod(k, 4)
                if c == 0 and i >= SPLIT:
                    filled(act, LAST_JOB[WEIGHTS[i - SPLIT]])
                s.copy(parts(k)[0], wraw[:, k % RAW, :]).then_inc(high_done, 1)

            def weight_high(w):
                for c in range(DC):
                    round_quarter(quarter(w, c))

            def target_hots(g):
                if g >= 2:
                    act.wait_ge(hots_dst, g - 1)
                for c in range(EG):
                    e = g * EG + c
                    last = s.activation(sq16[:, g % 2, c, :], iota16[:, :], ACT.Square, bias=edge_f[:, 2, e:e + 1])
                last.then_inc(sq_ready, 1)
                act.wait_ge(sq_ready, g + 1)
                if g >= 2:
                    act.wait_ge(hots_used, g - 1)
                s.activation(hot[:, g % 2, :, 1, :], sq16[:, g % 2, :, :], ACT.Relu, bias=1.0, scale=-1.0).then_inc(hots_dst, 1)

            def turned_high(prefix, pair):
                for t in range(NT):
                    job = f"{prefix}.{t}"
                    filled(act, job)
                    s.copy(pair[0][:, :, token(t)], bank(job)[:, :].rearrange("p (c n) -> p c n", c=DC))\
                        .then_inc(high_taken, 1)

            def elu_exp(u):
                act.wait_ge(phi_in, u + 1)
                s.activation(PT[:, u, :], PT[:, u, :], ACT.Exp).then_inc(phi_exp, 1)

            def performer_exp(u, job):
                stored(act, job)
                s.activation(PT[:, u, :], PT[:, u, :], ACT.Exp)
                s.activation(PR[:, u, :], PR[:, u, :], ACT.Exp).then_inc(phi_exp, 1)

            def attention(name, *meanwhile):
                a, causal = ATTENTIONS.index(name), name == "tm"
                quarters = [quarter(w, c) for w in meanwhile for c in range(DC)]
                for h in range(H):
                    act.wait_ge(score_max, H * a + h + 1)
                    if h >= 4:
                        filled(act, f"{name}.t{h - 4}")
                    for t in range(NT):
                        keys = P if causal and t == 0 else N
                        last = s.activation(PR[:, h % 4, t * N:t * N + keys], bank(f"{name}.s{h}")[:, t * N:t * N + keys],
                                            ACT.Exp, bias=nmax[:, h, t:t + 1], accum_out=psum_[:, h, t:t + 1])
                    last.then_inc(read_of(f"{name}.s{h}"), 1)
                    for k in quarters[2 * h - 2:2 * h] if h else []:
                        round_quarter(k)

            def shifted(job, dst, bias, j, scale=1.0):
                for f in range(2):
                    c = 2 * j + f
                    last = s.activation(dst[:, c, :], bank(job)[:, f * N:(f + 1) * N], ACT.Identity, bias=bias(c),
                                        scale=scale if isinstance(scale, float) else scale(c))
                return last

            def scaled(job, dst, j, square=None):
                filled(act, job)
                flat = lambda ap: ap[:, 2 * j:2 * j + 2, :].rearrange("p c n -> p (c n)")
                last = s.activation(flat(dst), bank(job)[:, :], ACT.Copy, scale=SCALE)
                if square is not None:
                    last = s.activation(flat(square), bank(job)[:, :], ACT.Square, scale=SCALE)
                last.then_inc(read_of(job), 1)

            def take_whole(job, dst):
                filled(act, job)
                s.copy(dst, bank(job)[:, :]).then_inc(read_of(job), 1)

            act.wait_ge(gate_neg, 1)
            s.activation(ew[:, 1, :], ew[:, 0, :], ACT.Exp, bias=gmax[:, 2:3]).then_inc(gate_exp, 1)
            weight_high("mix_v")
            turned_high("xT0", XT)
            act.wait_ge(consts, IOTA_CONST)
            act.wait_ge(dst_ready, 1)
            target_hots(0)
            weight_high("mix_k")
            target_hots(1)
            weight_high("mix_q")
            for u in range(2):
                elu_exp(u)
            target_hots(2)
            weight_high("gnn")
            for u in range(2, 4):
                elu_exp(u)
            target_hots(3)
            for t in range(NT):
                take_whole(f"gnn.{t}", hg[:, t, :])
            target_hots(4)
            weight_high("mix_p")
            target_hots(5)
            target_hots(6)
            target_hots(7)
            turned_high("mix.oT", OT)
            act.wait_ge(acc_read, 1)
            for t in range(NT):
                last = s.activation(att[:, t, :], acc[t][:, N:], ACT.Copy, accum_out=rowsum[:, t:t + 1])
            last.then_inc(row_sum, 1)
            take_whole("attT", attT[:, :, :].rearrange("p t n -> p (t n)"))
            turned_high("xT1", XT)
            act.wait_ge(logit_max, 1)
            s.activation(r[:, 8:8 + K0], r[:, 0:K0], ACT.Exp, bias=r[:, 32:33], accum_out=r[:, 34:35]).then_inc(logit_exp, 1)
            for w in ("ffn_v", "ffn_q", "ffn_k"):
                weight_high(w)
            take_whole("ffn_v.0", V[:, 0, :])
            for j in range(2):
                scaled(f"ffn_q.{j}", Q, j)
            weight_high("ffn_o")
            attention("ffn", "graph", "per_k", "per_v")
            turned_high("ffn.oT", OT)

            weight_high("per_q")
            turned_high("xT2", XT)
            for j in range(2):
                scaled(f"per_k.{j}", K, j, ksq)
            for i in range(2):
                job = f"g.msg.{i}"
                filled(act, job)
                s.copy(msg[0][:, 2 * i:2 * i + 2, :].rearrange("p c n -> p (c n)"), bank(job)[:, :]).then_inc(high_taken, 1)
            take_whole("per_v.0", V[:, 0, :])
            for j in range(2):
                scaled(f"per_q.{j}", Q, j, qsq)
            for u, job in enumerate(both("per.kn")):
                performer_exp(u, job)
            weight_high("per_o")
            for u, job in enumerate(both("per.qn")):
                performer_exp(2 + u, job)
            turned_high("per.oT", OT)
            filled(act, "r1.hid")
            s.activation(hid_c[:, :], bank("r1.hid")[:, 0:1], ACT.Gelu, bias=column("r1_b1")).then_inc(read_of("r1.hid"), 1)
            act.wait_ge(logit_max, 2)
            s.activation(r[:, 8:8 + 2 * K1], r[:, 0:2 * K1], ACT.Exp, bias=r[:, 32:33], accum_out=r[:, 34:35])\
                .then_inc(logit_exp, 1)
            for j in range(2):
                act.wait_ge(full_form, j + 1)
                shifted(f"xT3.{j}", XT[0], lambda c: column("ns_b", c), j, lambda c: column("ns_w", c))\
                    .then_inc(split_high, 1)
            for w in ("sp_v", "sp_q"):
                weight_high(w)
            for j in range(2):
                shifted(f"xT3.{j}", xtf, lambda c: column("nt_b", c), j, lambda c: column("nt_w", c))\
                    .then_inc(read_of(f"xT3.{j}"), 1)
                stored(act, f"xT3.{j}")
                s.copy(XT2[0][:, 2 * j:2 * j + 2, :], xtf[:, 2 * j:2 * j + 2, :]).then_inc(split_high, 1)
            for w in ("sp_k", "tm_q"):
                weight_high(w)
            act.wait_ge(scol_loaded, 16)
            for j in range(2):
                filled(act, f"sp_k.{j}")
                shifted(f"sp_k.{j}", K, lambda c: scol[:, DC + c:DC + c + 1], j).then_inc(read_of(f"sp_k.{j}"), 1)
            attention("sp", "tm_k", "tm_v", "sp_o")
            act.wait_ge(tcol_loaded, 16)
            for j in range(2):
                filled(act, f"tm_k.{j}")
                shifted(f"tm_k.{j}", K, lambda c: tcol[:, DC + c:DC + c + 1], j).then_inc(read_of(f"tm_k.{j}"), 1)
            turned_high("sp.oT", OT)
            attention("tm", "cr_q", "tm_o", "cr_k")
            for j in range(2):
                filled(act, f"sp_o.{j}")
                shifted(f"sp_o.{j}", SP[0], lambda c: scol[:, 2 * DC + c:2 * DC + c + 1], j).then_inc(split_high, 1)
            turned_high("tm.oT", OT)
            weight_high("cr_v")
            for j in range(2):
                stored(act, f"tm_o.{j}")
                s.copy(TM[0][:, 2 * j:2 * j + 2, :], tmf[:, 2 * j:2 * j + 2, :]).then_inc(split_high, 1)
            weight_high("cr_o")
            for j in range(2):
                filled(act, f"cr_k.{j}")
                shifted(f"cr_k.{j}", K, lambda c: column("cr_bk", c), j).then_inc(read_of(f"cr_k.{j}"), 1)
            attention("cr", "up_0", "up_1", "up_2")
            turned_high("cr.oT", OT)
            weight_high("up_3")
            for j in range(2):
                act.wait_ge(full_form, 3 + j)
                shifted(f"xT4.{j}", XT[0], lambda c: column("nm_b", c), j, lambda c: column("nm_w", c))\
                    .then_inc(split_high, 1)
            for j in range(FC // 2):
                job = f"up.{j}"
                filled(act, job)
                if j >= 4:
                    act.wait_ge(split_low, 7 + (j - 4) + 1)
                for f in range(2):
                    last = s.activation(gf[j % 4][:, f, :], bank(job)[:, f * N:(f + 1) * N], ACT.Gelu,
                                        bias=column("up_b", 2 * j + f))
                last.then_inc(read_of(job), 1)
                if j % 2:
                    weight_high(f"down_{j // 2}")

        @block.gpsimd
        def _(pool):
            g = nc.gpsimd
            made = [0]

            def make(ins):
                made[0] += 1
                ins.then_inc(consts, 1)
                pool.wait_ge(consts, made[0])

            def diagonal(tile):
                make(g.memset(tile[:, :], 0.0))
                make(g.affine_select(out=tile[:, :], in_=tile[:, :], compare_op=ALU.not_equal, fill=1.0, base=0,
                                     pattern=[[-1, P]], channel_multiplier=1))

            def rsqrt(n):
                for t in range(NT):
                    pool.wait_ge(ln_var, 2 * n + t + 1)
                    g.tensor_tensor(rstd[:, t:t + 1], ve[:, t:t + 1], half[:, 0:1], ALU.pow).then_inc(ln_rstd, 1)
                    pool.wait_ge(ln_rstd, 2 * n + t + 1)

            def weight_low(w):
                for c in range(DC):
                    k = quarter(w, c)
                    if k in LOW_ON_POOL:
                        pool.wait_ge(high_done, k + 1)
                        hi, lo = parts(k)
                        g.tensor_tensor(lo, wraw[:, k % RAW, :], hi.bitcast(F32), ALU.subtract).then_inc(low_done[0], 1)
                        low_ready(pool, k)

            def source_hots(n):
                if n >= 2:
                    pool.wait_ge(hots_used, n - 1)
                for c in range(EG):
                    e = n * EG + c
                    g.tensor_scalar(hot[:, n % 2, c, 0, :], iota16[:, :], edge_f[:, 0, e:e + 1], None, ALU.is_equal)\
                        .then_inc(hots_src, 1)
                    pool.wait_ge(hots_src, e + 1)

            diagonal(ident)
            make(g.memset(half[:, :], -0.5))
            assert made[0] == FIRST_CONSTS
            make(g.iota(iota16[:, :], [[1, N]], base=0, channel_multiplier=0, allow_small_or_imprecise_dtypes=True))
            assert made[0] == IOTA_CONST
            pool.wait_ge(gate_max, 1)
            g.partition_all_reduce(gmax[:, 1:2], gmax[:, 0:1], P, bass.bass_isa.ReduceOp.max).then_inc(gate_all, 1)
            pool.wait_ge(gate_all, 1)
            rsqrt(LN_IN0)
            weight_low("mix_v")
            pool.wait_ge(dst_ready, 1)
            source_hots(0)
            weight_low("mix_k")
            source_hots(1)
            make(g.iota(desc[:, :], [[-1, 4]], base=4, channel_multiplier=0, allow_small_or_imprecise_dtypes=True))
            diagonal(ident16)
            make(g.memset(mask16[:, :], 0.0))
            make(g.affine_select(out=mask16[:, :], in_=mask16[:, :], compare_op=ALU.is_ge, fill=MASKED, base=0,
                                 pattern=[[-1, P]], channel_multiplier=1))
            make(g.memset(ones[:, :], 1.0))
            make(g.memset(halves[:, :], 0.0))
            for b in range(2):
                s = slice(64 * b, 64 * b + 64)
                make(g.memset(halves[s, s], 1.0))
            make(g.memset(KV[:, :, :], 0.0))
            make(g.memset(KS[:, :, :], 0.0))
            make(g.memset(omega[:, :, :], 0.0))
            assert made[0] == ALL_CONSTS
            weight_low("mix_q")
            source_hots(2)
            weight_low("gnn")
            for n in range(3, 5):
                source_hots(n)
            weight_low("mix_p")
            for n in range(5, EC // EG):
                source_hots(n)
            pool.wait_ge(deg_ready, 1)
            g.tensor_tensor(dinv[:, :], deg[:, :], half[:, :], ALU.pow).then_inc(dinv_ready, 1)
            pool.wait_ge(dinv_ready, 1)
            rsqrt(LN_FFN)
            for w in ("ffn_v", "ffn_q", "ffn_k", "ffn_o", "graph", "per_k", "per_v"):
                weight_low(w)
            rsqrt(LN_IN1)
            weight_low("per_q")
            rsqrt(LN_GRAPH)
            weight_low("per_o")
            rsqrt(LN_X3)
            rsqrt(LN_Z)
            for w in ("sp_v", "sp_q", "sp_k", "tm_q", "tm_k", "tm_v", "sp_o", "cr_q", "tm_o", "cr_k", "cr_v", "cr_o",
                      "up_0", "up_1", "up_2"):
                weight_low(w)
            rsqrt(LN_MLP)
            for w in ("up_3", "down_0", "down_1", "down_2", "down_3"):
                weight_low(w)


def chunked(w):
    k, n = w.shape
    return w.reshape(k // P, P, n).transpose(1, 0, 2).reshape(P, k // P * n)


def by_column(b):
    return b.reshape(-1, P).T


def kernel(**inputs):
    import concourse.bacc as bacc
    from concourse.bass_utils import run_bass_kernel_spmd

    i = {k: np.asarray(a) for k, a in inputs.items()}
    f0, f1, g1, m0, m1 = "L0_ffn_", "L1_ffn_", "L1_gnn_", "L0_mix_", "L1_mix_"

    def heads(w):
        kv = w.shape[1] // 64
        return np.repeat(w.reshape(D, kv, 1, 64), H // kv, axis=2).reshape(D, D)

    static = {"mix_k": i[m0 + "Wk"], "mix_v": i[m0 + "Wv"], "mix_q": i[m0 + "Wq"], "mix_p": i[m0 + "Wp"],
              "gnn": i["L0_gnn_weight"], "per_k": i[m1 + "Wk"], "per_v": i[m1 + "Wv"], "per_q": i[m1 + "Wq"],
              "per_o": i[m1 + "Wo"], "cr_o": i[f1 + "cross_out_w"].T}
    for j, part in enumerate("qkv"):
        static[f"cr_{part}"] = i[f1 + "cross_in_w"][j * D:(j + 1) * D].T
    for j in range(4):
        static[f"up_{j}"] = i[f1 + "mlp_w1"][j * D:(j + 1) * D].T
        static[f"down_{j}"] = i[f1 + "mlp_w2"][:, j * D:(j + 1) * D].T
    laid = {k: chunked(w) for k, w in static.items()}
    laid["graph"] = np.concatenate([chunked(i[g1 + "Wm"]), chunked(i[g1 + "W1"]), i[g1 + "W2"]], axis=1)
    sp_in = i[f1 + "sp_in_w"].reshape(K1, 3, D, D)
    sp_b = i[f1 + "sp_in_b"].reshape(K1, 3, D)
    arrays = {
        "x": i["x"],
        "edges": np.stack([i["src"].reshape(P, EC), i["dst"].reshape(P, EC)], axis=1),
        "gate": i["edge_weight"].reshape(P, EC),
        "cols": np.concatenate(
            [by_column(i[k]) for k in (m0 + "bq", f0 + "r_b1", g1 + "gamma", g1 + "beta", f1 + "router_b1",
                                       f1 + "norm_s_w", f1 + "norm_s_b", f1 + "norm_t_w", f1 + "norm_t_b",
                                       f1 + "norm_mlp_w", f1 + "norm_mlp_b", f1 + "mlp_b1")]
            + [by_column(i[f1 + "cross_in_b"][j * D:(j + 1) * D]) for j in range(2)]
            + [i[f0 + "r_w2"], i[f1 + "router_w2"].T], axis=1),
        "rows": np.stack([i[m0 + "bv"], i[m0 + "bk"], i["L0_gnn_bias"], i[m0 + "bp"],
                          np.concatenate([i[g1 + "bm"], i[g1 + "b1"], np.zeros(D - N - HID, np.float32)]),
                          i[g1 + "b2"], i[f1 + "cross_in_b"][2 * D:], i[f1 + "cross_out_b"], i[f1 + "mlp_b2"]]),
        "router_rows": np.concatenate([i[f0 + "r_b2"], i[f1 + "router_b2"],
                                       np.zeros(16 - K0 - 2 * K1, np.float32)]).reshape(1, 16),
        "routers": np.stack([chunked(i[f0 + "r_w1"]), chunked(i[f1 + "router_w1"].T)], axis=1),
        "omegas": np.stack([i[m1 + "omega_q"], i[m1 + "omega_k"]]),
        "weights": np.stack([laid[w] for w in STATIC]),
        "ffn_w": np.stack([np.stack([chunked(i[f"{f0}wq{e}"]), chunked(heads(i[f"{f0}wk{e}"])),
                                     chunked(heads(i[f"{f0}wv{e}"])), chunked(i[f"{f0}wo{e}"])]) for e in range(K0)]),
        "sp_w": np.stack([np.stack([chunked(sp_in[e, j].T) for j in range(3)] + [chunked(i[f1 + "sp_out_w"][e].T)])
                          for e in range(K1)]),
        "tm_w": np.stack([np.stack([chunked(i[f"{f1}t{p}_w"][e].T) for p in "qkvp"]) for e in range(K1)]),
        "sp_cols": np.stack([np.concatenate([by_column(sp_b[e, 0]), by_column(sp_b[e, 1]),
                                             by_column(i[f1 + "sp_out_b"][e])], axis=1) for e in range(K1)]),
        "tm_cols": np.stack([np.concatenate([by_column(i[f"{f1}t{p}_b"][e]) for p in "qkp"], axis=1)
                             for e in range(K1)]),
        "sp_row": sp_b[:, 2],
        "tm_row": i[f1 + "tv_b"],
    }
    nc = bacc.Bacc("TRN2", target_bir_lowering=False, num_devices=1)
    feed, args = {}, {}
    for name, a in arrays.items():
        a = np.ascontiguousarray(a)
        feed[f"in_{name}"] = a
        args[name] = nc.dram_tensor(f"in_{name}", a.shape, mybir.dt.from_np(a.dtype), kind="ExternalInput").ap()
    args["out"] = nc.dram_tensor("out_0", (N, D), F32, kind="ExternalOutput").ap()
    build(nc, **args)
    result = run_bass_kernel_spmd(nc, [feed], core_ids=[0])
    return result.results[0]["out_0"]
```

```python
from contextlib import ExitStack

import numpy as np

import concourse.bass as bass
from concourse import mybir

ALU = mybir.AluOpType
ACT = mybir.ActivationFunctionType
AX = mybir.AxisListType
F32 = mybir.dt.float32
BF16 = mybir.dt.bfloat16
I32 = mybir.dt.int32
F32R = mybir.dt.float32r

P = 128
N = 256
D = 512
H = 8
NT = N // P
DC = D // P
HP = H // 2
HID = 128
E = 4096
EC = E // P
EG = 4
GROUPS = EC // EG
DEFERRED = 5
PLAIN = 4
SCALED = 5
FC = 4 * D // P
K0, K1 = 3, 4
EPS = 1e-5
SCALE = 0.125
MASKED = -1e30

RAW = 12
SPLIT = 4
ROWS = 4

WEIGHTS = (["mix_v", "mix_k", "mix_q", "gnn", "mix_p", "ffn_q", "ffn_k", "ffn_v", "ffn_o", "graph",
            "per_k", "per_v", "per_q", "per_o", "sp_q", "sp_k", "sp_v", "tm_q", "tm_k", "tm_v",
            "sp_o", "cr_q", "tm_o", "cr_k", "cr_v", "cr_o"]
           + [f"up_{i}" for i in range(4)] + [f"down_{i}" for i in range(4)])
STATIC = [w for w in WEIGHTS if w.split("_")[0] not in ("ffn", "sp", "tm")]
PART = {"q": 0, "k": 1, "v": 2, "o": 3}
BIAS_ROWS = ["mix_v", "mix_k", "gnn", "mix_p", "graph_in", "graph_out", "sp_v", "tm_v", "cr_v", "cr_o", "down"]
ROW_BEFORE = {"mix_k": ["mix_v", "mix_k"], "mix_q": ["gnn", "mix_p"], "graph": ["graph_in", "graph_out"],
              "sp_v": ["sp_v"], "tm_v": ["tm_v"], "cr_v": ["cr_v"], "cr_o": ["cr_o"], "down_0": ["down"]}
STATIC_ROWS = [r for r in BIAS_ROWS if r not in ("sp_v", "tm_v")]

COLS, _at = {}, 0
for _name, _width in [("mix_bq", DC), ("r0_b1", 1), ("gamma", 1), ("beta", 1), ("r1_b1", 1), ("ns_w", DC), ("ns_b", DC),
                      ("nt_w", DC), ("nt_b", DC), ("nm_w", DC), ("nm_b", DC), ("up_b", FC), ("cr_bq", DC),
                      ("cr_bk", DC), ("r0_w2", K0), ("r1_w2", 2 * K1)]:
    COLS[_name] = (_at, _at + _width)
    _at += _width
NCOLS = _at


MEANWHILE = {"sp": ["tm_q.0", "tm_q.1", "tm_k.0"], "tm": ["sp_o.0", "sp_o.1"]}


def attention_jobs(a):
    out = []
    for i in range(H + 3):
        out += MEANWHILE.get(a, [])[i - H:i - H + 1] if i >= H else []
        if i < H:
            out.append(f"{a}.s{i}")
        if 0 <= i - 2 < H:
            out.append(f"{a}.t{i - 2}")
    return out


def both(*names):
    return [f"{n}.{t}" for n in names for t in range(2)]


JOBS = (both("xT0", "mix_v", "mix_k", "mix_q", "gnn") + both("mix.kv") + ["mix.den"]
        + both("mix.num", "mix.oT") + ["cntT"] + both("mix_p", "adj")
        + both("xT1") + ["r0.hid", "r0.out"] + both("ffn_q", "ffn_k") + ["attT"] + both("ffn_v")
        + attention_jobs("ffn") + both("ffn.oT", "ffn_o")
        + ["xT2.0", "g.feat", "per_v.0", "xT2.1"] + both("per_k", "g.msg") + ["per_v.1", "g.hid"] + both("per_q")
        + ["g.zT"] + both("per.kf", "per.kn", "per.qf", "per.qn", "g.out")
        + both("per.kv") + ["per.den"] + both("per.num", "per.oT", "per_o")
        + both("r1.xT") + ["r1.hid", "r1.out"] + both("xT3", "sp_q", "sp_k", "sp_v")
        + attention_jobs("sp") + ["tm_k.1"] + both("tm_v", "sp.oT") + attention_jobs("tm")
        + both("cr_q", "tm.oT", "tm_o", "cr_k", "cr_v") + attention_jobs("cr")
        + both("cr.oT", "cr_o", "xT4") + [f"up.{j}" for j in range(FC // 2)] + both("down"))
ROTATING = 6
TURN = {name: divmod(i, ROTATING) for i, name in enumerate(JOBS)}
ATTENTIONS = ["ffn", "sp", "tm", "cr"]
SPLIT_SCORES = ["ffn", "sp", "cr"]

LAST_JOB = {w: f"{w}.1" for w in WEIGHTS} | {"graph": "g.out.1"}
LAST_JOB |= {f"up_{i}": f"up.{2 * i + 1}" for i in range(4)} | {f"down_{i}": "down.1" for i in range(4)}
ROW_DONE = {"mix_k": "mix_k.1", "mix_v": "mix_v.1", "gnn": "mix_p.1", "mix_p": "mix_p.1", "graph_in": "g.hid",
            "graph_out": "g.out.1", "sp_v": "sp_v.1", "tm_v": "tm_v.1", "cr_v": "cr_v.1", "cr_o": "cr_o.1",
            "down": "down.1"}

FIRST_CONSTS, IOTA_CONST, ALL_CONSTS = 3, 4, 16

LOW_ON_VECTOR = [4 * WEIGHTS.index(w) + c for w, cs in (("mix_v", (1, 3)), ("mix_q", (1, 3)), ("ffn_q", (1, 3)),
                                                        ("ffn_k", (1, 3)), ("per_o", (1,)), ("sp_q", (1, 3)),
                                                        ("sp_k", (1, 3))) for c in cs]
LOW_ON_POOL = [k for k in range(4 * len(WEIGHTS)) if k not in LOW_ON_VECTOR]
HIGH = both("xT0", "mix.oT", "xT1", "ffn.oT", "xT2", "g.msg", "per.oT", "sp.oT", "tm.oT", "cr.oT")

LN_IN0, LN_FFN, LN_IN1, LN_GRAPH, LN_X3, LN_Z, LN_MLP = range(7)


def build(nc, x, edges, gate, cols, rows, router_rows, routers, omegas, weights, ffn_w, sp_w, tm_w,
          sp_cols, tm_cols, sp_row, tm_row, out):
    with ExitStack() as ctx:
        def sb(name, shape, dt=F32):
            return ctx.enter_context(nc.sbuf_tensor(name, shape, dt))

        def sem(name):
            return ctx.enter_context(nc.semaphore(name))

        wraw = sb("wraw", [P, RAW, D])
        wh = sb("wh", [P, SPLIT, DC, D], F32R)
        wl = sb("wl", [P, SPLIT, DC, D], F32R)
        rslot = sb("rslot", [P, ROWS, D])
        X = sb("X", [P, NT, D])
        XN = sb("XN", [P, NT, D])
        ZN = sb("ZN", [P, NT, D])
        XT = [sb(f"XT{i}", [P, DC, N], F32R) for i in range(2)]
        with ExitStack() as counting:
            hot_odd = counting.enter_context(nc.sbuf_tensor("hot_odd", [P, EG, 4, N], F32R))
        XT2 = [sb(f"XT2{i}", [P, DC, N], F32R) for i in range(2)]
        OT = [sb(f"OT{i}", [P, DC, N], F32R) for i in range(2)]
        zT = [sb(f"zT{i}", [P, N], F32R) for i in range(2)]
        Q = sb("Q", [P, DC, N])
        K = sb("K", [P, DC, N])
        V = sb("V", [P, NT, HP, P + 1])
        O = sb("O", [P, NT, D])
        with ExitStack() as early:
            PR = early.enter_context(nc.sbuf_tensor("PR", [P, 4, NT * N], F32))
            PT = early.enter_context(nc.sbuf_tensor("PT", [P, 4, NT * N], F32))
            with ExitStack() as attending:
                QR, KR = [[attending.enter_context(nc.sbuf_tensor(f"{name}{i}", [P, DC, N], F32R)) for i in range(2)]
                          for name in ("QR", "KR")]
            with ExitStack() as counting:
                hot_even = counting.enter_context(nc.sbuf_tensor("hot_even", [P, EG, 4, N], F32R))
            big = early.enter_context(nc.sbuf_tensor("big", [P, FC * N], F32))
        G = [sb(f"G{i}", [P, FC, N], F32R) for i in range(2)]
        big2 = sb("big2", [P, 1024])
        KV = sb("KV", [P, HP, P])
        KS = sb("KS", [P, HP, 2])
        att = sb("att", [P, NT, N])
        attT = sb("attT", [P, NT, N])
        ident = sb("ident", [P, P])
        ident16 = sb("ident16", [P, P], BF16)
        mask16 = sb("mask16", [P, P], BF16)
        halves = sb("halves", [P, P])
        omega = sb("omega", [P, 2, P])
        router_w = sb("router_w", [P, 2, DC * HID])
        col = sb("col", [P, NCOLS])
        scol = sb("scol", [P, 3 * DC])
        tcol = sb("tcol", [P, 3 * DC])
        rrow = sb("rrow", [1, 16])
        desc = sb("desc", [1, 4])
        iota16 = sb("iota16", [P, N], BF16)
        edge_i = sb("edge_i", [P, 2, EC], I32)
        sq16 = sb("sq16", [P, 2, EG, N], BF16)
        edge_f = sb("edge_f", [P, 3, EC])
        ew = sb("ew", [P, 4, EC])
        ew16 = sb("ew16", [P, 2, EC], BF16)
        ewr = sb("ewr", [P, 2, EC], F32R)
        gmax = sb("gmax", [P, 4])
        bn = sb("bn", [P, NT, 6])
        mv = sb("mv", [P, NT, 2])
        ve = sb("ve", [P, NT])
        rstd = sb("rstd", [P, NT])
        half = sb("half", [P, NT])
        deg = sb("deg", [P, NT])
        dinv = sb("dinv", [P, NT])
        rowsum = sb("rowsum", [P, NT])
        rsum = sb("rsum", [P, NT])
        valid = sb("valid", [P, NT])
        nmax = sb("nmax", [P, H, NT])
        psum_ = sb("psum_", [P, H, NT])
        rprob = sb("rprob", [P, NT, H])
        den = sb("den", [P, NT, H])
        pool_t = sb("pool_t", [P, NT, DC])
        pool_c = sb("pool_c", [P, DC])
        hid_c = sb("hid_c", [P, 1])
        r = sb("r", [1, 64])
        ridx = sb("ridx", [1, 4], I32)
        hot = big[:, :].bitcast(BF16).rearrange("p (b c k n) -> p b c k n", b=2, c=EG, k=4)
        hotlo = big2[:, :].bitcast(BF16).rearrange("p (b c n) -> p b c n", b=2, c=EG)
        hot6, hot7 = [b[:, :, :].rearrange("p a n -> p (a n)").bitcast(BF16).rearrange("p (c k n) -> p c k n", c=EG, k=4)
                      for b in (PR, PT)]
        hotlo6, hotlo7 = [b[:, :, :].rearrange("p t n -> p (t n)").bitcast(BF16).rearrange("p (c n) -> p c n", c=EG)
                          for b in (attT, att)]
        cnt, adj = XN[:, 0, :].rearrange("p (t n) -> p t n", t=NT), XN[:, 1, :].rearrange("p (t n) -> p t n", t=NT)
        hg = ZN
        graph_out = K[:, :, :].rearrange("p (t a) n -> p t (a n)", t=NT)
        kphi_m, qphi_m = K[:, :, :].rearrange("p (t a) n -> p t (a n)", t=NT), Q
        ksq = big[:, 0:1024].rearrange("p (c n) -> p c n", c=DC)
        qsq = big[:, 1024:2048].rearrange("p (c n) -> p c n", c=DC)
        kphi_p = big[:, 2048:3072].rearrange("p (t n) -> p t n", t=NT)
        mfeat = big[:, 3072:3584].rearrange("p (t n) -> p t n", t=NT)
        hgr = big[:, 3584:3840].rearrange("p (t f) -> p t f", t=NT)
        zTf = big[:, 3840:4096]
        qphi_p = ZN[:, :, :].rearrange("p t (a n) -> p (t a) n", n=N)
        msg = XT2
        SP, TM = XT, XT2
        xsf = K
        xtf = ZN[:, :, :].rearrange("p t (a n) -> p (t a) n", n=N)
        tmf = PT[:, 0:2, :].rearrange("p a (b n) -> p (a b) n", n=N)
        gf = [Q[:, 0:2, :], Q[:, 2:4, :], K[:, 0:2, :], K[:, 2:4, :]]

        banks = [ctx.enter_context(nc.psum_tensor(f"bank{i}", [P, 512], F32)) for i in range(8)]
        acc = banks[6:8]

        raw_loaded = [sem(f"raw_loaded{i}") for i in range(RAW)]
        high_done = sem("high_done")
        low_done = [sem("low_by_pool"), sem("low_by_vector")]
        high_taken = sem("high_taken")
        full_form = sem("full_form")
        split_high = sem("split_high")
        split_low = sem("split_low")
        q_high, q_low, k_high = sem("q_high"), sem("q_low"), sem("k_high")
        row_loaded = [sem(f"row_loaded{i}") for i in range(ROWS)]
        full = [sem(f"bank_full{i}") for i in range(ROTATING)]
        read = [sem(f"bank_read{i}") for i in range(ROTATING)]
        acc_full, acc_read = sem("acc_full"), sem("acc_read")
        x_loaded = [sem(f"x_loaded{t}") for t in range(NT)]
        edges_loaded, params_loaded = sem("edges_loaded"), sem("params_loaded")
        scol_loaded, tcol_loaded = sem("scol_loaded"), sem("tcol_loaded")
        consts = sem("consts")
        gate_max, gate_all, gate_neg, gate_exp = sem("gate_max"), sem("gate_all"), sem("gate_neg"), sem("gate_exp")
        hots_src, hots_dst, hots_weighted = sem("hots_src"), sem("hots_dst"), sem("hots_weighted")
        hots_plain, hots_scaled = sem("hots_plain"), sem("hots_scaled")
        hots_used, counts_full, sums_full = sem("hots_used"), sem("counts_full"), sem("sums_full")
        dst_ready, sq_ready, row_sum, pool_read = sem("dst_ready"), sem("sq_ready"), sem("row_sum"), sem("pool_read")
        ln_var, ln_rstd, ln_out = sem("ln_var"), sem("ln_rstd"), sem("ln_out")
        biases_added, graph_biased = sem("biases_added"), sem("graph_biased")
        deg_ready, dinv_ready = sem("deg_ready"), sem("dinv_ready")
        adj_ready, att_ready = sem("adj_ready"), sem("att_ready")
        phi_in, phi_exp, phi_ready = sem("phi_in"), sem("phi_exp"), sem("phi_ready")
        score_max = sem("score_max")
        logit_max, logit_exp, route_ready = sem("logit_max"), sem("logit_exp"), sem("route_ready")
        out_ready, out_stored = sem("out_ready"), sem("out_stored")
        dve_step = sem("dve_step")

        def bank(job):
            return banks[TURN[job][1]]

        def filled(eng, job):
            eng.wait_ge(full[TURN[job][1]], TURN[job][0] + 1)

        def stored(eng, job):
            eng.wait_ge(read[TURN[job][1]], TURN[job][0] + 1)

        def full_of(job):
            return full[TURN[job][1]]

        def read_of(job):
            return read[TURN[job][1]]

        def quarter(w, c):
            return 4 * WEIGHTS.index(w) + c

        def low_ready(eng, k):
            if k in LOW_ON_VECTOR:
                eng.wait_ge(low_done[1], LOW_ON_VECTOR.index(k) + 1)
            else:
                eng.wait_ge(low_done[0], LOW_ON_POOL.index(k) + 1)

        def parts(k):
            i, c = divmod(k, 4)
            return wh[:, i % SPLIT, c, :], wl[:, i % SPLIT, c, :]

        def high_out(eng, job):
            eng.wait_ge(high_taken, HIGH.index(job) + 1)

        def hots(g):
            if g < DEFERRED:
                return (hot_odd if g % 2 else hot_even), None
            if g < 6:
                return hot[:, g % 2, :, :, :], hotlo[:, g % 2, :, :]
            return (hot6, hotlo6) if g == 6 else (hot7, hotlo7)

        def hots_free(eng, g):
            if g >= 6:
                eng.wait_ge(phi_ready, 4)
            elif g == DEFERRED:
                eng.wait_ge(hots_used, g)
            elif g >= 2:
                eng.wait_ge(hots_used, g - 1)

        def row(name):
            return rslot[:, BIAS_ROWS.index(name) % ROWS, :]

        def column(name, i=0):
            return col[:, COLS[name][0] + i:COLS[name][0] + i + 1]

        def by_pair(ap):
            return ap.rearrange("p (h n) -> p h n", h=HP)

        def token(t):
            return slice(t * P, (t + 1) * P)

        block = ctx.enter_context(nc.Block())

        @block.sync
        def _(sp):
            sp.dma_start(edge_i[:, :, :], edges).then_inc(edges_loaded, 16)
            sp.dma_start(ew[:, 0, :], gate).then_inc(edges_loaded, 16)
            for t in range(NT):
                sp.dma_start(X[:, t, :], x[t * P:(t + 1) * P, :]).then_inc(x_loaded[t], 16)

            index = {}

            def load_row(name):
                i = BIAS_ROWS.index(name)
                if i >= ROWS:
                    stored(sp, ROW_DONE[BIAS_ROWS[i - ROWS]])
                if name == "sp_v":
                    src = sp_row[bass.ds(index["sp"], 1), :]
                elif name == "tm_v":
                    src = tm_row[bass.ds(index["tm"], 1), :]
                else:
                    j = STATIC_ROWS.index(name)
                    src = rows[j:j + 1, :]
                sp.dma_start(row(name), src.partition_broadcast(P)).then_inc(row_loaded[i % ROWS], 16)

            def load_weight(w):
                family, part = (w.split("_") + [""])[:2]
                for c in range(DC):
                    k = quarter(w, c)
                    if k >= RAW:
                        sp.wait_ge(high_done, k - RAW + 1)
                        low_ready(sp, k - RAW)
                    if family in ("ffn", "sp", "tm"):
                        table = {"ffn": ffn_w, "sp": sp_w, "tm": tm_w}[family]
                        src = table[bass.ds(index[family], 1), PART[part], :, c * D:(c + 1) * D]\
                            .rearrange("a p n -> p (a n)")
                    else:
                        src = weights[STATIC.index(w), :, c * D:(c + 1) * D]
                    sp.dma_start(wraw[:, k % RAW, :], src).then_inc(raw_loaded[k % RAW], 16)

            for w in WEIGHTS:
                if w == "ffn_q":
                    sp.wait_ge(route_ready, 1)
                    index["ffn"] = nc.sync.value_load(ridx[0:1, 0:1], min_val=0, max_val=K0 - 1)
                if w == "sp_q":
                    sp.wait_ge(route_ready, 2)
                    index["sp"] = nc.sync.value_load(ridx[0:1, 2:3], min_val=0, max_val=K1 - 1)
                if w == "sp_k":
                    index["tm"] = nc.sync.value_load(ridx[0:1, 3:4], min_val=0, max_val=K1 - 1)
                for name in ROW_BEFORE.get(w, []):
                    load_row(name)
                load_weight(w)
                if w == "sp_k":
                    sp.dma_start(scol[:, :], sp_cols[bass.ds(index["sp"], 1), :, :].rearrange("a p n -> p (a n)"))\
                      .then_inc(scol_loaded, 16)
                    sp.dma_start(tcol[:, :], tm_cols[bass.ds(index["tm"], 1), :, :].rearrange("a p n -> p (a n)"))\
                      .then_inc(tcol_loaded, 16)
                if w == "mix_v":
                    sp.dma_start(col[:, :], cols).then_inc(params_loaded, 16)
                if w == "mix_p":
                    sp.dma_start(router_w[:, :, :], routers).then_inc(params_loaded, 16)
                    sp.dma_start(rrow[:, :], router_rows).then_inc(params_loaded, 16)
                    sp.wait_ge(consts, ALL_CONSTS)
                    for i in range(2):
                        for b in range(2):
                            sp.dma_start(omega[64 * b:64 * b + 64, i, 64 * b:64 * b + 64], omegas[i, :, :])\
                              .then_inc(params_loaded, 16)
            for t in range(NT):
                sp.wait_ge(out_ready, t + 1)
                sp.dma_start(out[t * P:(t + 1) * P, :], ZN[:, t, :]).then_inc(out_stored, 16)
            sp.wait_ge(out_stored, 16 * NT)

        @block.tensor
        def _(pe):
            mm, transpose = nc.tensor.matmul, nc.tensor.transpose

            def take(job):
                turn, b = TURN[job]
                if turn:
                    pe.wait_ge(read[b], turn)
                return banks[b]

            def keep_warm(n, ps=acc[0]):
                for _ in range(n):
                    mm(ps[:, 0:P], ident[:, :], ident[:, :], start=True, stop=True)

            def three(out, lhs, rhs, first, last):
                mm(out, lhs[0], rhs[0], start=first, stop=False)
                mm(out, lhs[0], rhs[1], start=False, stop=False)
                return mm(out, lhs[1], rhs[0], start=False, stop=last)

            def with_high(ps, w, src, t):
                for c in range(DC):
                    low_ready(pe, quarter(w, c))
                    for i, part in enumerate(parts(quarter(w, c))):
                        mm(ps[:, :], src[0][:, c, token(t)], part, start=c == i == 0, stop=False)

            def with_low(ps, w, src, t):
                for c in range(DC):
                    last = mm(ps[:, :], src[1][:, c, token(t)], parts(quarter(w, c))[0], start=False, stop=c == DC - 1)
                last.then_inc(full_of(f"{w}.{t}"), 1)

            def features_with_high(ps, w, src, j, cs, begin):
                for c in cs:
                    low_ready(pe, quarter(w, c))
                    for f in range(2):
                        for part in parts(quarter(w, c)):
                            mm(ps[:, f * N:(f + 1) * N], part[:, token(2 * (j % 2) + f)], src[0][:, c, :],
                               start=begin, stop=False, skip_group_check=True)
                            begin = False

            def features_with_low(ps, w, src, j, cs):
                for c in cs:
                    for f in range(2):
                        last = mm(ps[:, f * N:(f + 1) * N], parts(quarter(w, c))[0][:, token(2 * (j % 2) + f)],
                                  src[1][:, c, :], start=False, stop=c == DC - 1, skip_group_check=True)
                return last

            def of(pair, *index):
                return [part[index] for part in pair]

            def turn_tile(prefix, src, n, t):
                pe.wait_ge(ln_out, 2 * n + t + 1)
                ps = take(f"{prefix}.{t}")
                for c in range(DC):
                    last = transpose(ps[:, token(c)], src[:, t, token(c)], ident[:, :])
                last.then_inc(full_of(f"{prefix}.{t}"), 1)

            def to_features(prefix, src, n):
                for t in range(NT):
                    turn_tile(prefix, src, n, t)

            def per_token(w, src, t, turned=None):
                if turned:
                    high_out(pe, f"{turned}.{t}")
                ps = take(f"{w}.{t}")
                with_high(ps, w, src, t)
                if turned:
                    stored(pe, f"{turned}.{t}")
                with_low(ps, w, src, t)

            LAG = 2

            def both_tiles(w, src):
                pss = [take(f"{w}.{t}") for t in range(NT)]
                for c in range(DC + LAG):
                    if c < DC:
                        pe.wait_ge(high_done, quarter(w, c) + 1)
                        for t in range(NT):
                            mm(pss[t][:, :], src[0][:, c, token(t)], parts(quarter(w, c))[0], start=c == 0, stop=False)
                    if c < LAG:
                        continue
                    if c == LAG:
                        yield
                    b = c - LAG
                    low_ready(pe, quarter(w, b))
                    high, low = parts(quarter(w, b))
                    for t in range(NT):
                        mm(pss[t][:, :], src[0][:, b, token(t)], low, start=False, stop=False)
                        last = mm(pss[t][:, :], src[1][:, b, token(t)], high, start=False, stop=b == DC - 1)
                        if b == DC - 1:
                            last.then_inc(full_of(f"{w}.{t}"), 1)

            def both_halves(w, src):
                pss = [take(f"{w}.{j}") for j in range(2)]

                def passes(c, w_part, x_part, begin=False):
                    for j in range(2):
                        for f in range(2):
                            last = mm(pss[j][:, f * N:(f + 1) * N],
                                      parts(quarter(w, c))[w_part][:, token(2 * j + f)], src[x_part][:, c, :],
                                      start=begin and f == 0, stop=False, skip_group_check=True)
                        if c == DC - 1 and x_part == 1:
                            last.then_inc(full_of(f"{w}.{j}"), 1)

                for c in range(DC + LAG):
                    if c < DC:
                        pe.wait_ge(high_done, quarter(w, c) + 1)
                        passes(c, 0, 0, c == 0)
                    if c < LAG:
                        continue
                    if c == LAG:
                        yield
                    low_ready(pe, quarter(w, c - LAG))
                    passes(c - LAG, 1, 0)
                    passes(c - LAG, 0, 1)

            def per_feature(w, src, j, job=None, turned=None):
                ps = take(job or f"{w}.{j % 2}")
                if turned:
                    high_out(pe, f"{turned}.1")
                features_with_high(ps, w, src, j, range(DC), True)
                for t in range(NT) if turned else []:
                    stored(pe, f"{turned}.{t}")
                features_with_low(ps, w, src, j, range(DC)).then_inc(full_of(job or f"{w}.{j % 2}"), 1)

            def fresh_features(w, jobs, src, high, low):
                pss = [take(job) for job in jobs]
                for i in range(2):
                    high(i)
                    for j in range(2):
                        features_with_high(pss[j], w, src, j, (2 * i, 2 * i + 1), i == 0)
                for i in range(2):
                    low(i)
                    if i == 0:
                        for j in range(2):
                            features_with_low(pss[j], w, src, j, (0, 1))
                for j in range(2):
                    features_with_low(pss[j], w, src, j, (2, 3)).then_inc(full_of(jobs[j]), 1)

            def two_chunks(prefix, src, n):
                pss = [take(f"{prefix}.{j}") for j in range(2)]
                for t in range(NT):
                    pe.wait_ge(ln_out, 2 * n + t + 1)
                    for j in range(2):
                        for f in range(2):
                            at = f * N + t * P
                            last = transpose(pss[j][:, at:at + P], src[:, t, token(2 * j + f)], ident[:, :])
                        if t == NT - 1:
                            last.then_inc(full_of(f"{prefix}.{j}"), 1)

            def graph_w(at, n):
                i = WEIGHTS.index("graph") % SPLIT
                return [part[:, i, at // D, at % D:at % D + n] for part in (wh, wl)]

            def edge_group(g):
                if g < PLAIN:
                    pe.wait_ge(hots_src, EG * (g + 1))
                    pe.wait_ge(hots_dst, g + 1)
                else:
                    pe.wait_ge(hots_plain, g - PLAIN + 1)
                pe.wait_ge(hots_weighted, g + 1)
                h, _ = hots(g)
                for c in range(EG):
                    for t in range(NT):
                        src = h[:, c, 0, token(t)]
                        mm(acc[t][:, :], src, h[:, c, 1:3, :], start=g == c == 0, stop=False, skip_group_check=True)
                        last = mm(acc[t][:, N:], src, h[:, c, 3, :], start=False, stop=False, skip_group_check=True)
                last.then_inc(hots_used, 1)

            def edge_counts(g):
                pe.wait_ge(hots_plain, g - PLAIN + 1)
                h, _ = hots(g)
                for c in range(EG):
                    for t in range(NT):
                        last = mm(acc[t][:, 0:N], h[:, c, 0, token(t)], h[:, c, 1, :], start=False,
                                  stop=g == GROUPS - 1 and c == EG - 1, skip_group_check=True)
                if g == GROUPS - 1:
                    last.then_inc(counts_full, 1)

            def edge_sums(g, cs):
                pe.wait_ge(hots_scaled, g - SCALED + 1)
                h, hlo = hots(g)
                for c in cs:
                    for t in range(NT):
                        src, end = h[:, c, 0, token(t)], g == GROUPS - 1 and c == EG - 1
                        for part in (h[:, c, 2, :], h[:, c, 3, :], hlo[:, c, :]):
                            last = mm(acc[t][:, N:], src, part, start=False, stop=False, skip_group_check=True)
                if end:
                    last.then_inc(sums_full, 1)

            def linear_sums(name, kphi, first):
                pe.wait_ge(phi_ready, first + 2)
                for i in range(2):
                    ps = take(f"{name}.kv.{i}")
                    for p in range(2):
                        for t in range(NT):
                            last = mm(ps[:, p * (P + 1):(p + 1) * (P + 1)], kphi[:, t, token(2 * i + p)],
                                      V[:, t, 2 * i + p, :], start=t == 0, stop=t == NT - 1)
                    last.then_inc(full_of(f"{name}.kv.{i}"), 1)

            def linear_products(name, qphi, first):
                if name == "per":
                    keep_warm(5)
                pe.wait_ge(phi_ready, first + 4)
                for i in range(2):
                    stored(pe, f"{name}.kv.{i}")
                ps = take(f"{name}.den")
                for t in range(NT):
                    for p in range(HP):
                        at = t * H + 2 * p
                        last = mm(ps[:, at:at + 2], qphi[:, p, token(t)], KS[:, p, :], start=True, stop=True)
                last.then_inc(full_of(f"{name}.den"), 1)
                for t in range(NT):
                    ps = take(f"{name}.num.{t}")
                    for p in range(HP):
                        last = mm(ps[:, token(p)], qphi[:, p, token(t)], KV[:, p, :], start=True, stop=True)
                    last.then_inc(full_of(f"{name}.num.{t}"), 1)

            def heads_to_features(name):
                for t in range(NT):
                    ps = take(f"{name}.oT.{t}")
                    if t == 0 and name in ("ffn", "cr"):
                        keep_warm(4, ps)
                    if name in ATTENTIONS:
                        pe.wait_ge(acc_read, 1 + 2 * ATTENTIONS.index(name) + t + 1)
                    else:
                        stored(pe, f"{name}.num.{t}")
                    for c in range(DC):
                        last = transpose(ps[:, token(c)], O[:, t, token(c)], ident[:, :])
                    last.then_inc(full_of(f"{name}.oT.{t}"), 1)

            def router_hidden(n):
                pe.wait_ge(params_loaded, 16 * 7)
                pe.wait_ge(pool_read, 3 + n)
                ps = take(f"r{n}.hid")
                for c in range(DC):
                    last = mm(ps[:, 0:1], router_w[:, n, token(c)], pool_c[:, c:c + 1], start=c == 0, stop=c == DC - 1)
                last.then_inc(full_of(f"r{n}.hid"), 1)

            def router_logits(n):
                stored(pe, f"r{n}.hid")
                ps = take(f"r{n}.out")
                a, b = COLS[f"r{n}_w2"]
                mm(ps[0:1, 0:b - a], hid_c[:, :], col[:, a:b], start=True, stop=True)\
                    .then_inc(full_of(f"r{n}.out"), 1)

            def attention(name):
                a, causal = ATTENTIONS.index(name), name == "tm"

                def scores(h):
                    if h % 4 == 0:
                        stored(pe, f"{name}_k.{h // 4}")
                        if name in ("sp", "cr"):
                            pe.wait_ge(q_low, 2 * (name == "cr") + h // 4 + 1)
                        else:
                            stored(pe, f"{name}_q.{h // 4}")
                    ps = take(f"{name}.s{h}")
                    lo = 64 * (h % 2)
                    if not causal:
                        for t in range(NT):
                            q, k = [[part[lo:lo + 64, h // 2, at] for part in pair]
                                    for pair, at in ((QR, token(t)), (KR, slice(None)))]
                            last = three(ps[:, t * N:(t + 1) * N], q, k, True, True)
                        last.then_inc(full_of(f"{name}.s{h}"), 1)
                        return
                    q, k = Q[lo:lo + 64, h // 2, :], K[lo:lo + 64, h // 2, :]
                    for t in range(NT):
                        keys = (t + 1) * P if causal else N
                        last = mm(ps[:, t * N:t * N + keys], q[:, token(t)], k[:, 0:keys], start=True, stop=True)
                        if causal:
                            last = mm(ps[:, t * N + keys - P:t * N + keys], ident16[:, :], mask16[:, :], start=False,
                                      stop=True, skip_group_check=True)
                    last.then_inc(full_of(f"{name}.s{h}"), 1)

                def turn_probs(h):
                    stored(pe, f"{name}.s{h}")
                    ps = take(f"{name}.t{h}")
                    for i, (k, q) in enumerate([(0, 0), (0, 1), (1, 1)] + [(1, 0)] * (not causal)):
                        last = transpose(ps[:, token(i)], PR[:, h % 4, q * N + k * P:q * N + (k + 1) * P], ident[:, :])
                    last.then_inc(full_of(f"{name}.t{h}"), 1)

                def values(h):
                    stored(pe, f"{name}.t{h}")
                    if h == 0:
                        for t in range(NT):
                            stored(pe, f"{name}_v.{t}")
                    pt, lo = PT[:, h % 4, :], 64 * (h % 2)
                    for t in range(NT):
                        o = acc[t][:, 64 * h:64 * h + 64]
                        first = pt[:, token(t)]
                        last = mm(o, first, V[:, 0, h // 2, lo:lo + 64], start=True, stop=causal and t == 0)
                        if not (causal and t == 0):
                            last = mm(o, pt[:, token(3 - t)], V[:, 1, h // 2, lo:lo + 64], start=False, stop=True)
                    return last

                for i in range(H + 3):
                    if i < H:
                        scores(i)
                    else:
                        for job in MEANWHILE.get(name, [])[i - H:i - H + 1]:
                            w, j = job.split(".")
                            if job == "tm_q.0":
                                pe.wait_ge(split_low, 5)
                            if job == "sp_o.0":
                                for t in range(NT):
                                    stored(pe, f"sp.oT.{t}")
                            per_feature(w, XT2 if name == "sp" else OT, int(j))
                    if i == 2:
                        pe.wait_ge(acc_read, 1 + NT * a)
                        pe.wait_ge(row_sum, 1)
                        keep_warm(5 if causal else 2)
                    if 0 <= i - 2 < H:
                        turn_probs(i - 2)
                    if 0 <= i - 3:
                        last = values(i - 3)
                last.then_inc(acc_full, 1)

            def turn_table(job, table):
                ps = take(job)
                for t in range(NT):
                    for u in range(NT):
                        last = transpose(ps[:, u * N + t * P:u * N + (t + 1) * P], table[:, t, token(u)], ident[:, :])
                last.then_inc(full_of(job), 1)

            pe.wait_ge(consts, FIRST_CONSTS)
            keep_warm(16)
            to_features("xT0", XN, LN_IN0)
            for t in range(NT):
                high_out(pe, f"xT0.{t}")
            for _ in both_tiles("mix_v", XT):
                for t in range(NT):
                    stored(pe, f"xT0.{t}")
            edge_group(0)
            for t in range(NT):
                per_token("mix_k", XT, t)
            edge_group(1)
            for j in range(2):
                per_feature("mix_q", XT, j)
            edge_group(2)
            for t in range(NT):
                per_token("gnn", XT, t)
            edge_group(3)
            pe.wait_ge(consts, ALL_CONSTS)
            for t in range(NT):
                stored(pe, f"mix_v.{t}")
            linear_sums("mix", kphi_m, 0)
            edge_group(4)
            linear_products("mix", qphi_m, 0)
            for g in range(5, GROUPS):
                edge_counts(g)
            heads_to_features("mix")
            pe.wait_ge(acc_read, 1)
            turn_table("cntT", cnt)
            for t in range(NT):
                per_token("mix_p", OT, t, "mix.oT")
            pe.wait_ge(adj_ready, 1)
            for u in range(NT):
                stored(pe, f"gnn.{u}")
            for t in range(NT):
                ps = take(f"adj.{t}")
                for u in range(NT):
                    last = mm(ps[:, :], adj[:, u, token(t)], hg[:, u, :], start=u == 0, stop=u == NT - 1)
                last.then_inc(full_of(f"adj.{t}"), 1)

            edge_sums(5, range(EG))
            to_features("xT1", XN, LN_FFN)
            edge_sums(6, range(1))
            router_hidden(0)
            router_logits(0)
            edge_sums(6, range(1, EG))
            edge_sums(7, range(EG))
            for _ in both_halves("ffn_q", XT):
                for t in range(NT):
                    stored(pe, f"xT1.{t}")
            for j in range(2):
                per_feature("ffn_k", XT, j)
            pe.wait_ge(att_ready, 1)
            turn_table("attT", att)
            for t in range(NT):
                per_token("ffn_v", XT, t)
            attention("ffn")
            heads_to_features("ffn")
            for t in range(NT):
                per_token("ffn_o", OT, t, "ffn.oT")

            for c in range(DC):
                low_ready(pe, quarter("graph", c))
            turn_tile("xT2", XN, LN_IN1, 0)
            ps = take("g.feat")
            for t in range(NT):
                high_out(pe, f"xT2.{t}")
                for c in range(DC):
                    for i, part in enumerate(graph_w(c * N, N)):
                        mm(ps[:, t * N:(t + 1) * N], XT[0][:, c, token(t)], part, start=t == c == i == 0, stop=False,
                           skip_group_check=True)
                stored(pe, f"xT2.{t}")
                for c in range(DC):
                    last = mm(ps[:, t * N:(t + 1) * N], XT[1][:, c, token(t)], graph_w(c * N, N)[0], start=False,
                              stop=c == DC - 1, skip_group_check=True)
                if t == 0:
                    values_0 = take("per_v.0")
                    with_high(values_0, "per_v", XT, 0)
                    turn_tile("xT2", XN, LN_IN1, 1)
                    with_low(values_0, "per_v", XT, 0)
            last.then_inc(full_of("g.feat"), 1)
            for j in range(2):
                per_feature("per_k", XT, j)
            stored(pe, "g.feat")
            stored(pe, "attT")
            for i, table in enumerate((attT, att)):
                ps = take(f"g.msg.{i}")
                for f in range(2):
                    for u in range(NT):
                        last = mm(ps[:, f * N:(f + 1) * N], mfeat[:, u, token(f)], table[:, u, :], start=u == 0,
                                  stop=u == NT - 1)
                last.then_inc(full_of(f"g.msg.{i}"), 1)
            per_token("per_v", XT, 1)
            for i in range(2):
                stored(pe, f"g.msg.{i}")
            ps = take("g.hid")
            for t in range(NT):
                for c in range(DC):
                    last = three(ps[:, token(t)], of(msg, slice(None), c, token(t)), graph_w(DC * N + c * HID, HID),
                                 c == 0, c == DC - 1)
            last.then_inc(full_of("g.hid"), 1)
            for j in range(2):
                per_feature("per_q", XT, j)
            pe.wait_ge(ln_out, 2 * LN_GRAPH + 2)
            ps = take("g.zT")
            for t in range(NT):
                last = transpose(ps[:, token(t)], hgr[:, t, :], ident[:, :])
            last.then_inc(full_of("g.zT"), 1)
            for j in range(2):
                stored(pe, f"per_k.{j}")
            for job, lhs in (("kf", K), ("kn", ksq)):
                for t in range(NT):
                    ps = take(f"per.{job}.{t}")
                    for p in range(HP):
                        last = mm(ps[:, token(p)], lhs[:, p, token(t)], omega[:, 1, :] if job == "kf" else halves[:, :],
                                  start=True, stop=True)
                    last.then_inc(full_of(f"per.{job}.{t}"), 1)
            for j in range(2):
                stored(pe, f"per_q.{j}")
            for job, rhs in (("qf", Q), ("qn", qsq)):
                for j in range(2):
                    ps = take(f"per.{job}.{j}")
                    for f in range(2):
                        last = mm(ps[:, f * N:(f + 1) * N], omega[:, 0, :] if job == "qf" else halves[:, :],
                                  rhs[:, 2 * j + f, :], start=True, stop=True)
                    last.then_inc(full_of(f"per.{job}.{j}"), 1)
            pe.wait_ge(split_low, 1)
            for t in range(NT):
                ps = take(f"g.out.{t}")
                three(ps[:, :], of(zT, slice(None), token(t)), graph_w(DC * (N + HID), D), True, True)\
                    .then_inc(full_of(f"g.out.{t}"), 1)
            for t in range(NT):
                stored(pe, f"per_v.{t}")
            linear_sums("per", kphi_p, 4)
            linear_products("per", qphi_p, 4)
            heads_to_features("per")
            for t in range(NT):
                per_token("per_o", OT, t, "per.oT")

            keep_warm(8)
            to_features("r1.xT", XN, LN_X3)
            keep_warm(4)
            router_hidden(1)
            router_logits(1)
            two_chunks("xT3", ZN, LN_Z)
            keep_warm(16)
            pe.wait_ge(split_high, 2)
            for _ in both_halves("sp_q", XT):
                pe.wait_ge(split_low, 3)
            for j in range(2):
                per_feature("sp_k", XT, j)
            for t in range(NT):
                per_token("sp_v", XT, t)
            attention("sp")
            per_feature("tm_k", XT2, 1)
            for t in range(NT):
                per_token("tm_v", XT2, t)
            heads_to_features("sp")
            attention("tm")
            def spatial_low(i):
                if i == 0:
                    heads_to_features("tm")
                stored(pe, f"sp_o.{i}")

            fresh_features("cr_q", ["cr_q.0", "cr_q.1"], SP, lambda i: pe.wait_ge(split_high, 5 + i), spatial_low)
            for j in range(2):
                per_feature("tm_o", OT, j, turned="tm.oT")
            fresh_features("cr_k", ["cr_k.0", "cr_k.1"], TM, lambda i: pe.wait_ge(split_high, 7 + i),
                           lambda i: pe.wait_ge(split_low, 6 + i))
            for t in range(NT):
                per_token("cr_v", TM, t)
            attention("cr")
            heads_to_features("cr")
            for t in range(NT):
                per_token("cr_o", OT, t, "cr.oT")

            keep_warm(8)
            two_chunks("xT4", ZN, LN_MLP)
            keep_warm(3)
            fresh_features("up_0", ["up.0", "up.1"], XT, lambda i: pe.wait_ge(split_high, 9 + i),
                           lambda i: stored(pe, f"xT4.{i}"))
            for j in range(2, FC // 2):
                per_feature(f"up_{j // 2}", XT, j, f"up.{j}")
            for t in range(NT):
                ps = take(f"down.{t}")
                for c in range(FC):
                    if t == 0:
                        low_ready(pe, quarter("down_0", c))
                    if t == 0 and c % 2 == 0:
                        pe.wait_ge(split_low, 7 + c // 2 + 1)
                    last = three(ps[:, :], of(G, slice(None), c, token(t)), parts(quarter("down_0", c)), c == 0,
                                 c == FC - 1)
                last.then_inc(full_of(f"down.{t}"), 1)

        @block.vector
        def _(dve):
            v = nc.vector
            steps = [0]

            def link(ins):
                steps[0] += 1
                ins.then_inc(dve_step, 1)
                dve.wait_ge(dve_step, steps[0])

            def row_there(name):
                i = BIAS_ROWS.index(name)
                dve.wait_ge(row_loaded[i % ROWS], 16 * (i // ROWS + 1))
                return row(name)

            def ln_stats(n, t, src, width=D):
                link(v.bn_stats(bn[:, t, :], src[:, t, 0:width]))
                link(v.bn_aggr(mv[:, t, :], bn[:, t, :]))
                v.tensor_scalar(ve[:, t:t + 1], mv[:, t, 1:2], EPS, None, ALU.add).then_inc(ln_var, 1)

            def ln_apply(n, t, src, dst, width=D):
                dve.wait_ge(ln_rstd, 2 * n + t + 1)
                v.tensor_scalar(dst[:, t, 0:width], src[:, t, 0:width], mv[:, t, 0:1], rstd[:, t:t + 1],
                                ALU.subtract, ALU.mult).then_inc(ln_out, 1)

            def weighted_hots(g):
                hots_free(dve, g)
                h, _ = hots(g)
                for c in range(EG):
                    e = g * EG + c
                    for i in range(2):
                        last = v.tensor_scalar(h[:, c, 2 + i, :], iota16[:, :], edge_f[:, 1, e:e + 1],
                                               ewr[:, i, e:e + 1].bitcast(F32), ALU.is_equal, ALU.mult)
                last.then_inc(hots_weighted, 1)

            def plain_hots(g):
                hots_free(dve, g)
                h, _ = hots(g)
                for c in range(EG):
                    for kind in range(2):
                        last = v.tensor_scalar(h[:, c, kind, :], iota16[:, :], edge_f[:, kind, g * EG + c:g * EG + c + 1],
                                               None, ALU.is_equal)
                last.then_inc(hots_plain, 1)

            def weight_low(w):
                for c in range(DC):
                    k = quarter(w, c)
                    if k in LOW_ON_VECTOR:
                        dve.wait_ge(high_done, k + 1)
                        hi, lo = parts(k)
                        v.tensor_tensor(lo, wraw[:, k % RAW, :], hi.bitcast(F32), ALU.subtract).then_inc(low_done[1], 1)

            def turned_low(prefix, pair, t):
                job = f"{prefix}.{t}"
                high_out(dve, job)
                v.tensor_tensor(pair[1][:, :, token(t)], bank(job)[:, :].rearrange("p (c n) -> p c n", c=DC),
                                pair[0][:, :, token(t)].bitcast(F32), ALU.subtract).then_inc(read_of(job), 1)

            def chunks(ap, j):
                return ap[:, 2 * j:2 * j + 2, :]

            def by_chunk(job):
                return bank(job)[:, :].rearrange("p (c n) -> p c n", c=2)

            def value_row(t, name):
                job = f"{name}.{t}"
                filled(dve, job)
                v.tensor_tensor(V[:, t, :, 0:P], by_pair(bank(job)[:, :]), by_pair(row_there(name)), ALU.add)\
                    .then_inc(read_of(job), 1)

            def add_row(job, dst, name):
                filled(dve, job)
                v.tensor_tensor(dst, bank(job)[:, :], row_there(name), ALU.add).then_inc(read_of(job), 1)

            def elu_in(u, job):
                stored(dve, job)
                v.tensor_scalar(PT[:, u, :], PR[:, u, :], 0.0, None, ALU.min).then_inc(phi_in, 1)

            def elu_out(u, dst):
                dve.wait_ge(phi_exp, u + 1)
                v.scalar_tensor_tensor(dst, PR[:, u, :], 0.0, PT[:, u, :], ALU.max, ALU.add).then_inc(phi_ready, 1)

            def diagonals(name):
                for i in range(2):
                    job = f"{name}.kv.{i}"
                    filled(dve, job)
                    pairs, sums = slice(2 * i, 2 * i + 2), bank(job)[:, 0:2 * (P + 1)].rearrange("p (h n) -> p h n", h=2)
                    for b in range(2):
                        s = slice(64 * b, 64 * b + 64)
                        v.tensor_copy(KS[s, pairs, b], sums[s, :, P])
                        last = v.tensor_copy(KV[s, pairs, s], sums[s, :, s])
                    last.then_inc(read_of(job), 1)

            def by_head(ap):
                return ap.rearrange("p (h d) -> p h d", h=H)

            def linear_out(name):
                filled(dve, f"{name}.den")
                v.reciprocal(den[:, :, :].rearrange("p t h -> p (t h)"), bank(f"{name}.den")[:, 0:NT * H])\
                    .then_inc(read_of(f"{name}.den"), 1)
                stored(dve, f"{name}.den")
                for t in range(NT):
                    job = f"{name}.num.{t}"
                    filled(dve, job)
                    v.tensor_tensor(by_head(O[:, t, :]), by_head(bank(job)[:, :]),
                                    den[:, t, :].unsqueeze(2).broadcast_to([P, H, 64]), ALU.mult)\
                        .then_inc(read_of(job), 1)

            def pool_tile(job):
                filled(dve, job)
                return v.tensor_reduce(pool_t[:, int(job[-1]), :], bank(job)[:, :].rearrange("p (c n) -> p c n", c=DC),
                                       AX.X, ALU.add)

            def pooled():
                v.tensor_tensor(pool_c[:, :], pool_t[:, 0, :], pool_t[:, 1, :], ALU.add).then_inc(pool_read, 1)

            def route(n, k, groups):
                w = k * groups
                a, b = (0, K0) if n == 0 else (K0, K0 + 2 * K1)
                lg, pr, hit, at = r[:, 0:w], r[:, 8:8 + w], r[:, 16:16 + w], r[:, 24:24 + groups]
                grouped = lambda ap: ap.rearrange("p (g k) -> p g k", g=groups)
                filled(dve, f"r{n}.out")
                v.tensor_tensor(lg, bank(f"r{n}.out")[0:1, 0:w], rrow[:, a:b], ALU.add).then_inc(read_of(f"r{n}.out"), 1)
                stored(dve, f"r{n}.out")
                v.tensor_reduce(r[:, 32:33], lg, AX.X, ALU.max, negate=True).then_inc(logit_max, 1)
                if n == 1:
                    ln_apply(LN_Z, 1, XN, ZN)
                dve.wait_ge(logit_exp, n + 1)
                link(v.reciprocal(r[:, 33:34], r[:, 34:35]))
                link(v.tensor_scalar(lg, pr, r[:, 33:34], None, ALU.mult))
                link(v.tensor_reduce(r[:, 26:26 + groups], grouped(lg), AX.X, ALU.max))
                for i in range(groups):
                    last = v.scalar_tensor_tensor(hit[:, i * k:(i + 1) * k], lg[:, i * k:(i + 1) * k],
                                                  r[:, 26 + i:27 + i], desc[:, 4 - k:4], ALU.is_ge, ALU.mult)
                link(last)
                link(v.tensor_reduce(at, grouped(hit), AX.X, ALU.max))
                v.tensor_scalar(ridx[:, 2 * n:2 * n + groups], at, 1.0, -1.0, ALU.max, ALU.add).then_inc(route_ready, 1)

            def spatial_low():
                for j in range(2):
                    job = f"sp_o.{j}"
                    dve.wait_ge(split_high, 5 + j)
                    for f in range(2):
                        c = 2 * j + f
                        last = v.scalar_tensor_tensor(SP[1][:, c, :], bank(job)[:, f * N:(f + 1) * N],
                                                      scol[:, 2 * DC + c:2 * DC + c + 1], SP[0][:, c, :].bitcast(F32),
                                                      ALU.add, ALU.subtract)
                    last.then_inc(read_of(job), 1)

            def attention(name):
                a, causal = ATTENTIONS.index(name), name == "tm"
                for i in range(H + 2):
                    if i < H:
                        filled(dve, f"{name}.s{i}")
                        ps = bank(f"{name}.s{i}")
                        if causal:
                            v.tensor_reduce(nmax[:, i, 0:1], ps[:, 0:P], AX.X, ALU.max, negate=True)
                            v.tensor_reduce(nmax[:, i, 1:2], ps[:, N:2 * N], AX.X, ALU.max, negate=True)\
                                .then_inc(score_max, 1)
                        else:
                            v.tensor_reduce(nmax[:, i, :], ps[:, :].rearrange("p (t n) -> p t n", t=NT), AX.X, ALU.max,
                                            negate=True).then_inc(score_max, 1)
                    if i >= 2:
                        h, w = i - 2, 3 * P if causal else 4 * P
                        filled(dve, f"{name}.t{h}")
                        v.tensor_copy(PT[:, h % 4, 0:w], bank(f"{name}.t{h}")[:, 0:w]).then_inc(read_of(f"{name}.t{h}"), 1)
                if name == "tm":
                    spatial_low()
                stored(dve, f"{name}.s{H - 1}")
                link(v.reciprocal(rprob[:, :, :].rearrange("p t h -> p h t"), psum_[:, :, :]))
                dve.wait_ge(acc_full, a + 1)
                for t in range(NT):
                    v.tensor_tensor(by_head(O[:, t, :]), by_head(acc[t][:, :]),
                                    rprob[:, t, :].unsqueeze(2).broadcast_to([P, H, 64]), ALU.mult).then_inc(acc_read, 1)

            def add_to_x(job):
                t = int(job[-1])
                filled(dve, job)
                v.tensor_tensor(X[:, t, :], bank(job)[:, :], X[:, t, :], ALU.add).then_inc(read_of(job), 1)
                stored(dve, job)

            def scaled_query(job, j, bias):
                filled(dve, job)
                for f in range(2):
                    last = v.tensor_scalar(Q[:, 2 * j + f, :], bank(job)[:, f * N:(f + 1) * N], bias(2 * j + f), SCALE,
                                           ALU.add, ALU.mult)
                last.then_inc(read_of(job), 1)

            def query_low(name, j):
                dve.wait_ge(q_high, 2 * SPLIT_SCORES.index(name) + j + 1)
                v.tensor_tensor(chunks(QR[1], j), chunks(Q, j), chunks(QR[0], j).bitcast(F32), ALU.subtract)\
                    .then_inc(q_low, 1)

            def key_low(name, j, bias):
                job = f"{name}_k.{j}"
                dve.wait_ge(k_high, 2 * SPLIT_SCORES.index(name) + j + 1)
                for f in range(2):
                    c = 2 * j + f
                    last = v.scalar_tensor_tensor(KR[1][:, c, :], bank(job)[:, f * N:(f + 1) * N], bias(c),
                                                  KR[0][:, c, :].bitcast(F32), ALU.add, ALU.subtract)
                last.then_inc(read_of(job), 1)

            def scale_shift(job, dst, j, w, b):
                filled(dve, job)
                for f in range(2):
                    c = 2 * j + f
                    last = v.tensor_scalar(dst[:, c, :], bank(job)[:, f * N:(f + 1) * N], column(w, c), column(b, c),
                                           ALU.mult, ALU.add)
                return last

            def low_of(pair, whole, j, high):
                dve.wait_ge(split_high, high)
                return v.tensor_tensor(chunks(pair[1], j), whole, chunks(pair[0], j).bitcast(F32), ALU.subtract)

            dve.wait_ge(edges_loaded, 32)
            v.tensor_reduce(gmax[:, 0:1], ew[:, 0, :], AX.X, ALU.max).then_inc(gate_max, 1)
            v.tensor_copy(edge_f[:, 0:2, :], edge_i[:, :, :])
            v.tensor_scalar(edge_f[:, 2, :], edge_i[:, 1, :], -1.0, None, ALU.mult).then_inc(dst_ready, 1)
            dve.wait_ge(dst_ready, 1)
            for t in range(NT):
                dve.wait_ge(x_loaded[t], 16)
                ln_stats(LN_IN0, t, X)
            dve.wait_ge(gate_all, 1)
            v.tensor_scalar(gmax[:, 2:3], gmax[:, 1:2], 0.0, -1.0, ALU.max, ALU.mult).then_inc(gate_neg, 1)
            for t in range(NT):
                ln_apply(LN_IN0, t, X, XN)
            dve.wait_ge(gate_exp, 1)
            link(v.tensor_copy(ewr[:, 0, :], ew[:, 1, :]))
            v.tensor_tensor(ewr[:, 1, :], ew[:, 1, :], ewr[:, 0, :].bitcast(F32), ALU.subtract)
            link(v.tensor_copy(ew16[:, 0, :], ew[:, 1, :]))
            link(v.tensor_tensor(ew[:, 2, :], ew[:, 1, :], ew16[:, 0, :], ALU.subtract))
            link(v.tensor_copy(ew16[:, 1, :], ew[:, 2, :]))
            link(v.tensor_tensor(ew[:, 3, :], ew[:, 2, :], ew16[:, 1, :], ALU.subtract))
            for t in range(NT):
                turned_low("xT0", XT, t)
            weight_low("mix_v")

            dve.wait_ge(consts, IOTA_CONST)
            weighted_hots(0)
            for t in range(NT):
                value_row(t, "mix_v")
            weighted_hots(1)
            weight_low("mix_q")
            for t in range(NT):
                job = f"mix_k.{t}"
                filled(dve, job)
                v.tensor_tensor(PR[:, t, :], bank(job)[:, :], row_there("mix_k"), ALU.add).then_inc(read_of(job), 1)
                elu_in(t, job)
            weighted_hots(2)
            for t in range(NT):
                elu_out(t, kphi_m[:, t, :])
            for j in range(2):
                job = f"mix_q.{j}"
                filled(dve, job)
                for f in range(2):
                    last = v.tensor_scalar(PR[:, 2 + j, f * N:(f + 1) * N], bank(job)[:, f * N:(f + 1) * N],
                                           column("mix_bq", 2 * j + f), None, ALU.add)
                last.then_inc(read_of(job), 1)
                elu_in(2 + j, job)
            weighted_hots(3)
            for j in range(2):
                elu_out(2 + j, qphi_m[:, 2 * j:2 * j + 2, :].rearrange("p c n -> p (c n)"))
            plain_hots(4)
            weighted_hots(4)
            dve.wait_ge(consts, ALL_CONSTS)
            diagonals("mix")
            for g in range(PLAIN + 1, GROUPS):
                plain_hots(g)
            linear_out("mix")

            dve.wait_ge(counts_full, 1)
            for t in range(NT):
                last = v.tensor_scalar(cnt[:, t, :], acc[t][:, 0:N], 1.0, None, ALU.min)
            last.then_inc(acc_read, 1)
            dve.wait_ge(acc_read, 1)
            for t in range(NT):
                turned_low("mix.oT", OT, t)
            filled(dve, "cntT")
            for t in range(NT):
                last = v.tensor_tensor(adj[:, t, :], bank("cntT")[:, t * N:(t + 1) * N], cnt[:, t, :], ALU.max)
            last.then_inc(read_of("cntT"), 1)
            stored(dve, "cntT")
            for t in range(NT):
                last = v.tensor_tensor(adj[:, t, token(t)], adj[:, t, token(t)], ident[:, :], ALU.add)
            link(last)
            v.tensor_reduce(deg[:, :], adj[:, :, :], AX.X, ALU.add).then_inc(deg_ready, 1)
            dve.wait_ge(dinv_ready, 1)
            for t in range(NT):
                last = v.tensor_scalar(adj[:, t, :], adj[:, t, :], dinv[:, t:t + 1], None, ALU.mult)
            last.then_inc(adj_ready, 1)

            def add_adj(t):
                job = f"adj.{t}"
                filled(dve, job)
                v.scalar_tensor_tensor(X[:, t, :], bank(job)[:, :], dinv[:, t:t + 1], X[:, t, :], ALU.mult, ALU.add)\
                    .then_inc(read_of(job), 1)
                stored(dve, job)

            dve.wait_ge(biases_added, 2 * NT)
            for t in range(NT):
                add_to_x(f"mix_p.{t}")
            for t in range(NT):
                add_adj(t)
                ln_stats(LN_FFN, t, X)
            for t in range(NT):
                ln_apply(LN_FFN, t, X, XN)
            for t in range(NT):
                pool_tile(f"xT1.{t}").then_inc(pool_read, 1)
            dve.wait_ge(pool_read, NT)
            pooled()
            dve.wait_ge(params_loaded, 16 * 7)
            route(0, K0, 1)
            for t in range(NT):
                turned_low("xT1", XT, t)
            for w in ("ffn_q", "ffn_k"):
                weight_low(w)
            dve.wait_ge(row_sum, 1)
            v.tensor_scalar(valid[:, :], rowsum[:, :], 0.0, None, ALU.is_gt)
            link(v.tensor_scalar(rsum[:, :], rowsum[:, :], 1e-6, None, ALU.add))
            link(v.reciprocal(rsum[:, :], rsum[:, :]))
            for t in range(NT):
                last = v.tensor_scalar(att[:, t, :], att[:, t, :], rsum[:, t:t + 1], None, ALU.mult)
            last.then_inc(att_ready, 1)
            for j in range(2):
                job = f"ffn_q.{j}"
                dve.wait_ge(q_high, j + 1)
                v.scalar_tensor_tensor(chunks(QR[1], j), by_chunk(job), SCALE, chunks(QR[0], j).bitcast(F32), ALU.mult,
                                       ALU.subtract).then_inc(read_of(job), 1)
            for j in range(2):
                job = f"ffn_k.{j}"
                dve.wait_ge(k_high, j + 1)
                v.tensor_tensor(chunks(KR[1], j), by_chunk(job), chunks(KR[0], j).bitcast(F32), ALU.subtract)\
                    .then_inc(read_of(job), 1)
            filled(dve, "ffn_v.1")
            v.tensor_copy(V[:, 1, :, 0:P], by_pair(bank("ffn_v.1")[:, :])).then_inc(read_of("ffn_v.1"), 1)
            attention("ffn")
            for t in range(NT):
                turned_low("ffn.oT", OT, t)
            for t in range(NT):
                add_to_x(f"ffn_o.{t}")
                ln_stats(LN_IN1, t, X)
                if t:
                    turned_low("xT2", XT, 0)
                ln_apply(LN_IN1, t, X, XN)

            turned_low("xT2", XT, 1)
            filled(dve, "g.feat")
            brow = row_there("graph_in")
            v.tensor_tensor(mfeat, bank("g.feat")[:, :].rearrange("p (t n) -> p t n", t=NT),
                            brow[:, 0:N].unsqueeze(1).broadcast_to([P, NT, N]), ALU.add).then_inc(read_of("g.feat"), 1)
            for i in range(2):
                job = f"g.msg.{i}"
                high_out(dve, job)
                v.tensor_tensor(chunks(msg[1], i), by_chunk(job), chunks(msg[0], i).bitcast(F32), ALU.subtract)\
                    .then_inc(read_of(job), 1)
            filled(dve, "per_v.1")
            v.tensor_copy(V[:, 1, :, 0:P], by_pair(bank("per_v.1")[:, :])).then_inc(read_of("per_v.1"), 1)
            filled(dve, "g.hid")
            v.tensor_tensor(hgr, bank("g.hid")[:, 0:N].rearrange("p (t n) -> p t n", t=NT),
                            brow[:, N:N + HID].unsqueeze(1).broadcast_to([P, NT, HID]), ALU.add)\
                .then_inc(read_of("g.hid"), 1)
            stored(dve, "g.hid")
            for t in range(NT):
                ln_stats(LN_GRAPH, t, hgr, HID)
            for t in range(NT):
                ln_apply(LN_GRAPH, t, hgr, hgr, HID)
            filled(dve, "g.zT")
            v.tensor_scalar(zTf, bank("g.zT")[:, 0:N], column("gamma"), column("beta"), ALU.mult, ALU.add)\
                .then_inc(read_of("g.zT"), 1)
            stored(dve, "g.zT")
            link(v.tensor_scalar(zT[0][:, :], zTf, 0.0, None, ALU.max))
            v.scalar_tensor_tensor(zT[1][:, :], zTf, 0.0, zT[0][:, :].bitcast(F32), ALU.max, ALU.subtract)\
                .then_inc(split_low, 1)

            def exp_in(u, f_job, n_job):
                filled(dve, f_job)
                v.tensor_scalar(PR[:, u, :], bank(f_job)[:, :], 50.0, None, ALU.min).then_inc(read_of(f_job), 1)
                filled(dve, n_job)
                v.tensor_scalar(PT[:, u, :], bank(n_job)[:, :], 1e-16, -0.5, ALU.max, ALU.mult)\
                    .then_inc(read_of(n_job), 1)

            def exp_out(u, dst):
                dve.wait_ge(phi_exp, 4 + u + 1)
                v.scalar_tensor_tensor(dst, PT[:, u, :], 1e-8, PR[:, u, :], ALU.max, ALU.mult).then_inc(phi_ready, 1)

            exp_in(0, "per.kf.0", "per.kn.0")
            exp_in(1, "per.kf.1", "per.kn.1")
            exp_in(2, "per.qf.0", "per.qn.0")
            exp_out(0, kphi_p[:, 0, :])
            exp_out(1, kphi_p[:, 1, :])
            exp_in(3, "per.qf.1", "per.qn.1")
            exp_out(2, qphi_p[:, 0:2, :].rearrange("p c n -> p (c n)"))
            diagonals("per")
            exp_out(3, qphi_p[:, 2:4, :].rearrange("p c n -> p (c n)"))
            weight_low("per_o")
            linear_out("per")
            for t in range(NT):
                dve.wait_ge(graph_biased, t + 1)
                last = v.tensor_scalar(graph_out[:, t, :], graph_out[:, t, :], 0.0, valid[:, t:t + 1], ALU.max, ALU.mult)
            link(last)
            for t in range(NT):
                turned_low("per.oT", OT, t)
            for t in range(NT):
                last = v.tensor_tensor(X[:, t, :], X[:, t, :], graph_out[:, t, :], ALU.add)
            link(last)
            for t in range(NT):
                add_to_x(f"per_o.{t}")
                ln_stats(LN_X3, t, X)
            for t in range(NT):
                ln_apply(LN_X3, t, X, XN)

            for t in range(NT):
                job = f"r1.xT.{t}"
                pool_tile(job).then_inc(read_of(job), 1)
                stored(dve, job)
            pooled()
            for t in range(NT):
                ln_stats(LN_Z, t, XN)
            ln_apply(LN_Z, 0, XN, ZN)
            route(1, K1, 2)
            scale_shift("xT3.1", xsf, 1, "ns_w", "ns_b").then_inc(full_form, 1)
            dve.wait_ge(split_high, 1)
            scale_shift("xT3.0", xsf, 0, "ns_w", "ns_b").then_inc(full_form, 1)
            dve.wait_ge(full_form, 2)
            for j in range(2):
                low_of(XT, chunks(xsf, j), j, 1 + j).then_inc(split_low, 1)
            for j in range(2):
                scale_shift(f"xT3.{j}", xtf, j, "nt_w", "nt_b").then_inc(read_of(f"xT3.{j}"), 1)
            for w in ("sp_q", "sp_k"):
                weight_low(w)
            for j in range(2):
                low_of(XT2, chunks(xtf, j), j, 3 + j).then_inc(split_low, 1)
            dve.wait_ge(scol_loaded, 16)
            for j in range(2):
                scaled_query(f"sp_q.{j}", j, lambda c: scol[:, c:c + 1])
            for j in range(2):
                query_low("sp", j)
            for j in range(2):
                key_low("sp", j, lambda c: scol[:, DC + c:DC + c + 1])
            for t in range(NT):
                value_row(t, "sp_v")
            attention("sp")
            dve.wait_ge(tcol_loaded, 16)
            for j in range(2):
                scaled_query(f"tm_q.{j}", j, lambda c: tcol[:, c:c + 1])
            for t in range(NT):
                value_row(t, "tm_v")
            for t in range(NT):
                turned_low("sp.oT", OT, t)
            attention("tm")
            for t in range(NT):
                turned_low("tm.oT", OT, t)
            for j in range(2):
                scaled_query(f"cr_q.{j}", j, lambda c: column("cr_bq", c))
            for j in range(2):
                job = f"tm_o.{j}"
                filled(dve, job)
                for f in range(2):
                    c = 2 * j + f
                    last = v.scalar_tensor_tensor(tmf[:, c, :], bank(job)[:, f * N:(f + 1) * N],
                                                  tcol[:, 2 * DC + c:2 * DC + c + 1], xtf[:, c, :], ALU.add, ALU.add)
                last.then_inc(read_of(job), 1)
            for j in range(2):
                stored(dve, f"tm_o.{j}")
                low_of(TM, chunks(tmf, j), j, 7 + j).then_inc(split_low, 1)
            for j in range(2):
                query_low("cr", j)
            for j in range(2):
                key_low("cr", j, lambda c: column("cr_bk", c))
            for t in range(NT):
                value_row(t, "cr_v")
            attention("cr")
            for t in range(NT):
                turned_low("cr.oT", OT, t)
            for t in range(NT):
                last = v.tensor_tensor(XN[:, t, :], XN[:, t, :], row_there("cr_o"), ALU.add)
            link(last)
            for t in range(NT):
                job = f"cr_o.{t}"
                filled(dve, job)
                v.tensor_tensor(XN[:, t, :], bank(job)[:, :], XN[:, t, :], ALU.add).then_inc(read_of(job), 1)
                stored(dve, job)
                ln_stats(LN_MLP, t, XN)
            for t in range(NT):
                ln_apply(LN_MLP, t, XN, ZN)

            scale_shift("xT4.1", xsf, 1, "nm_w", "nm_b").then_inc(full_form, 1)
            dve.wait_ge(split_high, 9)
            scale_shift("xT4.0", xsf, 0, "nm_w", "nm_b").then_inc(full_form, 1)
            dve.wait_ge(full_form, 4)
            for j in range(2):
                low_of(XT, chunks(xsf, j), j, 9 + j).then_inc(read_of(f"xT4.{j}"), 1)
            for other in (XN[:, :, :], row_there("down").unsqueeze(1).broadcast_to([P, NT, D])):
                link(v.tensor_tensor(X[:, :, :], X[:, :, :], other, ALU.add))
            for j in range(FC // 2):
                stored(dve, f"up.{j}")
                link(v.tensor_copy(chunks(G[0], j), gf[j % 4]))
                v.tensor_tensor(chunks(G[1], j), gf[j % 4], chunks(G[0], j).bitcast(F32), ALU.subtract)\
                    .then_inc(split_low, 1)
            for t in range(NT):
                job = f"down.{t}"
                filled(dve, job)
                v.tensor_tensor(ZN[:, t, :], bank(job)[:, :], X[:, t, :], ALU.add).then_inc(out_ready, 1)

        @block.scalar
        def _(act):
            s = nc.scalar

            def round_quarter(k):
                act.wait_ge(raw_loaded[k % RAW], 16 * (k // RAW + 1))
                i, c = divmod(k, 4)
                if c == 0 and i >= SPLIT:
                    filled(act, LAST_JOB[WEIGHTS[i - SPLIT]])
                s.copy(parts(k)[0], wraw[:, k % RAW, :]).then_inc(high_done, 1)

            def weight_high(w):
                for c in range(DC):
                    round_quarter(quarter(w, c))

            def target_hots(g):
                if g >= 2:
                    act.wait_ge(hots_dst, g - 1)
                for c in range(EG):
                    e = g * EG + c
                    last = s.activation(sq16[:, g % 2, c, :], iota16[:, :], ACT.Square, bias=edge_f[:, 2, e:e + 1])
                last.then_inc(sq_ready, 1)
                act.wait_ge(sq_ready, g + 1)
                hots_free(act, g)
                s.activation(hots(g)[0][:, :, 1, :], sq16[:, g % 2, :, :], ACT.Relu, bias=1.0, scale=-1.0).then_inc(hots_dst, 1)

            def scaled_hots(g):
                act.wait_ge(hots_plain, g - PLAIN + 1)
                h, hlo = hots(g)
                for c in range(EG):
                    for i, o in enumerate((h[:, c, 2, :], h[:, c, 3, :], hlo[:, c, :])):
                        e = g * EG + c
                        last = s.activation(o, h[:, c, 1, :], ACT.Copy, scale=ew[:, 1 + i, e:e + 1])
                last.then_inc(hots_scaled, 1)

            def turned_high(prefix, pair, tiles=range(NT)):
                for t in tiles:
                    job = f"{prefix}.{t}"
                    filled(act, job)
                    if prefix == "xT1":
                        act.wait_ge(pool_read, t + 1)
                    s.copy(pair[0][:, :, token(t)], bank(job)[:, :].rearrange("p (c n) -> p c n", c=DC))\
                        .then_inc(high_taken, 1)

            def elu_exp(u):
                act.wait_ge(phi_in, u + 1)
                s.activation(PT[:, u, :], PT[:, u, :], ACT.Exp).then_inc(phi_exp, 1)

            def performer_exp(u, job):
                stored(act, job)
                s.activation(PT[:, u, :], PT[:, u, :], ACT.Exp)
                s.activation(PR[:, u, :], PR[:, u, :], ACT.Exp).then_inc(phi_exp, 1)

            def attention(name, *meanwhile):
                a, causal = ATTENTIONS.index(name), name == "tm"
                quarters = [quarter(w, c) for w in meanwhile for c in range(DC)]
                for h in range(H):
                    act.wait_ge(score_max, H * a + h + 1)
                    if h >= 4:
                        filled(act, f"{name}.t{h - 4}")
                    for t in range(NT):
                        keys = P if causal and t == 0 else N
                        last = s.activation(PR[:, h % 4, t * N:t * N + keys], bank(f"{name}.s{h}")[:, t * N:t * N + keys],
                                            ACT.Exp, bias=nmax[:, h, t:t + 1], accum_out=psum_[:, h, t:t + 1])
                    last.then_inc(read_of(f"{name}.s{h}"), 1)
                    round_quarter(quarters[h])

            def shifted(job, dst, bias, j, scale=1.0):
                for f in range(2):
                    c = 2 * j + f
                    last = s.activation(dst[:, c, :], bank(job)[:, f * N:(f + 1) * N], ACT.Identity, bias=bias(c),
                                        scale=scale if isinstance(scale, float) else scale(c))
                return last

            def scaled(job, dst, j, square=None):
                filled(act, job)
                flat = lambda ap: ap[:, 2 * j:2 * j + 2, :].rearrange("p c n -> p (c n)")
                last = s.activation(flat(dst), bank(job)[:, :], ACT.Copy, scale=SCALE)
                if square is not None:
                    last = s.activation(flat(square), bank(job)[:, :], ACT.Square, scale=SCALE)
                last.then_inc(read_of(job), 1)

            def query_high(name):
                for j in range(2):
                    stored(act, f"{name}_q.{j}")
                    s.copy(QR[0][:, 2 * j:2 * j + 2, :], Q[:, 2 * j:2 * j + 2, :]).then_inc(q_high, 1)

            def key_high(name, bias):
                for j in range(2):
                    filled(act, f"{name}_k.{j}")
                    shifted(f"{name}_k.{j}", KR[0], bias, j).then_inc(k_high, 1)

            def take_whole(job, dst, view=lambda ap: ap):
                filled(act, job)
                s.copy(dst, view(bank(job)[:, :])).then_inc(read_of(job), 1)

            for c in range(2):
                round_quarter(quarter("mix_v", c))
            act.wait_ge(gate_neg, 1)
            s.activation(ew[:, 1, :], ew[:, 0, :], ACT.Exp, bias=gmax[:, 2:3]).then_inc(gate_exp, 1)
            round_quarter(quarter("mix_v", 2))
            turned_high("xT0", XT)
            round_quarter(quarter("mix_v", 3))
            act.wait_ge(consts, IOTA_CONST)
            act.wait_ge(dst_ready, 1)
            target_hots(0)
            weight_high("mix_k")
            target_hots(1)
            weight_high("mix_q")
            for u in range(2):
                elu_exp(u)
            target_hots(2)
            weight_high("gnn")
            for u in range(2, 4):
                elu_exp(u)
            target_hots(3)
            for t in range(NT):
                take_whole(f"gnn.{t}", hg[:, t, :])
            weight_high("mix_p")
            scaled_hots(5)
            turned_high("mix.oT", OT)
            for g in range(6, GROUPS):
                scaled_hots(g)
            turned_high("xT1", XT)
            filled(act, "r0.hid")
            s.activation(hid_c[:, :], bank("r0.hid")[:, 0:1], ACT.Relu, bias=column("r0_b1"), scale=1.0 / N)\
                .then_inc(read_of("r0.hid"), 1)
            act.wait_ge(logit_max, 1)
            s.activation(r[:, 8:8 + K0], r[:, 0:K0], ACT.Exp, bias=r[:, 32:33], accum_out=r[:, 34:35]).then_inc(logit_exp, 1)
            weight_high("ffn_q")
            weight_high("ffn_k")
            act.wait_ge(sums_full, 1)
            for t in range(NT):
                last = s.activation(att[:, t, :], acc[t][:, N:], ACT.Copy, accum_out=rowsum[:, t:t + 1])
            last.then_inc(row_sum, 1)
            weight_high("ffn_v")
            for j in range(2):
                filled(act, f"ffn_q.{j}")
                s.activation(QR[0][:, 2 * j:2 * j + 2, :].rearrange("p c n -> p (c n)"), bank(f"ffn_q.{j}")[:, :], ACT.Copy,
                             scale=SCALE).then_inc(q_high, 1)
            for j in range(2):
                filled(act, f"ffn_k.{j}")
                s.copy(KR[0][:, 2 * j:2 * j + 2, :].rearrange("p c n -> p (c n)"), bank(f"ffn_k.{j}")[:, :])\
                    .then_inc(k_high, 1)
            take_whole("attT", attT[:, :, :].rearrange("p t n -> p (t n)"))
            weight_high("ffn_o")
            take_whole("ffn_v.0", V[:, 0, :, 0:P], by_pair)
            weight_high("graph")
            attention("ffn", "per_k", "per_v")
            turned_high("ffn.oT", OT)

            turned_high("xT2", XT, [0])
            weight_high("per_q")
            turned_high("xT2", XT, [1])
            take_whole("per_v.0", V[:, 0, :, 0:P], by_pair)
            for j in range(2):
                scaled(f"per_k.{j}", K, j, ksq)
            for i in range(2):
                job = f"g.msg.{i}"
                filled(act, job)
                s.copy(msg[0][:, 2 * i:2 * i + 2, :].rearrange("p c n -> p (c n)"), bank(job)[:, :]).then_inc(high_taken, 1)
            for j in range(2):
                scaled(f"per_q.{j}", Q, j, qsq)
            for u, job in enumerate(both("per.kn", "per.qn")):
                performer_exp(u, job)
            for t in range(NT):
                take_whole(f"g.out.{t}", graph_out[:, t, :])
            weight_high("per_o")
            turned_high("per.oT", OT)
            filled(act, "r1.hid")
            s.activation(hid_c[:, :], bank("r1.hid")[:, 0:1], ACT.Gelu, bias=column("r1_b1"),
                         scale=1.0 / N).then_inc(read_of("r1.hid"), 1)
            act.wait_ge(logit_max, 2)
            s.activation(r[:, 8:8 + 2 * K1], r[:, 0:2 * K1], ACT.Exp, bias=r[:, 32:33], accum_out=r[:, 34:35])\
                .then_inc(logit_exp, 1)
            for j in range(2):
                filled(act, f"xT3.{j}")
                if j == 1:
                    act.wait_ge(full_form, 1)
                shifted(f"xT3.{j}", XT[0], lambda c: column("ns_b", c), j, lambda c: column("ns_w", c))\
                    .then_inc(split_high, 1)
            for w in ("sp_q", "sp_k"):
                weight_high(w)
            for j in range(2):
                stored(act, f"xT3.{j}")
                s.copy(XT2[0][:, 2 * j:2 * j + 2, :], xtf[:, 2 * j:2 * j + 2, :]).then_inc(split_high, 1)
            weight_high("sp_v")
            query_high("sp")
            weight_high("tm_q")
            act.wait_ge(scol_loaded, 16)
            key_high("sp", lambda c: scol[:, DC + c:DC + c + 1])
            weight_high("tm_k")
            attention("sp", "tm_v", "sp_o")
            act.wait_ge(tcol_loaded, 16)
            for j in range(2):
                filled(act, f"tm_k.{j}")
                shifted(f"tm_k.{j}", K, lambda c: tcol[:, DC + c:DC + c + 1], j).then_inc(read_of(f"tm_k.{j}"), 1)
            turned_high("sp.oT", OT)
            weight_high("cr_q")
            attention("tm", "tm_o", "cr_k")
            for j in range(2):
                filled(act, f"sp_o.{j}")
                shifted(f"sp_o.{j}", SP[0], lambda c: scol[:, 2 * DC + c:2 * DC + c + 1], j).then_inc(split_high, 1)
            turned_high("tm.oT", OT)
            weight_high("cr_v")
            query_high("cr")
            for j in range(2):
                stored(act, f"tm_o.{j}")
                s.copy(TM[0][:, 2 * j:2 * j + 2, :], tmf[:, 2 * j:2 * j + 2, :]).then_inc(split_high, 1)
            weight_high("cr_o")
            key_high("cr", lambda c: column("cr_bk", c))
            weight_high("up_0")
            attention("cr", "up_1", "up_2")
            turned_high("cr.oT", OT)
            weight_high("up_3")
            for j in range(2):
                filled(act, f"xT4.{j}")
                if j == 1:
                    act.wait_ge(full_form, 3)
                shifted(f"xT4.{j}", XT[0], lambda c: column("nm_b", c), j, lambda c: column("nm_w", c))\
                    .then_inc(split_high, 1)
            for j in range(FC // 2):
                job = f"up.{j}"
                filled(act, job)
                if j >= 4:
                    act.wait_ge(split_low, 7 + (j - 4) + 1)
                for f in range(2):
                    last = s.activation(gf[j % 4][:, f, :], bank(job)[:, f * N:(f + 1) * N], ACT.Gelu,
                                        bias=column("up_b", 2 * j + f))
                last.then_inc(read_of(job), 1)
                if j % 2:
                    weight_high(f"down_{j // 2}")

        @block.gpsimd
        def _(pool):
            g = nc.gpsimd
            made = [0]

            def make(ins):
                made[0] += 1
                ins.then_inc(consts, 1)
                pool.wait_ge(consts, made[0])

            def diagonal(tile):
                make(g.memset(tile[:, :], 0.0))
                make(g.affine_select(out=tile[:, :], in_=tile[:, :], compare_op=ALU.not_equal, fill=1.0, base=0,
                                     pattern=[[-1, P]], channel_multiplier=1))

            def rsqrt(n):
                for t in range(NT):
                    pool.wait_ge(ln_var, 2 * n + t + 1)
                    g.tensor_tensor(rstd[:, t:t + 1], ve[:, t:t + 1], half[:, 0:1], ALU.pow).then_inc(ln_rstd, 1)
                    pool.wait_ge(ln_rstd, 2 * n + t + 1)

            def weight_low(w):
                for c in range(DC):
                    k = quarter(w, c)
                    if k in LOW_ON_POOL:
                        pool.wait_ge(high_done, k + 1)
                        hi, lo = parts(k)
                        g.tensor_tensor(lo, wraw[:, k % RAW, :], hi.bitcast(F32), ALU.subtract).then_inc(low_done[0], 1)
                        low_ready(pool, k)

            def source_hots(n):
                hots_free(pool, n)
                for c in range(EG):
                    e = n * EG + c
                    g.tensor_scalar(hots(n)[0][:, c, 0, :], iota16[:, :], edge_f[:, 0, e:e + 1], None, ALU.is_equal)\
                        .then_inc(hots_src, 1)
                    pool.wait_ge(hots_src, e + 1)

            diagonal(ident)
            make(g.memset(half[:, :], -0.5))
            assert made[0] == FIRST_CONSTS
            make(g.iota(iota16[:, :], [[1, N]], base=0, channel_multiplier=0, allow_small_or_imprecise_dtypes=True))
            assert made[0] == IOTA_CONST
            pool.wait_ge(gate_max, 1)
            g.partition_all_reduce(gmax[:, 1:2], gmax[:, 0:1], P, bass.bass_isa.ReduceOp.max).then_inc(gate_all, 1)
            pool.wait_ge(gate_all, 1)
            rsqrt(LN_IN0)
            weight_low("mix_v")
            pool.wait_ge(dst_ready, 1)
            source_hots(0)
            weight_low("mix_k")
            source_hots(1)
            weight_low("mix_q")
            source_hots(2)
            weight_low("gnn")
            source_hots(3)
            make(g.iota(desc[:, :], [[-1, 4]], base=4, channel_multiplier=0, allow_small_or_imprecise_dtypes=True))
            diagonal(ident16)
            make(g.memset(mask16[:, :], 0.0))
            make(g.affine_select(out=mask16[:, :], in_=mask16[:, :], compare_op=ALU.is_ge, fill=MASKED, base=0,
                                 pattern=[[-1, P]], channel_multiplier=1))
            make(g.memset(V[:, :, :, P:P + 1], 1.0))
            make(g.memset(halves[:, :], 0.0))
            for b in range(2):
                s = slice(64 * b, 64 * b + 64)
                make(g.memset(halves[s, s], 1.0))
            make(g.memset(KV[:, :, :], 0.0))
            make(g.memset(KS[:, :, :], 0.0))
            make(g.memset(omega[:, :, :], 0.0))
            assert made[0] == ALL_CONSTS
            weight_low("mix_p")
            for i, name in enumerate(("gnn", "mix_p")):
                slot = BIAS_ROWS.index(name)
                pool.wait_ge(row_loaded[slot % ROWS], 16 * (slot // ROWS + 1))
                for t in range(NT):
                    g.tensor_tensor(X[:, t, :], X[:, t, :], row(name), ALU.add).then_inc(biases_added, 1)
                    pool.wait_ge(biases_added, NT * i + t + 1)
            pool.wait_ge(deg_ready, 1)
            g.tensor_tensor(dinv[:, :], deg[:, :], half[:, :], ALU.pow).then_inc(dinv_ready, 1)
            pool.wait_ge(dinv_ready, 1)
            rsqrt(LN_FFN)
            for w in ("ffn_q", "ffn_k", "ffn_v", "ffn_o", "graph", "per_k", "per_v"):
                weight_low(w)
            rsqrt(LN_IN1)
            weight_low("per_q")
            rsqrt(LN_GRAPH)
            slot = BIAS_ROWS.index("graph_out")
            pool.wait_ge(row_loaded[slot % ROWS], 16 * (slot // ROWS + 1))
            for t in range(NT):
                stored(pool, f"g.out.{t}")
                h = graph_out[:, t, :]
                g.tensor_tensor(h, h, row("graph_out"), ALU.add).then_inc(graph_biased, 1)
                pool.wait_ge(graph_biased, t + 1)
            weight_low("per_o")
            rsqrt(LN_X3)
            rsqrt(LN_Z)
            for w in ("sp_q", "sp_k", "sp_v", "tm_q", "tm_k", "tm_v", "sp_o", "cr_q", "tm_o", "cr_k", "cr_v", "cr_o",
                      "up_0", "up_1", "up_2"):
                weight_low(w)
            rsqrt(LN_MLP)
            for w in ("up_3", "down_0", "down_1", "down_2", "down_3"):
                weight_low(w)


def chunked(w):
    k, n = w.shape
    return w.reshape(k // P, P, n).transpose(1, 0, 2).reshape(P, k // P * n)


def by_column(b):
    return b.reshape(-1, P).T


def kernel(**inputs):
    import concourse.bacc as bacc
    from concourse.bass_utils import run_bass_kernel_spmd

    i = {k: np.asarray(a) for k, a in inputs.items()}
    f0, f1, g1, m0, m1 = "L0_ffn_", "L1_ffn_", "L1_gnn_", "L0_mix_", "L1_mix_"

    def heads(w):
        kv = w.shape[1] // 64
        return np.repeat(w.reshape(D, kv, 1, 64), H // kv, axis=2).reshape(D, D)

    static = {"mix_k": i[m0 + "Wk"], "mix_v": i[m0 + "Wv"], "mix_q": i[m0 + "Wq"], "mix_p": i[m0 + "Wp"],
              "gnn": i["L0_gnn_weight"], "per_k": i[m1 + "Wk"], "per_v": i[m1 + "Wv"], "per_q": i[m1 + "Wq"],
              "per_o": i[m1 + "Wo"], "cr_o": i[f1 + "cross_out_w"].T}
    for j, part in enumerate("qkv"):
        static[f"cr_{part}"] = i[f1 + "cross_in_w"][j * D:(j + 1) * D].T
    for j in range(4):
        static[f"up_{j}"] = i[f1 + "mlp_w1"][j * D:(j + 1) * D].T
        static[f"down_{j}"] = i[f1 + "mlp_w2"][:, j * D:(j + 1) * D].T
    laid = {k: chunked(w) for k, w in static.items()}
    laid["graph"] = np.concatenate([chunked(i[g1 + "Wm"]), chunked(i[g1 + "W1"]), i[g1 + "W2"]], axis=1)
    sp_in = i[f1 + "sp_in_w"].reshape(K1, 3, D, D)
    sp_b = i[f1 + "sp_in_b"].reshape(K1, 3, D)
    arrays = {
        "x": i["x"],
        "edges": np.stack([i["src"].reshape(P, EC), i["dst"].reshape(P, EC)], axis=1),
        "gate": i["edge_weight"].reshape(P, EC),
        "cols": np.concatenate(
            [by_column(i[k]) for k in (m0 + "bq", f0 + "r_b1", g1 + "gamma", g1 + "beta", f1 + "router_b1",
                                       f1 + "norm_s_w", f1 + "norm_s_b", f1 + "norm_t_w", f1 + "norm_t_b",
                                       f1 + "norm_mlp_w", f1 + "norm_mlp_b", f1 + "mlp_b1")]
            + [by_column(i[f1 + "cross_in_b"][j * D:(j + 1) * D]) for j in range(2)]
            + [i[f0 + "r_w2"], i[f1 + "router_w2"].T], axis=1),
        "rows": np.stack([i[m0 + "bv"], i[m0 + "bk"], i["L0_gnn_bias"], i[m0 + "bp"],
                          np.concatenate([i[g1 + "bm"], i[g1 + "b1"], np.zeros(D - N - HID, np.float32)]),
                          i[g1 + "b2"], i[f1 + "cross_in_b"][2 * D:], i[f1 + "cross_out_b"], i[f1 + "mlp_b2"]]),
        "router_rows": np.concatenate([i[f0 + "r_b2"], i[f1 + "router_b2"],
                                       np.zeros(16 - K0 - 2 * K1, np.float32)]).reshape(1, 16),
        "routers": np.stack([chunked(i[f0 + "r_w1"]), chunked(i[f1 + "router_w1"].T)], axis=1),
        "omegas": np.stack([i[m1 + "omega_q"], i[m1 + "omega_k"]]),
        "weights": np.stack([laid[w] for w in STATIC]),
        "ffn_w": np.stack([np.stack([chunked(i[f"{f0}wq{e}"]), chunked(heads(i[f"{f0}wk{e}"])),
                                     chunked(heads(i[f"{f0}wv{e}"])), chunked(i[f"{f0}wo{e}"])]) for e in reversed(range(K0))]),
        "sp_w": np.stack([np.stack([chunked(sp_in[e, j].T) for j in range(3)] + [chunked(i[f1 + "sp_out_w"][e].T)])
                          for e in reversed(range(K1))]),
        "tm_w": np.stack([np.stack([chunked(i[f"{f1}t{p}_w"][e].T) for p in "qkvp"]) for e in reversed(range(K1))]),
        "sp_cols": np.stack([np.concatenate([by_column(sp_b[e, 0]), by_column(sp_b[e, 1]),
                                             by_column(i[f1 + "sp_out_b"][e])], axis=1)
                            for e in reversed(range(K1))]),
        "tm_cols": np.stack([np.concatenate([by_column(i[f"{f1}t{p}_b"][e]) for p in "qkp"], axis=1)
                             for e in reversed(range(K1))]),
        "sp_row": sp_b[::-1, 2],
        "tm_row": i[f1 + "tv_b"][::-1],
    }
    nc = bacc.Bacc("TRN2", target_bir_lowering=False, num_devices=1)
    feed, args = {}, {}
    for name, a in arrays.items():
        a = np.ascontiguousarray(a)
        feed[f"in_{name}"] = a
        args[name] = nc.dram_tensor(f"in_{name}", a.shape, mybir.dt.from_np(a.dtype), kind="ExternalInput").ap()
    args["out"] = nc.dram_tensor("out_0", (N, D), F32, kind="ExternalOutput").ap()
    build(nc, **args)
    result = run_bass_kernel_spmd(nc, [feed], core_ids=[0])
    return result.results[0]["out_0"]
```
